# Optimizing a Trainium2 kernel written in Bass

```python
import numpy as np
import jax
import jax.numpy as jnp

def _softmax(x, axis=-1):
    return jax.nn.softmax(x, axis=axis)

def _gelu(x):
    return jax.nn.gelu(x, approximate=True)

def _silu(x):
    return jax.nn.silu(x)

def _sigmoid(x):
    return jax.nn.sigmoid(x)

def _layernorm(x, axis=-1, eps=1e-05):
    m = jnp.mean(x, axis=axis, keepdims=True)
    v = jnp.var(x, axis=axis, keepdims=True)
    return (x - m) / jnp.sqrt(v + eps)

def _scatter_add(tgt, idx, src, axis=0):
    return tgt.at[idx].add(src)

def _segment_sum(src, seg, n):
    return jax.ops.segment_sum(src, seg, n)
kernel_name = 'mk_decoder_postln_d1_seqx_r4_8dabd5'

def setup_inputs(seed: int=0):
    np.random.seed(seed)
    _w = jnp.asarray

    def _rec_inputs():
        import jax
        import jax.numpy as jnp
        _rk = jax.random.key(seed)
        x = 0.0002417 + 0.9998 * jax.random.normal(jax.random.fold_in(_rk, 1), (8, 256, 256), jnp.float32)
        _lenS = 256 - jax.random.randint(jax.random.fold_in(_rk, 7), (8,), 0, max(1, 256 // 4) + 1, jnp.int32)
        _lenS2 = 120 - jax.random.randint(jax.random.fold_in(_rk, 8), (8,), 0, max(1, 120 // 4) + 1, jnp.int32)
        _ctx_1024P = jax.random.normal(jax.random.fold_in(_rk, 11), (8, 16, 256), jnp.float32)
        _ctx_1024c = jax.random.dirichlet(jax.random.fold_in(_rk, 511), 0.3 * jnp.ones((16,), jnp.float32), (8, 120))
        _ctx_1024t = jnp.einsum('bsk,bkd->bsd', _ctx_1024c, _ctx_1024P)
        _ctx_1024t = _ctx_1024t * jax.lax.rsqrt(jnp.mean(jnp.square(_ctx_1024t)) + 1e-12) * 0.953939
        ctx_1024 = 7.22013e-05 + 1.00017 * (_ctx_1024t + 0.3 * jax.random.normal(jax.random.fold_in(_rk, 611), (8, 120, 256), jnp.float32))
        _validS = jnp.arange(256)[None, :] < _lenS[:, None]
        _validS2 = jnp.arange(120)[None, :] < _lenS2[:, None]
        _causal = jnp.tril(jnp.ones((256, 256), dtype=bool))
        mask_BxS2_if0 = jnp.where(jnp.ones((8, 120), dtype=bool), 0, 1).astype(jnp.int32)
        return (x, ctx_1024, mask_BxS2_if0)
    x, ctx_1024, mask_BxS2_if0 = _rec_inputs()

    def _L0_attn_setup():
        import jax, jax.numpy as jnp
        import numpy as np
        CHUNK = 32
        H = 4

        def silu(x):
            return x * jax.nn.sigmoid(x)

        def l2norm(x):
            return x * jax.lax.rsqrt(jnp.sum(x * x, -1, keepdims=True) + 1e-06)

        def dwconv_causal(x_cl, w):
            k = w.shape[1]
            xp = jnp.pad(x_cl, ((0, 0), (0, 0), (k - 1, 0)))
            return jax.lax.conv_general_dilated(xp, w[:, None, :], (1,), 'VALID', dimension_numbers=('NCH', 'OIH', 'NCH'), feature_group_count=x_cl.shape[1])

        def short_conv_silu(x_bld, w):
            y = dwconv_causal(jnp.swapaxes(x_bld, 1, 2), w)
            return silu(jnp.swapaxes(y, 1, 2))

        def delta_rule_chunkwise(q, k, v, beta, chunk=CHUNK):
            b, h, L, dk = q.shape
            dv = v.shape[-1]
            pad = -L % chunk
            if pad:
                q, k, v = (jnp.pad(t, ((0, 0), (0, 0), (0, pad), (0, 0))) for t in (q, k, v))
                beta = jnp.pad(beta, ((0, 0), (0, 0), (0, pad)))
            n = (L + pad) // chunk
            q = l2norm(q)
            k = l2norm(k)
            v = v * beta[..., None]
            kb = k * beta[..., None]
            ch = lambda x: x.reshape(b, h, n, chunk, x.shape[-1])
            qc, kc, vc, kbc = map(ch, (q, k, v, kb))
            idx = jnp.arange(chunk)
            strict_lower = (idx[:, None] > idx[None, :]).astype(q.dtype)
            incl_lower = (idx[:, None] >= idx[None, :]).astype(q.dtype)
            attn = -jnp.einsum('bhncd,bhned->bhnce', kbc, kc) * strict_lower
            for i in range(1, chunk):
                upd = jnp.einsum('...j,...ji->...i', attn[..., i, :], attn[..., :, :i])
                attn = attn.at[..., i, :i].add(upd)
            attn = attn + jnp.eye(chunk, dtype=q.dtype)
            u = attn @ vc
            w = attn @ kbc
            xs = tuple((jnp.moveaxis(t, 2, 0) for t in (qc, kc, u, w)))
            S0 = jnp.zeros((b, h, dk, dv), q.dtype)

            def step(S, x):
                qi, ki, ui, wi = x
                a_loc = jnp.einsum('bhcd,bhed->bhce', qi, ki) * incl_lower
                ui = ui - wi @ S
                oi = qi @ S + a_loc @ ui
                S = S + jnp.einsum('bhcd,bhcv->bhdv', ki, ui)
                return (S, oi)
            S, o = jax.lax.scan(step, S0, xs)
            o = jnp.moveaxis(o, 0, 2).reshape(b, h, n * chunk, dv)[:, :, :L]
            return (o, S)

        def multiscale_conv(v, ms_w3, ms_w15, ms_w31, kernel_mix_w, channel_mixer_w):
            b, l, h, d = v.shape
            x = jnp.swapaxes(v.reshape(b, l, h * d), 1, 2)
            outs = [dwconv_causal(x, w) for w in (ms_w3, ms_w15, ms_w31)]
            y = jnp.concatenate(outs, axis=1)
            y = y.reshape(b, h, 3 * d, l).transpose(0, 3, 1, 2)
            y = y @ kernel_mix_w
            y = (y.reshape(b, l, h * d) @ channel_mixer_w).reshape(b, l, h, d)
            return y

        def _forward(hidden_states, Wq, Wk, Wv, Wb, conv_q_w, conv_k_w, conv_v_w, ms_w3, ms_w15, ms_w31, kernel_mix_w, channel_mixer_w, fusion_w1, fusion_b1, fusion_w2, fusion_b2, o_norm_w, Wo):
            b, L, D = hidden_states.shape
            h = H
            dk = Wq.shape[1] // h
            dv = Wv.shape[1] // h
            q = short_conv_silu(hidden_states @ Wq, conv_q_w).reshape(b, L, h, dk)
            k = short_conv_silu(hidden_states @ Wk, conv_k_w).reshape(b, L, h, dk)
            v = short_conv_silu(hidden_states @ Wv, conv_v_w).reshape(b, L, h, dv)
            v_direct = v
            beta = jax.nn.sigmoid(hidden_states @ Wb)
            tr = lambda x: jnp.swapaxes(x, 1, 2)
            delta_out, _S = delta_rule_chunkwise(tr(q), tr(k), tr(v), tr(beta))
            delta_out = jnp.swapaxes(delta_out, 1, 2)
            ms_out = multiscale_conv(v_direct, ms_w3, ms_w15, ms_w31, kernel_mix_w, channel_mixer_w)
            bn = lambda x: jnp.mean(jnp.abs(x), -1)
            gate_features = jnp.concatenate([hidden_states, bn(ms_out), bn(delta_out), bn(v_direct)], -1)
            hdn = jax.nn.gelu(gate_features @ fusion_w1 + fusion_b1, approximate=False)
            logits = (hdn @ fusion_w2 + fusion_b2).reshape(b, L, h, 3)
            wts = jax.nn.softmax(logits, -1)
            o = wts[..., 0:1] * ms_out + wts[..., 1:2] * delta_out + wts[..., 2:3] * v_direct
            o = o * jax.lax.rsqrt(jnp.mean(o * o, -1, keepdims=True) + 1e-05) * o_norm_w
            return o.reshape(b, L, h * dv) @ Wo
        B, L, D = (4, 512, 256)
        h, d = (H, D // H)
        key = jax.random.key(seed)
        ks = jax.random.split(key, 20)
        nrm = lambda k, shp, s: jax.random.normal(k, shp, dtype=jnp.float32) * s
        inp = {'hidden_states': nrm(ks[0], (B, L, D), 1.0), 'Wq': nrm(ks[1], (D, D), D ** (-0.5)), 'Wk': nrm(ks[2], (D, D), D ** (-0.5)), 'Wv': nrm(ks[3], (D, D), D ** (-0.5)), 'Wb': nrm(ks[4], (D, h), D ** (-0.5)), 'conv_q_w': nrm(ks[5], (D, 4), 0.3), 'conv_k_w': nrm(ks[6], (D, 4), 0.3), 'conv_v_w': nrm(ks[7], (D, 4), 0.3), 'ms_w3': nrm(ks[8], (D, 3), 0.02), 'ms_w15': nrm(ks[9], (D, 15), 0.02), 'ms_w31': nrm(ks[10], (D, 31), 0.02), 'kernel_mix_w': nrm(ks[11], (3 * d, d), (3 * d) ** (-0.5)), 'channel_mixer_w': nrm(ks[12], (D, D), D ** (-0.5)), 'fusion_w1': nrm(ks[13], (D + 3 * h, 2 * D), (D + 3 * h) ** (-0.5)), 'fusion_b1': jnp.zeros((2 * D,), jnp.float32), 'fusion_w2': nrm(ks[14], (2 * D, 3 * h), (2 * D) ** (-0.5)), 'fusion_b2': jnp.concatenate([jnp.zeros((2 * h,), jnp.float32), jnp.ones((h,), jnp.float32)]), 'o_norm_w': jnp.ones((d,), jnp.float32), 'Wo': nrm(ks[15], (D, D), D ** (-0.5))}
        return inp
    _L0_attn_all = _L0_attn_setup()
    _L0_attn_in = {k: v for k, v in _L0_attn_all.items() if k in ('Wq', 'Wk', 'Wv', 'Wb', 'conv_q_w', 'conv_k_w', 'conv_v_w', 'ms_w3', 'ms_w15', 'ms_w31', 'kernel_mix_w', 'channel_mixer_w', 'fusion_w1', 'fusion_b1', 'fusion_w2', 'fusion_b2', 'o_norm_w', 'Wo')}
    del _L0_attn_all

    def _L0_xattn_setup():
        import jax, jax.numpy as jnp
        import numpy as np
        import math
        B, M, D, H, NK = (4, 512, 256, 16, 5)
        HD = D // H

        def _gather_pad0(x, idx):
            Bx, Hx, W, hd = x.shape
            valid = (idx >= 0) & (idx < W)
            idxc = jnp.clip(idx, 0, W - 1).reshape(Bx, Hx, -1)
            g = jnp.take_along_axis(x, idxc[..., None], axis=2)
            g = g.reshape(idx.shape + (hd,))
            return g * valid[..., None].astype(x.dtype)
        key = jax.random.key(seed)
        ks = jax.random.split(key, 9)
        w = lambda k, shape: jax.random.normal(k, shape, jnp.float32) * 0.02
        return {'k': jax.random.normal(ks[0], (B, M, D), jnp.float32), 'v': jax.random.normal(ks[1], (B, M, D), jnp.float32), 'q': jax.random.normal(ks[2], (B, M, D), jnp.float32), 'mask': jnp.zeros((B, M), jnp.int32), 'Wk': w(ks[3], (D, D)), 'bk': jnp.zeros((D,), jnp.float32), 'Wv': w(ks[4], (D, D)), 'bv': jnp.zeros((D,), jnp.float32), 'Wq': w(ks[5], (D, D)), 'bq': jnp.zeros((D,), jnp.float32), 'Woff': w(ks[6], (H * NK, D)), 'boff': jnp.zeros((H * NK,), jnp.float32), 'Wo': w(ks[7], (D, D)), 'bo': jnp.zeros((D,), jnp.float32)}
    _L0_xattn_all = _L0_xattn_setup()
    _L0_xattn_in = {k: v for k, v in _L0_xattn_all.items() if k in ('Wk', 'bk', 'Wv', 'bv', 'Wq', 'bq', 'Woff', 'boff', 'Wo', 'bo')}
    del _L0_xattn_all

    def _L0_ffn_setup():
        import jax, jax.numpy as jnp
        import numpy as np
        B, S, D, H, E, K = (4, 512, 256, 1024, 8, 2)
        CAPACITY_FACTOR = 1.5
        C = int(CAPACITY_FACTOR * B * S * K / E)
        key = jax.random.key(seed)
        ks = jax.random.split(key, 6)
        x = jax.random.normal(ks[0], (B, S, D), dtype=jnp.float32)
        w_router = jax.random.normal(ks[1], (D, E), dtype=jnp.float32) * 0.02
        w1 = jax.random.normal(ks[2], (E, D, H), dtype=jnp.float32) * 0.02
        b1 = jnp.zeros((E, H), dtype=jnp.float32)
        w2 = jax.random.normal(ks[3], (E, H, D), dtype=jnp.float32) * 0.02
        b2 = jnp.zeros((E, D), dtype=jnp.float32)
        return {'x': x, 'w_router': w_router, 'w1': w1, 'b1': b1, 'w2': w2, 'b2': b2}
    _L0_ffn_all = _L0_ffn_setup()
    _L0_ffn_in = {k: v for k, v in _L0_ffn_all.items() if k in ('w_router', 'w1', 'b1', 'w2', 'b2')}
    del _L0_ffn_all
    return {'x': x, 'ctx_1024': ctx_1024, 'mask_BxS2_if0': mask_BxS2_if0, 'L0_attn_Wq': _L0_attn_in['Wq'], 'L0_attn_Wk': _L0_attn_in['Wk'], 'L0_attn_Wv': _L0_attn_in['Wv'], 'L0_attn_Wb': _L0_attn_in['Wb'], 'L0_attn_conv_q_w': _L0_attn_in['conv_q_w'], 'L0_attn_conv_k_w': _L0_attn_in['conv_k_w'], 'L0_attn_conv_v_w': _L0_attn_in['conv_v_w'], 'L0_attn_ms_w3': _L0_attn_in['ms_w3'], 'L0_attn_ms_w15': _L0_attn_in['ms_w15'], 'L0_attn_ms_w31': _L0_attn_in['ms_w31'], 'L0_attn_kernel_mix_w': _L0_attn_in['kernel_mix_w'], 'L0_attn_channel_mixer_w': _L0_attn_in['channel_mixer_w'], 'L0_attn_fusion_w1': _L0_attn_in['fusion_w1'], 'L0_attn_fusion_b1': _L0_attn_in['fusion_b1'], 'L0_attn_fusion_w2': _L0_attn_in['fusion_w2'], 'L0_attn_fusion_b2': _L0_attn_in['fusion_b2'], 'L0_attn_o_norm_w': _L0_attn_in['o_norm_w'], 'L0_attn_Wo': _L0_attn_in['Wo'], 'L0_xattn_Wk': _L0_xattn_in['Wk'], 'L0_xattn_bk': _L0_xattn_in['bk'], 'L0_xattn_Wv': _L0_xattn_in['Wv'], 'L0_xattn_bv': _L0_xattn_in['bv'], 'L0_xattn_Wq': _L0_xattn_in['Wq'], 'L0_xattn_bq': _L0_xattn_in['bq'], 'L0_xattn_Woff': _L0_xattn_in['Woff'], 'L0_xattn_boff': _L0_xattn_in['boff'], 'L0_xattn_Wo': _L0_xattn_in['Wo'], 'L0_xattn_bo': _L0_xattn_in['bo'], 'L0_ffn_w_router': _L0_ffn_in['w_router'], 'L0_ffn_w1': _L0_ffn_in['w1'], 'L0_ffn_b1': _L0_ffn_in['b1'], 'L0_ffn_w2': _L0_ffn_in['w2'], 'L0_ffn_b2': _L0_ffn_in['b2']}

def reference(x, ctx_1024, mask_BxS2_if0, L0_attn_Wq, L0_attn_Wk, L0_attn_Wv, L0_attn_Wb, L0_attn_conv_q_w, L0_attn_conv_k_w, L0_attn_conv_v_w, L0_attn_ms_w3, L0_attn_ms_w15, L0_attn_ms_w31, L0_attn_kernel_mix_w, L0_attn_channel_mixer_w, L0_attn_fusion_w1, L0_attn_fusion_b1, L0_attn_fusion_w2, L0_attn_fusion_b2, L0_attn_o_norm_w, L0_attn_Wo, L0_xattn_Wk, L0_xattn_bk, L0_xattn_Wv, L0_xattn_bv, L0_xattn_Wq, L0_xattn_bq, L0_xattn_Woff, L0_xattn_boff, L0_xattn_Wo, L0_xattn_bo, L0_ffn_w_router, L0_ffn_w1, L0_ffn_b1, L0_ffn_w2, L0_ffn_b2):
    import jax
    import jax.numpy as jnp

    def _L0_attn_ref(hidden_states, Wq, Wk, Wv, Wb, conv_q_w, conv_k_w, conv_v_w, ms_w3, ms_w15, ms_w31, kernel_mix_w, channel_mixer_w, fusion_w1, fusion_b1, fusion_w2, fusion_b2, o_norm_w, Wo):
        import jax, jax.numpy as jnp
        import numpy as np
        CHUNK = 32
        H = 4

        def silu(x):
            return x * jax.nn.sigmoid(x)

        def l2norm(x):
            return x * jax.lax.rsqrt(jnp.sum(x * x, -1, keepdims=True) + 1e-06)

        def dwconv_causal(x_cl, w):
            k = w.shape[1]
            xp = jnp.pad(x_cl, ((0, 0), (0, 0), (k - 1, 0)))
            return jax.lax.conv_general_dilated(xp, w[:, None, :], (1,), 'VALID', dimension_numbers=('NCH', 'OIH', 'NCH'), feature_group_count=x_cl.shape[1])

        def short_conv_silu(x_bld, w):
            y = dwconv_causal(jnp.swapaxes(x_bld, 1, 2), w)
            return silu(jnp.swapaxes(y, 1, 2))

        def delta_rule_chunkwise(q, k, v, beta, chunk=CHUNK):
            b, h, L, dk = q.shape
            dv = v.shape[-1]
            pad = -L % chunk
            if pad:
                q, k, v = (jnp.pad(t, ((0, 0), (0, 0), (0, pad), (0, 0))) for t in (q, k, v))
                beta = jnp.pad(beta, ((0, 0), (0, 0), (0, pad)))
            n = (L + pad) // chunk
            q = l2norm(q)
            k = l2norm(k)
            v = v * beta[..., None]
            kb = k * beta[..., None]
            ch = lambda x: x.reshape(b, h, n, chunk, x.shape[-1])
            qc, kc, vc, kbc = map(ch, (q, k, v, kb))
            idx = jnp.arange(chunk)
            strict_lower = (idx[:, None] > idx[None, :]).astype(q.dtype)
            incl_lower = (idx[:, None] >= idx[None, :]).astype(q.dtype)
            attn = -jnp.einsum('bhncd,bhned->bhnce', kbc, kc) * strict_lower
            for i in range(1, chunk):
                upd = jnp.einsum('...j,...ji->...i', attn[..., i, :], attn[..., :, :i])
                attn = attn.at[..., i, :i].add(upd)
            attn = attn + jnp.eye(chunk, dtype=q.dtype)
            u = attn @ vc
            w = attn @ kbc
            xs = tuple((jnp.moveaxis(t, 2, 0) for t in (qc, kc, u, w)))
            S0 = jnp.zeros((b, h, dk, dv), q.dtype)

            def step(S, x):
                qi, ki, ui, wi = x
                a_loc = jnp.einsum('bhcd,bhed->bhce', qi, ki) * incl_lower
                ui = ui - wi @ S
                oi = qi @ S + a_loc @ ui
                S = S + jnp.einsum('bhcd,bhcv->bhdv', ki, ui)
                return (S, oi)
            S, o = jax.lax.scan(step, S0, xs)
            o = jnp.moveaxis(o, 0, 2).reshape(b, h, n * chunk, dv)[:, :, :L]
            return (o, S)

        def multiscale_conv(v, ms_w3, ms_w15, ms_w31, kernel_mix_w, channel_mixer_w):
            b, l, h, d = v.shape
            x = jnp.swapaxes(v.reshape(b, l, h * d), 1, 2)
            outs = [dwconv_causal(x, w) for w in (ms_w3, ms_w15, ms_w31)]
            y = jnp.concatenate(outs, axis=1)
            y = y.reshape(b, h, 3 * d, l).transpose(0, 3, 1, 2)
            y = y @ kernel_mix_w
            y = (y.reshape(b, l, h * d) @ channel_mixer_w).reshape(b, l, h, d)
            return y

        def _forward(hidden_states, Wq, Wk, Wv, Wb, conv_q_w, conv_k_w, conv_v_w, ms_w3, ms_w15, ms_w31, kernel_mix_w, channel_mixer_w, fusion_w1, fusion_b1, fusion_w2, fusion_b2, o_norm_w, Wo):
            b, L, D = hidden_states.shape
            h = H
            dk = Wq.shape[1] // h
            dv = Wv.shape[1] // h
            q = short_conv_silu(hidden_states @ Wq, conv_q_w).reshape(b, L, h, dk)
            k = short_conv_silu(hidden_states @ Wk, conv_k_w).reshape(b, L, h, dk)
            v = short_conv_silu(hidden_states @ Wv, conv_v_w).reshape(b, L, h, dv)
            v_direct = v
            beta = jax.nn.sigmoid(hidden_states @ Wb)
            tr = lambda x: jnp.swapaxes(x, 1, 2)
            delta_out, _S = delta_rule_chunkwise(tr(q), tr(k), tr(v), tr(beta))
            delta_out = jnp.swapaxes(delta_out, 1, 2)
            ms_out = multiscale_conv(v_direct, ms_w3, ms_w15, ms_w31, kernel_mix_w, channel_mixer_w)
            bn = lambda x: jnp.mean(jnp.abs(x), -1)
            gate_features = jnp.concatenate([hidden_states, bn(ms_out), bn(delta_out), bn(v_direct)], -1)
            hdn = jax.nn.gelu(gate_features @ fusion_w1 + fusion_b1, approximate=False)
            logits = (hdn @ fusion_w2 + fusion_b2).reshape(b, L, h, 3)
            wts = jax.nn.softmax(logits, -1)
            o = wts[..., 0:1] * ms_out + wts[..., 1:2] * delta_out + wts[..., 2:3] * v_direct
            o = o * jax.lax.rsqrt(jnp.mean(o * o, -1, keepdims=True) + 1e-05) * o_norm_w
            return o.reshape(b, L, h * dv) @ Wo
        return _forward(hidden_states, Wq, Wk, Wv, Wb, conv_q_w, conv_k_w, conv_v_w, ms_w3, ms_w15, ms_w31, kernel_mix_w, channel_mixer_w, fusion_w1, fusion_b1, fusion_w2, fusion_b2, o_norm_w, Wo)

    def _L0_xattn_ref(k, v, q, mask, Wk, bk, Wv, bv, Wq, bq, Woff, boff, Wo, bo):
        import jax, jax.numpy as jnp
        import numpy as np
        import math
        B, M, D, H, NK = (4, 512, 256, 16, 5)
        HD = D // H

        def _gather_pad0(x, idx):
            Bx, Hx, W, hd = x.shape
            valid = (idx >= 0) & (idx < W)
            idxc = jnp.clip(idx, 0, W - 1).reshape(Bx, Hx, -1)
            g = jnp.take_along_axis(x, idxc[..., None], axis=2)
            g = g.reshape(idx.shape + (hd,))
            return g * valid[..., None].astype(x.dtype)
        Bq, Q, _ = q.shape
        key_len = k.shape[1]
        K = jnp.einsum('bmd,ed->bme', k, Wk) + bk
        V = jnp.einsum('bmd,ed->bme', v, Wv) + bv
        Qp = jnp.einsum('bqd,ed->bqe', q, Wq) + bq
        off = jnp.einsum('bqd,ed->bqe', Qp, Woff) + boff
        off = off.reshape(Bq, Q, H, NK).transpose(0, 2, 1, 3)
        Kh = K.reshape(Bq, key_len, H, HD).transpose(0, 2, 1, 3)
        Vh = V.reshape(Bq, key_len, H, HD).transpose(0, 2, 1, 3)
        Qh = Qp.reshape(Bq, Q, H, HD).transpose(0, 2, 1, 3)
        loc = jnp.arange(Q, dtype=jnp.float32)[:, None]
        left = -NK // 2
        ref = jnp.arange(left, NK + left, dtype=jnp.float32)
        sign_lens = (1 - mask).sum(-1).astype(jnp.float32) - 1.0
        loc_x = jnp.mod(ref + off + loc, sign_lens[:, None, None, None])
        xg = loc_x / (key_len - 1) * 2.0 - 1.0
        ix = ((xg + 1.0) * key_len - 1.0) / 2.0
        x0 = jnp.floor(ix)
        dx = ix - x0
        i0 = x0.astype(jnp.int32)
        i1 = i0 + 1
        w0 = (1.0 - dx)[..., None]
        w1 = dx[..., None]
        sk = 0.5 * (w0 * _gather_pad0(Kh, i0) + w1 * _gather_pad0(Kh, i1))
        sv = 0.5 * (w0 * _gather_pad0(Vh, i0) + w1 * _gather_pad0(Vh, i1))
        scores = jnp.einsum('bhqd,bhqkd->bhqk', Qh / math.sqrt(HD), sk)
        attn = jax.nn.softmax(scores, axis=-1)
        ctx = jnp.einsum('bhqk,bhqkd->bhqd', attn, sv)
        ctx = ctx.transpose(0, 2, 1, 3).reshape(Bq, Q, H * HD)
        return jnp.einsum('bqd,ed->bqe', ctx, Wo) + bo

    def _L0_ffn_ref(x, w_router, w1, b1, w2, b2):
        import jax, jax.numpy as jnp
        import numpy as np
        B, S, D, H, E, K = (4, 512, 256, 1024, 8, 2)
        CAPACITY_FACTOR = 1.5
        C = int(CAPACITY_FACTOR * B * S * K / E)
        Bs, Ss, Ds = x.shape
        N = Bs * Ss
        xf = x.reshape(N, Ds)
        logits = xf @ w_router
        probs = jax.nn.softmax(logits, axis=-1)
        gate, eidx = jax.lax.top_k(probs, K)
        gate = gate / jnp.sum(gate, axis=-1, keepdims=True)
        oh = jax.nn.one_hot(eidx, E, dtype=jnp.float32)
        ohf = oh.reshape(N * K, E)
        pos = jnp.cumsum(ohf, axis=0) - 1.0
        posk = jnp.sum(pos * ohf, axis=-1).reshape(N, K).astype(jnp.int32)
        keep = posk < C
        gate = gate * keep.astype(gate.dtype)
        e_flat = eidx.reshape(-1)
        p_flat = jnp.where(keep, posk, 0).reshape(-1)
        contrib = (xf[:, None, :] * keep[..., None].astype(xf.dtype)).reshape(N * K, Ds)
        expert_in = jnp.zeros((E, C, Ds), dtype=xf.dtype).at[e_flat, p_flat].add(contrib)
        h = jax.nn.relu(jnp.einsum('ecd,edh->ech', expert_in, w1) + b1[:, None, :])
        expert_out = jnp.einsum('ech,eho->eco', h, w2) + b2[:, None, :]
        tok = expert_out[e_flat, p_flat].reshape(N, K, -1)
        y = jnp.sum(tok * gate[..., None], axis=1)
        return y.reshape(Bs, Ss, -1)
    x = _layernorm(x + _L0_attn_ref(x, L0_attn_Wq, L0_attn_Wk, L0_attn_Wv, L0_attn_Wb, L0_attn_conv_q_w, L0_attn_conv_k_w, L0_attn_conv_v_w, L0_attn_ms_w3, L0_attn_ms_w15, L0_attn_ms_w31, L0_attn_kernel_mix_w, L0_attn_channel_mixer_w, L0_attn_fusion_w1, L0_attn_fusion_b1, L0_attn_fusion_w2, L0_attn_fusion_b2, L0_attn_o_norm_w, L0_attn_Wo), axis=-1)
    x = _layernorm(x + _L0_xattn_ref(ctx_1024, ctx_1024, x, mask_BxS2_if0, L0_xattn_Wk, L0_xattn_bk, L0_xattn_Wv, L0_xattn_bv, L0_xattn_Wq, L0_xattn_bq, L0_xattn_Woff, L0_xattn_boff, L0_xattn_Wo, L0_xattn_bo), axis=-1)
    x = _layernorm(x + _L0_ffn_ref(x, L0_ffn_w_router, L0_ffn_w1, L0_ffn_b1, L0_ffn_w2, L0_ffn_b2), axis=-1)
    return x

_drawn_inputs = setup_inputs


def setup_inputs(seed=0):
    import zlib

    import numpy as np

    out = dict(_drawn_inputs(seed))
    spreads = {'L0_attn_fusion_b1': (0.0, 0.282),
     'L0_attn_o_norm_w': (1.0, 0.2),
     'L0_xattn_bk': (0.0, 0.8),
     'L0_xattn_bv': (0.0, 0.308),
     'L0_xattn_bq': (0.0, 0.8),
     'L0_xattn_boff': (0.0, 0.8),
     'L0_xattn_bo': (0.0, 0.1),
     'L0_ffn_b1': (0.0, 0.1),
     'L0_ffn_b2': (0.0, 0.1)}
    factors = {'L0_attn_ms_w3': 2.693, 'L0_xattn_Wk': 8.0, 'L0_xattn_Wq': 8.0, 'L0_xattn_Woff': 7.748}
    for name, (base, spread) in spreads.items():
        noise = np.random.default_rng([zlib.crc32(name.encode()), seed]).standard_normal(out[name].shape)
        drawn = base * np.exp(spread * noise) if base else spread * noise
        out[name] = jnp.asarray(drawn.astype(out[name].dtype))
    for name, factor in factors.items():
        out[name] = (out[name] * factor).astype(out[name].dtype)
    return out
```

```python
from contextlib import ExitStack

import concourse.bass as bass
from concourse import mybir

P = 128
B, T, D = 8, 256, 256
NC = T // P
H, HD = 4, 64
S2 = 120
XH, XD, NK = 16, 16, 5
E, TOPK, HID = 8, 2, 1024
CAP = int(1.5 * 4 * 512 * TOPK / E)
NT = CAP // P
EPS = 1e-5
TAPS = (3, 15, 31)
PAD = max(TAPS) - 1

(M_DIAG8, M_IN32, M_IN128, M_DIAG8T, M_IN32T, M_IN128T, M_INCL, M_EYE, M_BEFORE, M_ONES) = range(10)
NMASK = 10
ROUND = 1.5 * 2.0 ** 23
ZEROED, PREPARED = 8, 4
TAP_ORDER = [(tap, s, hf) for tap in range(max(TAPS)) for s in range(3) for hf in range(2)
             if tap < TAPS[s]]
TAP_AT = {tap: n for n, tap in enumerate(TAP_ORDER)}

INVERSE = ["gram", "gramT", "P2", "P2T", "P4", "T2T", "T8T", "T8", "W", "WT", "W2", "U", "T32T",
           "T32", "Y", "YT", "Y2", "V", "TT", "aT"]
A_USES = (["k_proj", "v_proj", "q_proj", "sums", "k_tok", "v_tok", "k_chan"]
          + [f"{s}{c}" for s in INVERSE for c in range(NC)]
          + ["u0", "wT1", "S0", "o0", "u1", "o1"]
          + ["mix", "ms", "statT", "hid0", "hid1", "logit", "oT", "attn"])
B_USES = (["Kt", "Vt", "x1T", "Qc", "off0", "off1", "Qt"]
          + [f"dist{k}{half}_{j}" for k in range(NK) for half in range(2) for j in range(XH // 4)]
          + ["ctxT", "xout", "x2T", "route", "pos"])
G_USES = [f"gather{k}_{c}" for k in range(NK) for c in range(NC)]
C_USES = ([f"xeT{j}" for j in range(NT // 2)] + [f"h{m}{a}" for m in range(HID // P) for a in "ab"]
          + [f"y{j}" for j in range(NT // 2)])

PER = dict(
    xT_in=16, xt_in=16, conv=24, tanh=3, silu=3, sq=2, rinv=2, beta_th=1, beta=2, vb=1, kb=1,
    x8=2, t1=2, taps=98, stat=3, fuse=6, wexp=1, v3=1, osum=2, osq=1, orms=2, orr=1, on=1,
    var1=4, rstd1=1, x1=2,
    ctx_in=16, mask_in=16, length=4, ixp=13, nhat=10, hats_used=5, prod=5, scr=5, scs=2, sexp=1, att=3, av=1,
    av0=1, actx=2, var2=5, rstd2=1, x2=2, rmax=2, rexp=1, top=11, ohs=2, count=2, slots=12,
    x2_out=16, slot_out=16, gate_out=16, scatter=64,
    w_in0=32, w_in1=32, be_in0=32, be_in1=32, xe_in0=16, xe_in1=16, y_out=16,
    f_in0=48, f_in1=48, row_in0=64, row_in1=64, mix=4, fvar=4, frs=1, fo=2, out_done=16,
)


def at_least(eng, semaphore, value):
    if not (isinstance(value, int) and value <= 0):
        eng.wait_ge(semaphore, value)


def bank_ring(ctx, nc, name, uses, banks):
    return dict(
        use={u: n for n, u in enumerate(uses)}, uses=len(uses), banks=banks,
        filled=ctx.enter_context(nc.semaphore(f"{name}_filled")),
        read=[ctx.enter_context(nc.semaphore(f"{name}_read{b}")) for b in range(len(banks))],
        per=[len(range(b, len(uses), len(banks))) for b in range(len(banks))])


def place(ring, use):
    return ring["use"][use] % len(ring["banks"]), ring["use"][use] // len(ring["banks"])


def bank_of(ring, use):
    return ring["banks"][place(ring, use)[0]]


def was_read(ring, use):
    return ring["read"][place(ring, use)[0]]


def wait_read(ring, eng, i, *uses):
    last = {}
    for b, n in [place(ring, u) for u in uses]:
        last[b] = max(n, last[b]) if b in last else n
    for b in last:
        eng.wait_ge(ring["read"][b], i * ring["per"][b] + last[b] + 1)


def take(ring, pe, i, use, *after):
    b, n = place(ring, use)
    at_least(pe, ring["read"][b], i * ring["per"][b] + n)
    wait_read(ring, pe, i, *[u for u in after if place(ring, u)[0] != b])
    return ring["banks"][b]


def wait_filled(ring, eng, i, use):
    eng.wait_ge(ring["filled"], i * ring["uses"] + ring["use"][use] + 1)
    return bank_of(ring, use)


def wait_filled_before(ring, eng, i):
    at_least(eng, ring["filled"], i * ring["uses"])


def decoder_layer(nc, x_tok, xT, ctxT, mask, wqkv, wb, convw, msw, kmix, cmix, fw1, fw1s, fb1, fw2,
                  fb2, onorm, wo, xwT, xbias, xbq, woff, boff, ref_pos, wr, w1, b1, w2, b2, masks,
                  headsel, selector, positions, expert_ids, out):
    f32, bf16, u32 = mybir.dt.float32, mybir.dt.bfloat16, mybir.dt.uint32
    i32 = mybir.dt.int32
    ALU, ACT, AX = mybir.AluOpType, mybir.ActivationFunctionType, mybir.AxisListType

    x2_dram = nc.dram_tensor("x2_rows", (B, P, NC, D), f32).ap()
    slot_dram = nc.dram_tensor("slots", (B, P, NC * TOPK), u32).ap()
    gate_dram = nc.dram_tensor("gates", (B, P, NC * TOPK), f32).ap()
    xe_dram = nc.dram_tensor("expert_in", (E * CAP, D), f32).ap()
    ye_dram = nc.dram_tensor("expert_out", (E * CAP, D), f32).ap()

    ctx = ExitStack()
    with ctx:
        phase1 = ExitStack()

        def keep(name, shape, dt=f32):
            return ctx.enter_context(nc.sbuf_tensor(name, shape, dt))

        def sb(name, shape, dt=f32):
            return phase1.enter_context(nc.sbuf_tensor(name, shape, dt))

        sem = {n: ctx.enter_context(nc.semaphore(n)) for n in PER}
        consts_in = ctx.enter_context(nc.semaphore("consts_in"))
        zeroed = ctx.enter_context(nc.semaphore("zeroed"))
        xe_zero = ctx.enter_context(nc.semaphore("xe_zero"))
        prepared = ctx.enter_context(nc.semaphore("prepared"))

        psum = [ctx.enter_context(nc.psum_tensor(f"bank{b}", [P, 512], f32)) for b in range(8)]
        A = bank_ring(ctx, nc, "A", A_USES, psum[0:4])
        Bk = bank_ring(ctx, nc, "B", B_USES, psum[4:6])
        G = bank_ring(ctx, nc, "G", G_USES, psum[6:8])
        C = bank_ring(ctx, nc, "C", C_USES, psum)

        mk = keep("masks", [P, NMASK, P])
        half_m = keep("minus_half", [P, 16])
        wqkv_sb = sb("wqkv", [P, 3, 2, D])
        wb_sb = sb("wb", [P, 2, H])
        convw_sb = sb("convw", [P, 3, 2, 4])
        msw_sb = [sb(f"msw{s}", [P, 2, TAPS[s]]) for s in range(3)]
        kmix_sb = sb("kmix", [P, 6, P])
        cmix_sb = sb("cmix", [P, 2, D])
        fw1_sb = sb("fw1", [P, 2, 2 * D])
        fw1s_sb = sb("fw1s", [3 * H, 2 * D])
        fb1_sb = sb("fb1", [P, 4])
        fw2_sb = sb("fw2", [P, 4, 3 * H])
        fb2_sb = sb("fb2", [P, 3 * H])
        onorm_sb = sb("onorm", [P, 1])
        wo_sb = sb("wo", [P, 2, D])
        xwT_sb = sb("xwT", [P, 4, 2, D])
        bq_sb = sb("bq", [P, 2])
        xb_sb = sb("xb", [P, 3, D])
        woff_sb = sb("woff", [P, 2, 3, 96])
        offb_sb = sb("offb", [96, 3])
        refp_sb = sb("refp", [96, 3])
        offc_sb = sb("offc", [96, 3])
        wr_sb = sb("wr", [P, 2, E])
        headsel_sb = sb("headsel", [P, 2])
        sel_sb = sb("sel", [97, 32, S2], bf16)
        posq = sb("posq", [96, T])
        eids = sb("eids", [P, E])

        xT_sb = sb("xT", [P, 2, T])
        xt_sb = sb("x_tok", [P, NC, D])
        pre = sb("pre", [P, 3, 2, 3 + T])
        y = sb("y", [P, 3, 2, T])
        th = sb("th", [P, 3, 2, T])
        qk = sb("qk", [P, 2, 2, T])
        vpad = sb("vpad", [P, 2, PAD + T])
        sq = th
        sums = sb("sums", [P, 24])
        rinv = sb("rinv", [P, NC, 2, H])
        bth = sb("bth", [P, NC, H])
        beta = sb("beta", [P, NC, H])
        nbeta = sb("nbeta", [P, NC, H])
        kn = sb("kn", [P, NC, D])
        vt = sb("vt", [P, NC, D])
        vb = sb("vb", [P, NC, D])
        kb = sb("kb", [P, D])
        kz = sb("kz", [P, 2, 2, T])
        XT = [[sb(f"XT{s}_{c}", [P, H, P]) for s in range(3)] for c in range(NC)]
        W = [[sb(f"W{s}_{c}", [P, H, P]) for s in range(3)] for c in range(NC)]
        Ta = [sb(f"Ta{c}", [P, H, P]) for c in range(NC)]
        Tb = [sb(f"Tb{c}", [P, H, P]) for c in range(NC)]
        Tn = [sb(f"Tn{c}", [P, H, P]) for c in range(NC)]
        nbG = [W[c][2] for c in range(NC)]
        X8 = Tb
        aT = Tn
        u_sb = [sb(f"u{c}", [P, D]) for c in range(NC)]
        wTn = sb("wTn", [P, 2, P])
        S_sb = sb("S", [P, H, HD])
        delta = sb("delta", [P, NC, D])
        acc = sb("acc", [P, 3, 2, T])
        y1 = y[:, 0, :, :]
        ms = sb("ms", [P, NC, D])
        st = sb("st", [P, NC, 3 * H])
        gst = sb("gst", [3 * H, T])
        hdn = y[:, 1:3, :, :].rearrange("p a b t -> p (a b) t")
        lg = sb("lg", [P, NC * H, 3])
        lmx = sb("lmx", [P, NC * H])
        lex = sb("lex", [P, NC * H, 3])
        wts = sb("wts", [P, NC * H, 3])
        o1 = sb("o1", [P, NC, D])
        o2 = sb("o2", [P, NC, D])
        o3 = sb("o3", [P, NC, D])
        rms = sb("rms", [P, NC * H])
        rrms = sb("rrms", [P, NC * H])
        oT = qk[:, 0, :, :]
        bns = sb("bns", [P, NC, 6])
        mv = sb("mv", [P, NC, 2])
        ve = sb("ve", [P, NC])
        rstd = sb("rstd", [P, NC])
        xr = o3
        x1 = sb("x1", [P, NC, D])

        ctxT_sb = sb("ctxT", [P, 2, S2])
        mask_sb = sb("mask", [96, S2], i32)
        maskf = sb("maskf", [96, S2])
        msum = sb("msum", [96, 1])
        Lb = sb("L", [96, 1])
        rL = sb("rL", [96, 1])
        x1T = sb("x1T", [P, 2, T])
        QT = sb("QT", [P, 2, T])
        Qs = sb("Qs", [P, NC, D])
        ixp = sb("ixp", [97, 3, T], bf16)
        tab = sb("tab", [S2, XH, 2, XD])
        nhat = [sb(f"nhat{j}", [S2, XH // 2, T]) for j in range(2)]
        loc = nhat[1][0:96, 0:3, :]
        tmp = nhat[1][0:96, 3:6, :]
        gs = sb("gs", [P, NC, NK, XH, 2, XD])
        prod = [sb(f"prod{j}", [P, NC, XH, XD]) for j in range(2)]
        sc = sb("sc", [P, NC, NK, XH])
        scm = sb("scm", [P, NC, XH])
        scd = sb("scd", [P, NC, NK, XH])
        sce = sb("sce", [P, NC, NK, XH])
        av = gs[:, :, :, :, 1, :]
        actx = sb("actx", [P, NC, D])
        cT = x1T
        bns2 = sb("bns2", [P, NC, 6])
        mv2 = sb("mv2", [P, NC, 2])
        ve2 = sb("ve2", [P, NC])
        rstd2 = sb("rstd2", [P, NC])
        xr2 = actx
        x2 = sb("x2", [P, NC, D])
        x2T = QT
        pr = sb("pr", [P, NC, E])
        prm = sb("prm", [P, NC])
        prd = sb("prd", [P, NC, E])
        prx = sb("prx", [P, NC, E])
        top = sb("top", [P, NC, E])
        topi = sb("topi", [P, NC, E], u32)
        topf = sb("topf", [P, NC, E])
        gsum = sb("gsum", [P, NC])
        oh = sb("oh", [P, NC, TOPK, E])
        ohs = sb("ohs", [P, NC, E])
        count = sb("count", [P, E])
        pos = sb("pos", [P, NC, E])
        psel = sb("psel", [P, NC, TOPK, E])
        esel = sb("esel", [P, NC, TOPK, E])
        junk = sb("junk", [P, 2])
        pk = sb("pk", [P, NC, TOPK])
        ek = sb("ek", [P, NC, TOPK])
        drop = sb("drop", [P, NC, TOPK])
        gate = sb("gate", [P, NC, TOPK])
        gslot = sb("gslot", [P, NC, TOPK])
        sslot = sb("sslot", [P, NC, TOPK])
        gslot_i = sb("gslot_i", [P, NC * TOPK], u32)
        sslot_i = sb("sslot_i", [P, NC * TOPK], u32)
        zero = gs[:, :, :, :, :, :].rearrange("p a b c d e -> p (a b c d e)")[:, 0:4096]

        phase1.close()
        w1_sb = [keep(f"w1_{j}", [P, 2, HID]) for j in range(2)]
        w2_sb = [keep(f"w2_{j}", [P, HID // P, D]) for j in range(2)]
        xe = [ctx.enter_context(nc.sbuf_tensor(f"xe{j}", [P, NT, D], f32)) for j in range(2)]
        xeT = ctx.enter_context(nc.sbuf_tensor("xeT", [P, 2, CAP], f32))
        hT = ctx.enter_context(nc.sbuf_tensor("hT", [P, HID // P, CAP], f32))
        ye = [ctx.enter_context(nc.sbuf_tensor(f"ye{j}", [P, NT, D], f32)) for j in range(2)]
        b1_sb = [ctx.enter_context(nc.sbuf_tensor(f"b1_{j}", [P, HID // P], f32)) for j in range(2)]
        b2_sb = [ctx.enter_context(nc.sbuf_tensor(f"b2_{j}", [P, D], f32)) for j in range(2)]
        fx = [ctx.enter_context(nc.sbuf_tensor(f"fx{j}", [P, NC, D], f32)) for j in range(2)]
        fslot = [ctx.enter_context(nc.sbuf_tensor(f"fslot{j}", [P, NC * TOPK], u32)) for j in range(2)]
        fgate = [ctx.enter_context(nc.sbuf_tensor(f"fgate{j}", [P, NC * TOPK], f32)) for j in range(2)]
        frow = [ctx.enter_context(nc.sbuf_tensor(f"frow{j}", [P, NC, TOPK, D], f32)) for j in range(2)]
        fy = [ctx.enter_context(nc.sbuf_tensor(f"fy{j}", [P, NC, D], f32)) for j in range(2)]
        fbn = [ctx.enter_context(nc.sbuf_tensor(f"fbn{j}", [P, NC, 6], f32)) for j in range(2)]
        fmv = [ctx.enter_context(nc.sbuf_tensor(f"fmv{j}", [P, NC, 2], f32)) for j in range(2)]
        fve = [ctx.enter_context(nc.sbuf_tensor(f"fve{j}", [P, NC], f32)) for j in range(2)]
        frs = [ctx.enter_context(nc.sbuf_tensor(f"frs{j}", [P, NC], f32)) for j in range(2)]
        fo = [ctx.enter_context(nc.sbuf_tensor(f"fo{j}", [P, NC, D], f32)) for j in range(2)]

        eye = mk[:, M_EYE, :]

        def mask4(m):
            return mk[:, m, :].unsqueeze(1).broadcast_to([P, H, P])

        def heads(ap, width=HD):
            return ap.unsqueeze(3).broadcast_to([P, NC, H, width])

        def split(ap, h=H):
            return ap.rearrange("p c (h d) -> p c h d", h=h)

        block = ctx.enter_context(nc.Block())

        loads = [
            (mk[:, :, :], masks), (wqkv_sb[:, :, :, :], wqkv), (wb_sb[:, :, :], wb),
            (convw_sb[:, :, :, :], convw), (kmix_sb[:, :, :], kmix), (cmix_sb[:, :, :], cmix),
            (fw1_sb[:, :, :], fw1), (fw1s_sb[:, :], fw1s), (fb1_sb[:, :], fb1),
            (fw2_sb[:, :, :], fw2), (fb2_sb[:, :], fb2.partition_broadcast(P)),
            (onorm_sb[0:HD, :], onorm), (onorm_sb[HD:P, :], onorm), (wo_sb[:, :, :], wo),
            (xwT_sb[:, :, :, :], xwT), (bq_sb[:, :], xbq),
            (xb_sb[:, :, :], xbias.partition_broadcast(P)), (wr_sb[:, :, :], wr),
            (headsel_sb[:, :], headsel), (sel_sb[:, :, :], selector),
            (posq[:, :], positions.partition_broadcast(96)),
            (eids[:, :], expert_ids.partition_broadcast(P)),
            (offb_sb[:, :], boff), (refp_sb[:, :], ref_pos), (woff_sb[:, :, :, :], woff),
        ] + [(msw_sb[s][:, :, :], msw[s]) for s in range(3)]
        CONSTS = 16 * len(loads)

        @block.sync
        def _(sp):
            def a_loads(i):
                wait_filled_before(A, sp, i)
                sp.dma_start(xT_sb[:, :, :], xT[i, :, :, :]).then_inc(sem["xT_in"], 16)
                sp.wait_ge(sem["x1"], i * PER["x1"])
                sp.dma_start(xt_sb[:, :, :], x_tok[i, :, :, :]).then_inc(sem["xt_in"], 16)

            def b_loads(i):
                wait_filled_before(Bk, sp, i)
                sp.dma_start(ctxT_sb[:, :, :], ctxT[i, :, :, :]).then_inc(sem["ctx_in"], 16)
                sp.wait_ge(sem["ixp"], i * PER["ixp"])
                sp.dma_start(mask_sb[:, :], mask[i, :].partition_broadcast(96))\
                    .then_inc(sem["mask_in"], 16)

            def stores(i):
                sp.wait_ge(sem["x2"], (i + 1) * PER["x2"])
                sp.dma_start(x2_dram[i, :, :, :], x2[:, :, :]).then_inc(sem["x2_out"], 16)
                sp.wait_ge(sem["slots"], (i + 1) * PER["slots"])
                sp.dma_start(slot_dram[i, :, :], gslot_i[:, :]).then_inc(sem["slot_out"], 16)
                sp.dma_start(gate_dram[i, :, :], gate[:, :, :].rearrange("p c k -> p (c k)"))\
                    .then_inc(sem["gate_out"], 16)

            def load_weights(e, j):
                sp.dma_start(w1_sb[j][:, :, :], w1[e, :, :, :]).then_inc(sem[f"w_in{j}"], 16)
                sp.dma_start(w2_sb[j][:, :, :], w2[e, :, :, :]).then_inc(sem[f"w_in{j}"], 16)

            def load_rows(e, j):
                sp.dma_start(b1_sb[j][:, :], b1[e, :, :]).then_inc(sem[f"be_in{j}"], 16)
                sp.dma_start(b2_sb[j][:, :], b2[e, :].partition_broadcast(P))\
                    .then_inc(sem[f"be_in{j}"], 16)
                sp.dma_start(xe[j][:, :, :],
                             xe_dram[bass.ts(e, CAP), :].rearrange("(t p) d -> p t d", p=P))\
                    .then_inc(sem[f"xe_in{j}"], 16)

            for dst, src in loads:
                sp.dma_start(dst, src).then_inc(consts_in, 16)
            with sp.Fori(0, B) as i:
                a_loads(i)
                b_loads(i)
                stores(i)
            sp.wait_ge(sem["scatter"], B * PER["scatter"])
            sp.wait_ge(sem["gate_out"], B * PER["gate_out"])
            sp.wait_ge(sem["slot_out"], B * PER["slot_out"])
            sp.wait_ge(sem["x2_out"], B * PER["x2_out"])
            for j in range(2):
                load_weights(j, j)
                load_rows(j, j)

            def store_expert(e, j):
                wait_read(C, sp, e, C_USES[-1])
                sp.dma_start(ye_dram[bass.ts(e, CAP), :].rearrange("(t p) d -> p t d", p=P),
                             ye[j][:, :, :]).then_inc(sem["y_out"], 16)

            with sp.Fori(0, E // 2 - 1) as pair:
                for j in range(2):
                    e = pair * 2 + j
                    store_expert(e, j)
                    load_weights(e + 2, j)
                    load_rows(e + 2, j)
            for j in range(2):
                store_expert(E - 2 + j, j)

            def d_loads(i, j):
                sp.dma_start(fx[j][:, :, :], x2_dram[i, :, :, :]).then_inc(sem[f"f_in{j}"], 16)
                sp.dma_start(fslot[j][:, :], slot_dram[i, :, :]).then_inc(sem[f"f_in{j}"], 16)
                sp.dma_start(fgate[j][:, :], gate_dram[i, :, :]).then_inc(sem[f"f_in{j}"], 16)

            def d_store(i, j):
                sp.wait_ge(sem["fo"], (i + 1) * PER["fo"])
                sp.dma_start(out[i, :, :, :], fo[j][:, :, :]).then_inc(sem["out_done"], 16)

            for j in range(2):
                d_loads(j, j)
            with sp.Fori(0, B // 2 - 1) as pair:
                for j in range(2):
                    d_store(pair * 2 + j, j)
                    d_loads(pair * 2 + j + 2, j)
            for j in range(2):
                d_store(B - 2 + j, j)
            sp.wait_ge(sem["out_done"], B * PER["out_done"])

        @block.tensor
        def _(pe):
            def mm(o, lhsT, rhs, first=True, last=True):
                return nc.tensor.matmul(o, lhsT, rhs, start=first, stop=last)

            def need(name, i, k):
                at_least(pe, sem[name], i * PER[name] + k)

            def turn(o, a, ident=None):
                return nc.tensor.transpose(o, a, eye if ident is None else ident)

            def turn_tiles(ring, i, use, src, *after):
                bank = take(ring, pe, i, use, *after)
                for hf in range(2):
                    for c in range(NC):
                        last = turn(bank[:, hf * T + c * P:hf * T + (c + 1) * P],
                                    src[:, c, hf * P:(hf + 1) * P])
                last.then_inc(ring["filled"], 1)

            def turn_chans(ring, i, use, src, *after):
                bank = take(ring, pe, i, use, *after)
                for c in range(NC):
                    for hf in range(2):
                        last = turn(bank[:, c * D + hf * P:c * D + (hf + 1) * P],
                                    src[:, hf, c * P:(c + 1) * P])
                last.then_inc(ring["filled"], 1)

            def chan_product(ring, i, use, w, src, *after, n=2):
                bank = take(ring, pe, i, use, *after)
                for m in range(n):
                    for k in range(2):
                        last = mm(bank[:, m * T:(m + 1) * T], w[:, k, m * P:(m + 1) * P],
                                  src[:, k, :], k == 0, k == 1)
                last.then_inc(ring["filled"], 1)

            def token_product(ring, i, use, src, w, *after):
                bank = take(ring, pe, i, use, *after)
                n = w.shape[2]
                for c in range(NC):
                    for k in range(2):
                        last = mm(bank[:, c * n:(c + 1) * n], src[:, k, c * P:(c + 1) * P],
                                  w[:, k, :], k == 0, k == 1)
                last.then_inc(ring["filled"], 1)

            def per_head(i, use, lhsT, rhs, after=()):
                bank = take(A, pe, i, use, *after)
                for h in range(H):
                    if rhs is None:
                        last = turn(bank[:, h * P:(h + 1) * P], lhsT(h))
                    else:
                        last = mm(bank[:, h * P:(h + 1) * P], lhsT(h), rhs(h))
                last.then_inc(A["filled"], 1)


            def stage_a(i):
                need("xT_in", i, 16)
                chan_product(A, i, "k_proj", wqkv_sb[:, 1, :, :], xT_sb)
                chan_product(A, i, "v_proj", wqkv_sb[:, 2, :, :], xT_sb)
                chan_product(A, i, "q_proj", wqkv_sb[:, 0, :, :], xT_sb)
                bank = take(A, pe, i, "sums")
                need("sq", i, 2)
                for c in range(NC):
                    for t in range(2):
                        for hf in range(2):
                            at = c * 8 + t * 4 + hf * 2
                            mm(bank[:, at:at + 2], sq[:, t, hf, c * P:(c + 1) * P], headsel_sb[:, :])
                for c in range(NC):
                    for k in range(2):
                        last = mm(bank[:, 16 + c * H:16 + (c + 1) * H],
                                  xT_sb[:, k, c * P:(c + 1) * P], wb_sb[:, k, :], k == 0, k == 1)
                last.then_inc(A["filled"], 1)
                turn_chans(A, i, "k_tok", qk[:, 1, :, :])
                need("silu", i, 2)
                turn_chans(A, i, "v_tok", vpad[:, :, PAD:])
                turn_tiles(A, i, "k_chan", kn, "k_tok")

                def chunk(c):
                    return slice(c * P, (c + 1) * P)

                steps = {
                    "gram": lambda c: per_head(i, f"gram{c}", lambda h: kz[:, h // 2, h % 2, chunk(c)],
                                               lambda h: kz[:, h // 2, h % 2, chunk(c)],
                                               ["k_chan"]),
                    "gramT": lambda c: per_head(i, f"gramT{c}", lambda h: nbG[c][:, h, :], None,
                                                [f"gram{c}"]),
                    "P2": lambda c: (need("x8", i, c + 1),
                                     per_head(i, f"P2{c}", lambda h: XT[c][0][:, h, :],
                                              lambda h: X8[c][:, h, :], [f"gramT{c}"])),
                    "P2T": lambda c: per_head(i, f"P2T{c}", lambda h: X8[c][:, h, :],
                                              lambda h: XT[c][0][:, h, :]),
                    "P4": lambda c: per_head(i, f"P4{c}", lambda h: W[c][1][:, h, :],
                                             lambda h: W[c][0][:, h, :], [f"P2{c}", f"P2T{c}"]),
                    "T2T": lambda c: (need("t1", i, c + 1),
                                      per_head(i, f"T2T{c}", lambda h: W[c][0][:, h, :],
                                               lambda h: Ta[c][:, h, :])),
                    "T8T": lambda c: per_head(i, f"T8T{c}", lambda h: W[c][2][:, h, :],
                                              lambda h: Tb[c][:, h, :], [f"P4{c}", f"T2T{c}"]),
                    "T8": lambda c: per_head(i, f"T8{c}", lambda h: Ta[c][:, h, :], None,
                                             [f"T8T{c}"]),
                    "aT": lambda c: per_head(i, f"aT{c}", lambda h: kz[:, h // 2, h % 2, chunk(c)],
                                             lambda h: qk[:, 0, h // 2, chunk(c)]),
                }
                for s, (t, w, wt, w2_, u, tt) in enumerate(
                        [("T8", "W", "WT", "W2", "U", "T32T"), ("T32", "Y", "YT", "Y2", "V", "TT")]):
                    def level(s=s, t=t, w=w, wt=wt, w2_=w2_, u=u, tt=tt):
                        xo = s + 1
                        return {
                            w: lambda c: per_head(i, f"{w}{c}", lambda h: XT[c][xo][:, h, :],
                                                  lambda h: Tn[c][:, h, :], [f"{t}{c}"]),
                            wt: lambda c: per_head(i, f"{wt}{c}", lambda h: Tn[c][:, h, :],
                                                   lambda h: XT[c][xo][:, h, :]),
                            w2_: lambda c: per_head(i, f"{w2_}{c}", lambda h: W[c][1][:, h, :],
                                                    lambda h: W[c][0][:, h, :],
                                                    [f"{w}{c}", f"{wt}{c}"]),
                            u: lambda c: per_head(i, f"{u}{c}", lambda h: W[c][2][:, h, :],
                                                  lambda h: Ta[c][:, h, :], [f"{w2_}{c}"]),
                            tt: lambda c: per_head(i, f"{tt}{c}", lambda h: W[c][0][:, h, :],
                                                   lambda h: Tb[c][:, h, :], [f"{u}{c}"]),
                        }
                    steps.update(level())
                steps["T32"] = lambda c: per_head(i, f"T32{c}", lambda h: Ta[c][:, h, :], None,
                                                  [f"T32T{c}"])
                for name in INVERSE:
                    for c in range(NC):
                        steps[name](c)

                need("vb", i, 1)
                bank = take(A, pe, i, "u0", "TT0")
                for h in range(H):
                    last = mm(bank[:, h * HD:(h + 1) * HD], Ta[0][:, h, :],
                              vb[:, 0, h * HD:(h + 1) * HD])
                last.then_inc(A["filled"], 1)
                need("kb", i, 1)
                bank = take(A, pe, i, "wT1", "TT1")
                for h in range(H):
                    last = mm(bank[(h % 2) * HD:(h % 2 + 1) * HD, (h // 2) * P:(h // 2 + 1) * P],
                              kb[:, h * HD:(h + 1) * HD], Ta[1][:, h, :])
                last.then_inc(A["filled"], 1)
                bank = take(A, pe, i, "S0", "u0")
                for h in range(H):
                    last = mm(bank[(h % 2) * HD:(h % 2 + 1) * HD, h * HD:(h + 1) * HD],
                              kn[:, 0, h * HD:(h + 1) * HD], u_sb[0][:, h * HD:(h + 1) * HD])
                last.then_inc(A["filled"], 1)
                bank = take(A, pe, i, "o0", "aT0")
                for h in range(H):
                    last = mm(bank[:, h * HD:(h + 1) * HD], aT[0][:, h, :],
                              u_sb[0][:, h * HD:(h + 1) * HD])
                last.then_inc(A["filled"], 1)
                bank = take(A, pe, i, "u1", "wT1", "S0")
                for h in range(H):
                    mm(bank[:, h * HD:(h + 1) * HD], Ta[1][:, h, :],
                       vb[:, 1, h * HD:(h + 1) * HD], True, False)
                    last = mm(bank[:, h * HD:(h + 1) * HD], wTn[:, h // 2, :], S_sb[:, h, :],
                              False, True)
                last.then_inc(A["filled"], 1)
                bank = take(A, pe, i, "o1", "u1", "aT1")
                for h in range(H):
                    mm(bank[:, h * HD:(h + 1) * HD], aT[1][:, h, :],
                       u_sb[1][:, h * HD:(h + 1) * HD], True, False)
                    last = mm(bank[:, h * HD:(h + 1) * HD], qk[:, 0, h // 2, P:T], S_sb[:, h, :],
                              False, True)
                last.then_inc(A["filled"], 1)

                need("taps", i, PER["taps"])
                bank = take(A, pe, i, "mix")
                for m in range(2):
                    for k in range(3):
                        j = 3 * m + k
                        last = mm(bank[:, m * T:(m + 1) * T], kmix_sb[:, j, :],
                                  acc[:, j // 2, j % 2, :], k == 0, k == 2)
                last.then_inc(A["filled"], 1)
                token_product(A, i, "ms", y1, cmix_sb, "mix")
                need("stat", i, 3)
                bank = take(A, pe, i, "statT")
                for c in range(NC):
                    last = turn(bank[0:3 * H, c * P:(c + 1) * P], st[:, c, :])
                last.then_inc(A["filled"], 1)
                for n in range(2):
                    bank = take(A, pe, i, f"hid{n}", "statT")
                    for m in range(2):
                        at = (2 * n + m) * P
                        for k in range(2):
                            mm(bank[:, m * T:(m + 1) * T], fw1_sb[:, k, at:at + P], xT_sb[:, k, :],
                               k == 0, False)
                        last = mm(bank[:, m * T:(m + 1) * T], fw1s_sb[:, at:at + P], gst[:, :],
                                  False, True)
                    last.then_inc(A["filled"], 1)
                bank = take(A, pe, i, "logit", "hid0", "hid1")
                for c in range(NC):
                    for m in range(4):
                        last = mm(bank[:, c * 3 * H:(c + 1) * 3 * H], hdn[:, m, c * P:(c + 1) * P],
                                  fw2_sb[:, m, :], m == 0, m == 3)
                last.then_inc(A["filled"], 1)
                need("on", i, 1)
                turn_tiles(A, i, "oT", o1)
                token_product(A, i, "attn", oT, wo_sb, "oT")

            def stage_b(i):
                need("ctx_in", i, 16)
                for use, t in (("Kt", 0), ("Vt", 1)):
                    bank = take(Bk, pe, i, use)
                    for k in range(2):
                        last = mm(bank[0:S2, 0:D], ctxT_sb[:, k, :], xwT_sb[:, t, k, :],
                                  k == 0, k == 1)
                    last.then_inc(Bk["filled"], 1)
                need("x1", i, 2)
                turn_tiles(Bk, i, "x1T", x1)
                chan_product(Bk, i, "Qc", xwT_sb[:, 2, :, :], x1T, "x1T")
                for n, groups in ((0, (0, 1)), (1, (2,))):
                    bank = take(Bk, pe, i, f"off{n}", "Qc")
                    for m, g in enumerate(groups):
                        for k in range(2):
                            last = mm(bank[0:96, m * T:(m + 1) * T], woff_sb[:, k, g, :],
                                      QT[:, k, :], k == 0, k == 1)
                    last.then_inc(Bk["filled"], 1)
                turn_chans(Bk, i, "Qt", QT)

                def distances(k, half):
                    for j in range(XH // 4):
                        bank = take(Bk, pe, i, f"dist{k}{half}_{j}")
                        for m in range(2):
                            r = (k % 2) * XH + half * XH // 2 + 2 * j + m
                            last = mm(bank[0:S2, m * T:(m + 1) * T], sel_sb[:, r, :],
                                      ixp[:, k // 2, :])
                        last.then_inc(Bk["filled"], 1)

                def gathers(k, half):
                    need("nhat", i, 2 * k + half + 1)
                    if k == 0 and half == 0:
                        wait_read(Bk, pe, i, "Kt", "Vt")
                    for c in range(NC):
                        use = f"gather{k}_{c}"
                        bank = bank_of(G, use) if half else take(G, pe, i, use)
                        for h in range(XH // 2):
                            head = half * XH // 2 + h
                            last = mm(bank[:, head * 32:(head + 1) * 32],
                                      nhat[half][:, h, c * P:(c + 1) * P],
                                      tab[:, head, :, :].rearrange("p a d -> p (a d)"))
                        if half:
                            last.then_inc(G["filled"], 1)
                    if not half:
                        last.then_inc(sem["hats_used"], 1)

                need("ixp", i, PER["ixp"])
                distances(0, 0)
                distances(0, 1)
                for k in range(NK):
                    for half in range(2):
                        gathers(k, half)
                        if k + 1 < NK:
                            distances(k + 1, half)
                need("actx", i, 2)
                turn_tiles(Bk, i, "ctxT", actx)
                token_product(Bk, i, "xout", cT, xwT_sb[:, 3, :, :], "ctxT")
                need("x2", i, 2)
                turn_tiles(Bk, i, "x2T", x2)
                token_product(Bk, i, "route", x2T, wr_sb, "x2T")
                need("ohs", i, 2)
                bank = take(Bk, pe, i, "pos")
                for c in range(NC):
                    o = bank[:, c * E:(c + 1) * E]
                    mm(o, mk[:, M_BEFORE, :], ohs[:, c, :], True, False)
                    if c == 1:
                        mm(o, mk[:, M_ONES, :], ohs[:, 0, :], False, False)
                    last = mm(o, mk[:, M_ONES, :], count[:, :], False, True)
                last.then_inc(Bk["filled"], 1)

            def stage_c(e, pair, j):
                pe.wait_ge(sem[f"w_in{j}"], (pair + 1) * PER["w_in0"])
                pe.wait_ge(sem[f"xe_in{j}"], (pair + 1) * PER["xe_in0"])
                for n in range(NT // 2):
                    bank = take(C, pe, e, f"xeT{n}")
                    for k in range(2):
                        for t in range(2):
                            last = turn(bank[:, k * T + t * P:k * T + (t + 1) * P],
                                        xe[j][:, 2 * n + t, k * P:(k + 1) * P])
                    last.then_inc(C["filled"], 1)
                for m in range(HID // P):
                    for part, (lo, hi) in (("a", (0, 512)), ("b", (512, CAP))):
                        bank = take(C, pe, e, f"h{m}{part}", *(C_USES[:NT // 2] if m == 0 else ()))
                        for k in range(2):
                            last = mm(bank[:, 0:hi - lo], w1_sb[j][:, k, m * P:(m + 1) * P],
                                      xeT[:, k, lo:hi], k == 0, k == 1)
                        last.then_inc(C["filled"], 1)
                for n in range(NT // 2):
                    bank = take(C, pe, e, f"y{n}", *(C_USES[NT // 2:-NT // 2] if n == 0 else ()))
                    for t in range(2):
                        at = (2 * n + t) * P
                        for m in range(HID // P):
                            last = mm(bank[:, t * D:(t + 1) * D], hT[:, m, at:at + P],
                                      w2_sb[j][:, m, :], m == 0, m == HID // P - 1)
                    last.then_inc(C["filled"], 1)

            pe.wait_ge(consts_in, CONSTS)
            pe.wait_ge(prepared, PREPARED)
            pe.wait_ge(zeroed, ZEROED)
            with pe.Fori(0, B) as i:
                stage_a(i)
                stage_b(i)
            for ring, banks in ((A, 4), (Bk, 2), (G, 2)):
                for b in range(banks):
                    pe.wait_ge(ring["read"][b], B * ring["per"][b])
            with pe.Fori(0, E // 2) as pair:
                for j in range(2):
                    stage_c(pair * 2 + j, pair, j)

        @block.scalar
        def _(act):
            def need(name, i, k):
                at_least(act, sem[name], i * PER[name] + k)

            def read_out(ring, i, use, dst, view, func=ACT.Copy, **kw):
                bank = wait_filled(ring, act, i, use)
                nc.scalar.activation(dst, view(bank), func, **kw).then_inc(was_read(ring, use), 1)

            def all_of(bank):
                return bank[:, :]

            def halves(bank):
                return bank[:, :].rearrange("p (c t) -> p c t", c=2)

            def per_head(bank):
                return bank[:, :].rearrange("p (h t) -> p h t", h=H)

            def stage_a(i):
                for use, t in (("k_proj", 1), ("v_proj", 2), ("q_proj", 0)):
                    read_out(A, i, use, pre[:, t, :, 3:], halves)
                for n, t in enumerate((1, 2, 0)):
                    need("conv", i, 8 * (n + 1))
                    act.activation(th[:, t, :, :], y[:, t, :, :], ACT.Tanh).then_inc(sem["tanh"], 1)
                wait_read(A, act, i, "sums")
                act.activation(bth[:, :, :], sums[:, 16:24].rearrange("p (c h) -> p c h", c=NC),
                               ACT.Tanh, scale=0.5).then_inc(sem["beta_th"], 1)
                read_out(A, i, "v_tok", vt[:, :, :], halves)
                bank = wait_filled(A, act, i, "k_chan")
                for m in range(2):
                    rows = slice(m * HD, (m + 1) * HD)
                    last = act.activation(kz[rows, :, m, :], halves(bank)[rows], ACT.Copy)
                last.then_inc(was_read(A, "k_chan"), 1)
                into = {"P2": lambda c: W[c][0], "P2T": lambda c: W[c][1], "P4": lambda c: W[c][2],
                        "T8": lambda c: Tn[c], "W": lambda c: W[c][0], "WT": lambda c: W[c][1],
                        "W2": lambda c: W[c][2], "T32": lambda c: Tn[c], "Y": lambda c: W[c][0],
                        "YT": lambda c: W[c][1], "Y2": lambda c: W[c][2]}
                for name in INVERSE:
                    for c in range(NC):
                        if name in into:
                            read_out(A, i, f"{name}{c}", into[name](c)[:, :, :], per_head)
                read_out(A, i, "u0", u_sb[0][:, :], lambda b: b[:, 0:D])
                read_out(A, i, "wT1", wTn[:, :, :],
                         lambda b: b[:, 0:2 * P].rearrange("p (c t) -> p c t", c=2), scale=-1.0)
                bank = wait_filled(A, act, i, "S0")
                for m in range(2):
                    rows = slice(m * HD, (m + 1) * HD)
                    last = act.activation(
                        S_sb[rows, m:H:2, :],
                        bank[rows, 0:D].rearrange("p (h d) -> p h d", h=H)[:, m:H:2, :], ACT.Copy)
                last.then_inc(was_read(A, "S0"), 1)
                read_out(A, i, "u1", u_sb[1][:, :], lambda b: b[:, 0:D])
                read_out(A, i, "mix", y1[:, :, :], halves)
                read_out(A, i, "ms", ms[:, :, :], halves)
                read_out(A, i, "statT", gst[:, :], lambda b: b[0:3 * H, 0:T], scale=1.0 / HD)
                for n in range(2):
                    bank = wait_filled(A, act, i, f"hid{n}")
                    for m in range(2):
                        last = nc.scalar.activation(hdn[:, 2 * n + m, :], bank[:, m * T:(m + 1) * T],
                                                    ACT.Gelu, bias=fb1_sb[:, 2 * n + m:2 * n + m + 1])
                    last.then_inc(was_read(A, f"hid{n}"), 1)
                need("fuse", i, 2)
                act.activation(lex[:, :, :], lg[:, :, :], ACT.Exp).then_inc(sem["wexp"], 1)
                read_out(A, i, "oT", oT[:, :, :], halves)

            def stage_b(i):
                read_out(Bk, i, "x1T", x1T[:, :, :], halves)
                bank = wait_filled(Bk, act, i, "Qc")
                for m in range(2):
                    last = nc.scalar.activation(QT[:, m, :], bank[:, m * T:(m + 1) * T],
                                                ACT.Identity, bias=bq_sb[:, m:m + 1])
                last.then_inc(was_read(Bk, "Qc"), 1)
                need("prod", i, 0)
                read_out(Bk, i, "Qt", Qs[:, :, :], halves, scale=0.5 * XD ** -0.5)

                def distances(k, half):
                    if half:
                        act.wait_ge(G["filled"], i * G["uses"] + k * NC)
                    else:
                        act.wait_ge(sem["hats_used"], i * PER["hats_used"] + k)
                    for j in range(XH // 4):
                        read_out(Bk, i, f"dist{k}{half}_{j}", nhat[half][:, 2 * j:2 * j + 2, :],
                                 lambda b: b[0:S2, :].rearrange("p (m t) -> p m t", m=2), ACT.Abs)

                distances(0, 0)
                distances(0, 1)
                need("actx", i, 0)
                for k in range(NK):
                    if k + 1 < NK:
                        distances(k + 1, 0)
                    for c in range(NC):
                        read_out(G, i, f"gather{k}_{c}",
                                 gs[:, c, k, :, :, :].rearrange("p h a d -> p (h a d)"), all_of)
                    if k + 1 < NK:
                        distances(k + 1, 1)
                need("scs", i, 2)
                act.activation(sce[:, :, :, :], scd[:, :, :, :], ACT.Exp).then_inc(sem["sexp"], 1)
                read_out(Bk, i, "ctxT", cT[:, :, :], halves)
                read_out(Bk, i, "x2T", x2T[:, :, :], halves)
                need("rmax", i, 2)
                act.activation(prx[:, :, :], prd[:, :, :], ACT.Exp).then_inc(sem["rexp"], 1)

            def stage_c(e, pair, j):
                act.wait_ge(sem[f"be_in{j}"], (pair + 1) * PER["be_in0"])
                for n in range(NT // 2):
                    read_out(C, e, f"xeT{n}", xeT[:, :, 2 * n * P:(2 * n + 2) * P], halves)
                for m in range(HID // P):
                    for part, (lo, hi) in (("a", (0, 512)), ("b", (512, CAP))):
                        read_out(C, e, f"h{m}{part}", hT[:, m, lo:hi],
                                 lambda b, n=hi - lo: b[:, 0:n], ACT.Relu,
                                 bias=b1_sb[j][:, m:m + 1])

            act.wait_ge(consts_in, CONSTS)
            act.wait_ge(zeroed, ZEROED)
            act.wait_ge(xe_zero, 48)
            with act.Fori(0, B) as i:
                stage_a(i)
                stage_b(i)
            with act.Fori(0, E // 2) as pair:
                for j in range(2):
                    stage_c(pair * 2 + j, pair, j)

        @block.vector
        def _(dve):
            given, batch = {}, [0]

            def begin(i, names):
                batch[0] = i
                for name in names:
                    given[name] = 0

            def end(names):
                for name in names:
                    assert given[name] == PER[name], (name, given[name], PER[name])

            def count_in(ins, name):
                given[name] += 1
                ins.then_inc(sem[name], 1)

            def own(name, k):
                dve.wait_ge(sem[name], batch[0] * PER[name] + k)

            def link(ins, name):
                count_in(ins, name)
                own(name, given[name])

            def need(name, i, k):
                at_least(dve, sem[name], i * PER[name] + k)

            def stage_a(i):
                names = ("conv", "silu", "beta", "t1", "taps", "stat", "fuse", "osum", "orms", "on",
                       "var1", "x1")
                begin(i, names)

                def short_conv(t):
                    for tap in range(4):
                        for hf in range(2):
                            w = convw_sb[:, t, hf, tap:tap + 1]
                            src = pre[:, t, hf, tap:tap + T]
                            if tap == 0:
                                ins = dve.tensor_scalar(y[:, t, hf, :], src, w, None, ALU.mult)
                            else:
                                own("conv", given["conv"] - 1)
                                ins = dve.scalar_tensor_tensor(y[:, t, hf, :], src, w,
                                                               y[:, t, hf, :], ALU.mult, ALU.add)
                            count_in(ins, "conv")

                def silu(n, t, dst):
                    need("tanh", i, n)
                    count_in(dve.scalar_tensor_tensor(dst, th[:, t, :, :], 1.0, y[:, t, :, :],
                                                    ALU.add, ALU.mult), "silu")

                done = [0]

                def taps(n):
                    for _ in range(n):
                        if done[0] == PER["taps"]:
                            return
                        tap, scale, hf = TAP_ORDER[done[0]]
                        w = msw_sb[scale][:, hf, tap:tap + 1]
                        at = PAD - (TAPS[scale] - 1) + tap
                        src = vpad[:, hf, at:at + T]
                        dst = acc[:, scale, hf, :]
                        if tap == 0:
                            ins = dve.tensor_scalar(dst, src, w, None, ALU.mult)
                        else:
                            own("taps", TAP_AT[tap - 1, scale, hf] + 1)
                            ins = dve.scalar_tensor_tensor(dst, src, w, dst, ALU.mult, ALU.add)
                        count_in(ins, "taps")
                        done[0] += 1

                wait_read(A, dve, i, "k_proj")
                short_conv(1)
                wait_read(A, dve, i, "v_proj")
                short_conv(2)
                silu(1, 1, qk[:, 1, :, :])
                wait_read(A, dve, i, "q_proj")
                short_conv(0)
                silu(2, 2, vpad[:, :, PAD:])
                silu(3, 0, qk[:, 0, :, :])
                own("silu", 2)
                taps(6)
                bank = wait_filled(A, dve, i, "sums")
                dve.tensor_copy(sums[:, :], bank[:, 0:24]).then_inc(was_read(A, "sums"), 1)
                need("beta_th", i, 1)
                count_in(dve.tensor_scalar(beta[:, :, :], bth[:, :, :], 0.5, 0.5, ALU.mult, ALU.add),
                       "beta")
                link(dve.tensor_scalar(nbeta[:, :, :], bth[:, :, :], -0.5, -0.5, ALU.mult, ALU.add),
                     "beta")
                need("rinv", i, 2)
                bank = wait_filled(A, dve, i, "k_tok")
                dve.tensor_tensor(split(kn[:, :, :]),
                                  bank[:, :].rearrange("p (c h d) -> p c h d", c=NC, h=H),
                                  heads(rinv[:, :, 1, :]), ALU.mult)\
                    .then_inc(was_read(A, "k_tok"), 1)

                def evict(use, dst, in1, op):
                    bank = wait_filled(A, dve, i, use)
                    dve.tensor_tensor(dst, bank[:, :].rearrange("p (h t) -> p h t", h=H), in1, op)\
                        .then_inc(was_read(A, use), 1)

                for name in INVERSE:
                    for c in range(NC):
                        use = f"{name}{c}"
                        if name == "gram":
                            evict(use, nbG[c][:, :, :],
                                  nbeta[:, c, :].unsqueeze(2).broadcast_to([P, H, P]), ALU.mult)
                        elif name == "gramT":
                            bank = wait_filled(A, dve, i, use)
                            for n, m in enumerate((M_IN128T, M_IN32T, M_DIAG8T)):
                                last = dve.tensor_tensor(
                                    XT[c][2 - n][:, :, :],
                                    bank[:, :].rearrange("p (h t) -> p h t", h=H), mask4(m), ALU.mult)
                            last.then_inc(was_read(A, use), 1)
                            wait_read(A, dve, i, use)
                            link(dve.tensor_tensor(Ta[c][:, :, :], XT[c][0][:, :, :], mask4(M_EYE),
                                                   ALU.add), "t1")
                        elif name in ("T2T", "U", "V"):
                            evict(use, Tb[c][:, :, :], Ta[c][:, :, :], ALU.add)
                            wait_read(A, dve, i, use)
                        elif name in ("T8T", "T32T", "TT"):
                            evict(use, Ta[c][:, :, :], Tb[c][:, :, :], ALU.add)
                            wait_read(A, dve, i, use)
                        elif name == "aT":
                            evict(use, aT[c][:, :, :], mask4(M_INCL), ALU.mult)
                        taps(3 if name not in ("gram", "gramT", "aT") else 1)
                for c in range(NC):
                    bank = wait_filled(A, dve, i, f"o{c}")
                    dve.tensor_tensor(delta[:, c, :].rearrange("p (h d) -> p h d", h=H),
                                      bank[:, 0:D].rearrange("p (h d) -> p h d", h=H),
                                      rinv[:, c, 0, :].unsqueeze(2).broadcast_to([P, H, HD]),
                                      ALU.mult).then_inc(was_read(A, f"o{c}"), 1)
                    if c == 0:
                        taps(PER["taps"])
                wait_read(A, dve, i, "o0", "o1", "v_tok", "ms")
                for n, src in enumerate((ms, delta, vt)):
                    count_in(dve.tensor_reduce(st[:, :, n * H:(n + 1) * H], split(src[:, :, :]),
                                             AX.X, ALU.add, apply_absolute_value=True), "stat")
                bank = wait_filled(A, dve, i, "logit")
                dve.tensor_tensor(lg[:, :, :].rearrange("p (c h) x -> p c (h x)", c=NC),
                                  bank[:, 0:6 * H].rearrange("p (c x) -> p c x", c=NC),
                                  fb2_sb[:, :].unsqueeze(1).broadcast_to([P, NC, 3 * H]),
                                  ALU.add).then_inc(was_read(A, "logit"), 1)
                wait_read(A, dve, i, "logit")
                link(dve.tensor_reduce(lmx[:, :], lg[:, :, :], AX.X, ALU.max), "fuse")

                def over3(ap):
                    return ap.unsqueeze(2).broadcast_to([P, NC * H, 3])

                link(dve.tensor_tensor(lg[:, :, :], lg[:, :, :], over3(lmx[:, :]), ALU.subtract),
                     "fuse")
                need("wexp", i, 1)
                link(dve.tensor_reduce(lmx[:, :], lex[:, :, :], AX.X, ALU.add), "fuse")
                link(dve.reciprocal(lmx[:, :], lmx[:, :]), "fuse")
                link(dve.tensor_tensor(wts[:, :, :], lex[:, :, :], over3(lmx[:, :]), ALU.mult),
                     "fuse")

                def weight(n):
                    return heads(wts[:, :, n].rearrange("p (c h) -> p c h", c=NC))

                dve.tensor_tensor(split(o1[:, :, :]), split(ms[:, :, :]), weight(0), ALU.mult)
                link(dve.tensor_tensor(split(o2[:, :, :]), split(delta[:, :, :]), weight(1),
                                       ALU.mult), "fuse")
                link(dve.tensor_tensor(o1[:, :, :], o1[:, :, :], o2[:, :, :], ALU.add), "osum")
                need("v3", i, 1)
                link(dve.tensor_tensor(o1[:, :, :], o1[:, :, :], o3[:, :, :], ALU.add), "osum")
                need("osq", i, 1)
                link(dve.tensor_reduce(rms[:, :].rearrange("p (c h) -> p c h", c=NC),
                                       split(o2[:, :, :]), AX.X, ALU.add), "orms")
                link(dve.tensor_scalar(rms[:, :], rms[:, :], 1.0 / HD, EPS, ALU.mult, ALU.add),
                     "orms")
                need("orr", i, 1)
                link(dve.tensor_tensor(split(o1[:, :, :]), split(o1[:, :, :]),
                                       heads(rrms[:, :].rearrange("p (c h) -> p c h", c=NC)),
                                       ALU.mult), "on")
                need("xt_in", i, 16)
                bank = wait_filled(A, dve, i, "attn")
                dve.tensor_tensor(xr[:, :, :], bank[:, :].rearrange("p (c d) -> p c d", c=NC),
                                  xt_sb[:, :, :], ALU.add).then_inc(was_read(A, "attn"), 1)
                wait_read(A, dve, i, "attn")
                layer_norm(i, xr, x1, bns, mv, ve, rstd, "var1", "rstd1", "x1")
                end(names)

            def layer_norm(i, src, dst, bn, m, v, r, var, rs, done):
                for c in range(NC):
                    count_in(dve.bn_stats(bn[:, c, :], src[:, c, :]), var)
                own(var, given[var])
                dve.nop(nofuse=True)
                for c in range(NC):
                    last = dve.bn_aggr(m[:, c, :], bn[:, c, :])
                link(last, var)
                link(dve.tensor_scalar(v[:, :], m[:, :, 1], EPS, None, ALU.add), var)
                need(rs, i, 1)
                for c in range(NC):
                    count_in(dve.tensor_scalar(dst[:, c, :], src[:, c, :], m[:, c, 0:1],
                                             r[:, c:c + 1], ALU.subtract, ALU.mult), done)

            def stage_b(i):
                names = ("length", "ixp", "nhat", "scr", "scs", "att", "av0", "actx", "var2", "x2",
                       "rmax", "top", "ohs", "count", "slots")
                begin(i, names)
                need("mask_in", i, 16)
                link(dve.tensor_copy(maskf[:, :], mask_sb[:, :]), "length")
                link(dve.tensor_reduce(msum[:, :], maskf[:, :], AX.X, ALU.add), "length")
                link(dve.tensor_scalar(Lb[:, :], msum[:, :], -1.0, float(S2 - 1), ALU.mult, ALU.add),
                     "length")
                link(dve.reciprocal(rL[:, :], Lb[:, :]), "length")
                for n, use in enumerate(("Kt", "Vt")):
                    bank = wait_filled(Bk, dve, i, use)
                    dve.scalar_tensor_tensor(tab[:, :, n, :],
                                             bank[0:S2, 0:D].rearrange("p (h d) -> p h d", h=XH),
                                             (-1.0, -0.5)[n],
                                             xb_sb[0:S2, n, :].rearrange("p (h d) -> p h d", h=XH),
                                             ALU.mult, ALU.subtract)\
                        .then_inc(was_read(Bk, use), 1)
                dve.wait_ge(G["filled"], i * G["uses"])
                for n, groups in ((0, (0, 1)), (1, (2,))):
                    bank = wait_filled(Bk, dve, i, f"off{n}")
                    for m, g in enumerate(groups):
                        last = dve.scalar_tensor_tensor(loc[:, g, :], bank[0:96, m * T:(m + 1) * T],
                                                        offc_sb[:, g:g + 1], posq[:, :],
                                                        ALU.add, ALU.add)
                    last.then_inc(was_read(Bk, f"off{n}"), 1)
                wait_read(Bk, dve, i, "off0", "off1")
                link(dve.tensor_scalar(tmp[:, :, :], loc[:, :, :], rL[:, :], None, ALU.mult), "ixp")
                link(dve.tensor_scalar(tmp[:, :, :], tmp[:, :, :], ROUND, None, ALU.add), "ixp")
                link(dve.tensor_scalar(tmp[:, :, :], tmp[:, :, :], ROUND, Lb[:, :], ALU.subtract,
                                       ALU.mult), "ixp")
                link(dve.tensor_tensor(loc[:, :, :], loc[:, :, :], tmp[:, :, :], ALU.subtract),
                     "ixp")
                link(dve.tensor_scalar(tmp[:, :, :], loc[:, :, :], Lb[:, :], 0.0, ALU.mult,
                                       ALU.is_lt), "ixp")
                link(dve.tensor_scalar(tmp[:, :, :], tmp[:, :, :], Lb[:, :], None, ALU.mult), "ixp")
                link(dve.tensor_tensor(loc[:, :, :], loc[:, :, :], tmp[:, :, :], ALU.add), "ixp")
                link(dve.tensor_scalar(loc[:, :, :], loc[:, :, :], S2 / (S2 - 1.0), -0.5, ALU.mult,
                                       ALU.add), "ixp")
                wait_filled_before(Bk, dve, i)
                link(dve.tensor_copy(ixp[0:96, :, :], loc[:, :, :]), "ixp")
                link(dve.tensor_tensor(loc[:, :, :], loc[:, :, :], ixp[0:96, :, :], ALU.subtract),
                     "ixp")
                count_in(dve.tensor_copy(ixp[32:64, :, :], loc[32:64, :, :]), "ixp")
                link(dve.tensor_copy(ixp[64:96, :, :], loc[64:96, :, :]), "ixp")
                link(dve.tensor_tensor(ixp[64:96, :, :], loc[64:96, :, :], ixp[64:96, :, :],
                                       ALU.subtract), "ixp")
                for k in range(NK):
                    for half in range(2):
                        wait_read(Bk, dve, i, f"dist{k}{half}_{XH // 4 - 1}", f"dist{k}{half}_{XH // 4 - 2}")
                        count_in(dve.tensor_scalar(nhat[half][:, :, :], nhat[half][:, :, :], 1.0,
                                                 0.0, ALU.subtract, ALU.min), "nhat")
                    if k:
                        score(i, k - 1)
                score(i, NK - 1)
                own("scr", NK)
                link(dve.tensor_reduce(scm[:, :, :], sc[:, :, :, :].rearrange("p c k h -> p c h k"),
                                       AX.X, ALU.max), "scs")

                def over_k(ap):
                    return ap.unsqueeze(2).broadcast_to([P, NC, NK, XH])

                link(dve.tensor_tensor(scd[:, :, :, :], sc[:, :, :, :], over_k(scm[:, :, :]),
                                       ALU.subtract), "scs")
                need("sexp", i, 1)
                link(dve.tensor_reduce(scm[:, :, :], sce[:, :, :, :].rearrange("p c k h -> p c h k"),
                                       AX.X, ALU.add), "att")
                link(dve.reciprocal(scm[:, :, :], scm[:, :, :]), "att")
                link(dve.tensor_tensor(sce[:, :, :, :], sce[:, :, :, :], over_k(scm[:, :, :]),
                                       ALU.mult), "att")
                link(dve.tensor_tensor(av[:, 0, :, :, :], gs[:, 0, :, :, 1, :],
                                       sce[:, 0, :, :].unsqueeze(3)
                                       .broadcast_to([P, NK, XH, XD]), ALU.mult), "av0")
                for c in range(NC):
                    if c == 1:
                        need("av", i, 1)
                    count_in(dve.tensor_reduce(actx[:, c, :].rearrange("p (h d) -> p h d", h=XH),
                                             av[:, c, :, :, :].rearrange("p k h d -> p h d k"),
                                             AX.X, ALU.add),
                           "actx")
                bank = wait_filled(Bk, dve, i, "xout")
                dve.tensor_tensor(xr2[:, :, :], bank[:, :].rearrange("p (c d) -> p c d", c=NC),
                                  x1[:, :, :], ALU.add).then_inc(was_read(Bk, "xout"), 1)
                wait_read(Bk, dve, i, "xout")
                link(dve.tensor_tensor(xr2[:, :, :], xr2[:, :, :],
                                       xb_sb[:, 2, :].unsqueeze(1).broadcast_to([P, NC, D]),
                                       ALU.add), "var2")
                need("x2_out", i, 0)
                need("scatter", i, 0)
                layer_norm(i, xr2, x2, bns2, mv2, ve2, rstd2, "var2", "rstd2", "x2")
                bank = wait_filled(Bk, dve, i, "route")
                logits = bank[:, 0:NC * E].rearrange("p (c e) -> p c e", c=NC)
                link(dve.tensor_reduce(prm[:, :], logits, AX.X, ALU.max), "rmax")

                def over_e(ap):
                    return ap.unsqueeze(2).broadcast_to([P, NC, E])

                dve.tensor_tensor(prd[:, :, :], logits, over_e(prm[:, :]), ALU.subtract)\
                    .then_inc(was_read(Bk, "route"), 1)
                count_in(dve.memset(junk[:, :], 0.0), "rmax")
                need("rexp", i, 1)
                link(dve.tensor_reduce(prm[:, :], prx[:, :, :], AX.X, ALU.add), "top")
                link(dve.reciprocal(prm[:, :], prm[:, :]), "top")
                link(dve.tensor_tensor(pr[:, :, :], prx[:, :, :], over_e(prm[:, :]), ALU.mult),
                     "top")
                dve.nop(nofuse=True)
                count_in(dve.max(top[:, 0, :], pr[:, 0, :]), "top")
                link(dve.max(top[:, 1, :], pr[:, 1, :]), "top")
                dve.nop(nofuse=True)
                count_in(dve.max_index(topi[:, 0, :], top[:, 0, :], pr[:, 0, :]), "top")
                link(dve.max_index(topi[:, 1, :], top[:, 1, :], pr[:, 1, :]), "top")
                link(dve.tensor_copy(topf[:, :, :], topi[:, :, :]), "top")
                link(dve.tensor_tensor(gsum[:, :], top[:, :, 0], top[:, :, 1], ALU.add), "top")
                link(dve.reciprocal(gsum[:, :], gsum[:, :]), "top")
                need("gate_out", i, 0)
                link(dve.tensor_tensor(gate[:, :, :], top[:, :, 0:TOPK],
                                       gsum[:, :].unsqueeze(2).broadcast_to([P, NC, TOPK]),
                                       ALU.mult), "top")
                ids = eids[:, :].unsqueeze(1).broadcast_to([P, TOPK, E])
                for c in range(NC):
                    dve.tensor_tensor(oh[:, c, :, :], ids, topf[:, c, 0:TOPK].unsqueeze(2)
                                      .broadcast_to([P, TOPK, E]), ALU.is_equal)
                link(dve.memset(junk[:, :], 0.0), "ohs")
                link(dve.tensor_tensor(ohs[:, :, :], oh[:, :, 0, :], oh[:, :, 1, :], ALU.add), "ohs")
                bank = wait_filled(Bk, dve, i, "pos")
                dve.tensor_copy(pos[:, :, :], bank[:, 0:NC * E].rearrange("p (c e) -> p c e", c=NC))\
                    .then_inc(was_read(Bk, "pos"), 1)
                for c in range(NC):
                    link(dve.tensor_tensor(count[:, :], count[:, :], ohs[:, c, :], ALU.add), "count")
                wait_read(Bk, dve, i, "pos")
                for c in range(NC):
                    count_in(dve.tensor_tensor(psel[:, c, :, :], oh[:, c, :, :],
                                             pos[:, c, :].unsqueeze(1).broadcast_to([P, TOPK, E]),
                                             ALU.mult), "slots")
                    link(dve.tensor_tensor(esel[:, c, :, :], oh[:, c, :, :], ids, ALU.mult), "slots")
                count_in(dve.tensor_reduce(pk[:, :, :], psel[:, :, :, :], AX.X, ALU.add), "slots")
                link(dve.tensor_reduce(ek[:, :, :], esel[:, :, :, :], AX.X, ALU.add), "slots")
                link(dve.tensor_scalar(drop[:, :, :], pk[:, :, :], float(CAP), None, ALU.is_ge),
                     "slots")
                link(dve.tensor_scalar(pk[:, :, :], pk[:, :, :], float(CAP - 1), None, ALU.min),
                     "slots")
                link(dve.scalar_tensor_tensor(gslot[:, :, :], ek[:, :, :], float(CAP), pk[:, :, :],
                                              ALU.mult, ALU.add), "slots")
                link(dve.scalar_tensor_tensor(sslot[:, :, :], drop[:, :, :], float(E * CAP),
                                              gslot[:, :, :], ALU.mult, ALU.add), "slots")
                need("slot_out", i, 0)
                dve.tensor_scalar(ek[:, :, :], drop[:, :, :], -1.0, 1.0, ALU.mult, ALU.add)
                dve.tensor_copy(gslot_i[:, :], gslot[:, :, :].rearrange("p c k -> p (c k)"))
                link(dve.tensor_copy(sslot_i[:, :], sslot[:, :, :].rearrange("p c k -> p (c k)")),
                     "slots")
                link(dve.tensor_tensor(gate[:, :, :], gate[:, :, :], ek[:, :, :], ALU.mult), "slots")
                end(names)

            def score(i, k):
                need("prod", i, k + 1)
                count_in(dve.tensor_reduce(sc[:, :, k, :], prod[k % 2][:, :, :, :], AX.X, ALU.add),
                       "scr")

            def stage_c(e, pair, j):
                dve.wait_ge(sem[f"be_in{j}"], (pair + 1) * PER["be_in0"])
                dve.wait_ge(sem["y_out"], pair * 2 * PER["y_out"])
                for n in range(NT // 2):
                    bank = wait_filled(C, dve, e, f"y{n}")
                    dve.tensor_tensor(ye[j][:, 2 * n:2 * n + 2, :],
                                      bank[:, :].rearrange("p (t d) -> p t d", t=2),
                                      b2_sb[j][:, :].unsqueeze(1).broadcast_to([P, 2, D]),
                                      ALU.add).then_inc(was_read(C, f"y{n}"), 1)

            def stage_d(i, pair, j):
                names = ("mix", "fvar", "fo")
                begin(i, names)
                need(f"f_in{j}", pair, PER["f_in0"])
                need(f"row_in{j}", pair, PER["row_in0"])
                for c in range(NC):
                    count_in(dve.scalar_tensor_tensor(fy[j][:, c, :], frow[j][:, c, 0, :],
                                                    fgate[j][:, 2 * c:2 * c + 1], fx[j][:, c, :],
                                                    ALU.mult, ALU.add), "mix")
                for c in range(NC):
                    own("mix", c + 1)
                    count_in(dve.scalar_tensor_tensor(fy[j][:, c, :], frow[j][:, c, 1, :],
                                                    fgate[j][:, 2 * c + 1:2 * c + 2],
                                                    fy[j][:, c, :], ALU.mult, ALU.add), "mix")
                own("mix", 4)
                dve.wait_ge(sem["out_done"], pair * 2 * PER["out_done"])
                layer_norm(i, fy[j], fo[j], fbn[j], fmv[j], fve[j], frs[j], "fvar", "frs", "fo")
                end(names)

            dve.wait_ge(consts_in, CONSTS)
            dve.wait_ge(zeroed, ZEROED)
            dve.tensor_scalar(convw_sb[:, :, :, :], convw_sb[:, :, :, :], 0.5, None, ALU.mult)\
                .then_inc(prepared, 1)
            dve.tensor_scalar(wo_sb[:, :, :], wo_sb[:, :, :], onorm_sb[:, :], None, ALU.mult)\
                .then_inc(prepared, 1)
            dve.tensor_scalar(xb_sb[:, 1, :], xb_sb[:, 1, :], 0.5, None, ALU.mult)\
                .then_inc(prepared, 1)
            dve.tensor_tensor(offc_sb[:, :], offb_sb[:, :], refp_sb[:, :], ALU.add)\
                .then_inc(prepared, 1)
            dve.wait_ge(prepared, PREPARED)
            with dve.Fori(0, B) as i:
                stage_a(i)
                stage_b(i)
            with dve.Fori(0, E // 2) as pair:
                for j in range(2):
                    stage_c(pair * 2 + j, pair, j)
            with dve.Fori(0, B // 2) as pair:
                for j in range(2):
                    stage_d(pair * 2 + j, pair, j)

        @block.gpsimd
        def _(pool):
            def need(name, i, k):
                at_least(pool, sem[name], i * PER[name] + k)

            def rsqrt(dst, src, shape, name):
                n = 1
                for d in shape:
                    n *= d
                h = half_m[:, 0:n]
                if len(shape) == 2:
                    h = h.rearrange("p (a b) -> p a b", a=shape[0])
                pool.tensor_tensor(dst, src, h, ALU.pow).then_inc(sem[name], 1)

            def stage_a(i):
                for n, t in ((1, 1), (3, 0)):
                    need("silu", i, n)
                    pool.tensor_tensor(sq[:, t, :, :], qk[:, t, :, :], qk[:, t, :, :], ALU.mult)\
                        .then_inc(sem["sq"], 1)
                wait_read(A, pool, i, "sums")
                pool.nop(nofuse=True)
                pool.tensor_scalar(sums[:, 0:16], sums[:, 0:16], 1e-6, None, ALU.add)\
                    .then_inc(sem["rinv"], 1)
                need("rinv", i, 1)
                rsqrt(rinv[:, :, :, :].rearrange("p c t h -> p (c t h)"), sums[:, 0:16], [16],
                      "rinv")
                need("beta", i, 2)
                wait_read(A, pool, i, "v_tok")
                pool.tensor_tensor(split(vb[:, :, :]), split(vt[:, :, :]), heads(beta[:, :, :]),
                                   ALU.mult).then_inc(sem["vb"], 1)
                wait_read(A, pool, i, "k_tok")
                pool.tensor_tensor(kb[:, :].rearrange("p (h d) -> p h d", h=H),
                                   kn[:, 1, :].rearrange("p (h d) -> p h d", h=H),
                                   beta[:, 1, :].unsqueeze(2).broadcast_to([P, H, HD]),
                                   ALU.mult).then_inc(sem["kb"], 1)
                for c in range(NC):
                    wait_read(A, pool, i, f"gram{c}")
                    pool.tensor_tensor(X8[c][:, :, :], nbG[c][:, :, :], mask4(M_DIAG8), ALU.mult)\
                        .then_inc(sem["x8"], 1)
                need("fuse", i, 5)
                pool.tensor_tensor(split(o3[:, :, :]), split(vt[:, :, :]),
                                   heads(wts[:, :, 2].rearrange("p (c h) -> p c h", c=NC)),
                                   ALU.mult).then_inc(sem["v3"], 1)
                need("osum", i, 2)
                pool.tensor_tensor(o2[:, :, :], o1[:, :, :], o1[:, :, :], ALU.mult)\
                    .then_inc(sem["osq"], 1)
                need("orms", i, 2)
                rsqrt(rrms[:, :], rms[:, :], [8], "orr")
                need("var1", i, 4)
                rsqrt(rstd[:, :], ve[:, :], [2], "rstd1")

            def stage_b(i):
                wait_read(Bk, pool, i, "Qt")
                for k in range(NK):
                    for c in range(NC):
                        wait_read(G, pool, i, f"gather{k}_{c}")
                    need("scr", i, max(0, k - 1))
                    pool.tensor_tensor(prod[k % 2][:, :, :, :], gs[:, :, k, :, 0, :],
                                       split(Qs[:, :, :], XH), ALU.mult).then_inc(sem["prod"], 1)
                need("att", i, 3)
                pool.tensor_tensor(av[:, 1, :, :, :], gs[:, 1, :, :, 1, :],
                                   sce[:, 1, :, :].unsqueeze(3).broadcast_to([P, NK, XH, XD]),
                                   ALU.mult).then_inc(sem["av"], 1)
                need("var2", i, 5)
                rsqrt(rstd2[:, :], ve2[:, :], [2], "rstd2")
                need("slots", i, PER["slots"])
                pool.nop(nofuse=True)
                for c in range(NC):
                    for k in range(TOPK):
                        n = c * TOPK + k
                        pool.indirect_dma_start(
                            out=xe_dram, out_offset=bass.IndirectOffsetOnAxis(
                                ap=sslot_i[:, n:n + 1], axis=0),
                            in_=x2[:, c, :], in_offset=None, bounds_check=E * CAP - 1,
                            oob_is_err=False).then_inc(sem["scatter"], 16)

            def stage_d(pair, j):
                need(f"f_in{j}", pair, PER["f_in0"])
                pool.nop(nofuse=True)
                for c in range(NC):
                    for k in range(TOPK):
                        n = c * TOPK + k
                        pool.indirect_dma_start(
                            out=frow[j][:, c, k, :], out_offset=None, in_=ye_dram,
                            in_offset=bass.IndirectOffsetOnAxis(ap=fslot[j][:, n:n + 1], axis=0))\
                            .then_inc(sem[f"row_in{j}"], 16)

            def norm_d(i, j):
                need("fvar", i, 4)
                rsqrt(frs[j][:, :], fve[j][:, :], [2], "frs")

            for n, (ap, value) in enumerate(
                    ((pre[:, :, :, 0:3], 0.0), (vpad[:, :, 0:PAD], 0.0), (zero, 0.0),
                     (kz[:, :, :, :], 0.0), (S_sb[:, :, :], 0.0),
                     (half_m[:, :], -0.5), (count[:, :], 0.0), (ixp[96:97, :, :], 1.0))):
                pool.memset(ap, value).then_inc(zeroed, 1)
                pool.wait_ge(zeroed, n + 1)
            for n in range(3):
                pool.dma_start(xe_dram[bass.ts(n, E * CAP // 3), :]
                               .rearrange("(p t) d -> p (t d)", p=P), zero).then_inc(xe_zero, 16)
            pool.wait_ge(xe_zero, 48)
            pool.wait_ge(consts_in, CONSTS)
            with pool.Fori(0, B) as i:
                stage_a(i)
                stage_b(i)
            pool.wait_ge(sem["y_out"], E * PER["y_out"])
            stage_d(0, 0)
            with pool.Fori(0, B // 2 - 1) as pair:
                i = pair * 2
                stage_d(pair, 1)
                norm_d(i, 0)
                need("fo", i, PER["fo"])
                stage_d(pair + 1, 0)
                norm_d(i + 1, 1)
                need("fo", i + 1, PER["fo"])
            stage_d(B // 2 - 1, 1)
            norm_d(B - 2, 0)
            norm_d(B - 1, 1)


def kernel(**inputs):
    import numpy as np
    import concourse.bacc as bacc
    from concourse.bass_utils import run_bass_kernel_spmd

    a = {k: np.asarray(v) for k, v in inputs.items()}

    def rows(w, k):
        return w.reshape(k, P, -1).transpose(1, 0, 2)

    x = a["x"]
    r, c = np.arange(P)[:, None], np.arange(P)[None, :]
    below = r > c
    diag8 = below & (r // 8 == c // 8)
    in32 = below & (r // 32 == c // 32) & ~diag8
    in128 = below & ~(r // 32 == c // 32)
    table = [diag8, in32, in128, diag8.T, in32.T, in128.T, r <= c, r == c, r < c, r + c >= 0]
    masks = np.stack(table, 1).astype(np.float32)
    kmw = a["L0_attn_kernel_mix_w"]
    kmix = np.zeros((6, P, P), np.float32)
    for row in range(0, 3 * D, HD):
        head, at = divmod(row, 3 * HD)
        j, p = divmod(row, P)
        kmix[j, p:p + HD, (head % 2) * HD:(head % 2 + 1) * HD] = kmw[at:at + HD]
    woff = a["L0_xattn_Woff"].reshape(XH, NK, D).transpose(1, 0, 2).reshape(NK * XH, D)
    boff = a["L0_xattn_boff"].reshape(XH, NK).T.reshape(NK * XH)
    wo3 = np.zeros((3, 96, D), np.float32)
    bo3 = np.zeros((3, 96), np.float32)
    ref3 = np.zeros((3, 96), np.float32)
    for g in range(3):
        for part in range(3):
            n = min(32, NK * XH - 32 * g)
            wo3[g, part * 32:part * 32 + n] = woff[32 * g:32 * g + n]
            bo3[g, part * 32:part * 32 + n] = boff[32 * g:32 * g + n]
            ref3[g, part * 32:part * 32 + n] = (np.arange(32 * g, 32 * g + n) // XH) - (NK + 1) // 2
    import ml_dtypes
    selector = np.zeros((97, 32, S2), ml_dtypes.bfloat16)
    for p in range(96):
        selector[p, p % 32, :] = 1
    selector[96, :, :] = -np.arange(S2)
    headsel = (r[:, 0:1] // HD == np.arange(2)[None, :]).astype(np.float32)
    arrays = dict(
        x_tok=x.reshape(B, NC, P, D).transpose(0, 2, 1, 3),
        xT=x.transpose(0, 2, 1).reshape(B, 2, P, T).transpose(0, 2, 1, 3),
        ctxT=a["ctx_1024"].transpose(0, 2, 1).reshape(B, 2, P, S2).transpose(0, 2, 1, 3),
        mask=a["mask_BxS2_if0"],
        wqkv=np.stack([rows(a[f"L0_attn_W{n}"], 2) for n in "qkv"], 1),
        wb=rows(a["L0_attn_Wb"], 2),
        convw=np.stack([rows(a[f"L0_attn_conv_{n}_w"], 2) for n in "qkv"], 1),
        msw3=rows(a["L0_attn_ms_w3"], 2), msw15=rows(a["L0_attn_ms_w15"], 2),
        msw31=rows(a["L0_attn_ms_w31"], 2),
        kmix=kmix.transpose(1, 0, 2), cmix=rows(a["L0_attn_channel_mixer_w"], 2),
        fw1=rows(a["L0_attn_fusion_w1"][:D], 2), fw1s=a["L0_attn_fusion_w1"][D:],
        fb1=a["L0_attn_fusion_b1"].reshape(4, P).T, fw2=rows(a["L0_attn_fusion_w2"], 4),
        fb2=a["L0_attn_fusion_b2"], onorm=a["L0_attn_o_norm_w"].reshape(HD, 1),
        wo=rows(a["L0_attn_Wo"], 2),
        xwT=np.stack([rows(a[f"L0_xattn_W{n}"].T, 2) for n in "kvqo"], 1),
        xbias=np.stack([a[f"L0_xattn_b{n}"] for n in "kvo"]), xbq=a["L0_xattn_bq"].reshape(2, P).T,
        woff=np.stack([rows(np.ascontiguousarray(wo3[g].T), 2) for g in range(3)], 2),
        boff=bo3.T, ref_pos=ref3.T, wr=rows(a["L0_ffn_w_router"], 2),
        w1=a["L0_ffn_w1"].reshape(E, 2, P, HID).transpose(0, 2, 1, 3),
        b1=a["L0_ffn_b1"].reshape(E, HID // P, P).transpose(0, 2, 1),
        w2=a["L0_ffn_w2"].reshape(E, HID // P, P, D).transpose(0, 2, 1, 3),
        b2=a["L0_ffn_b2"], masks=masks, headsel=headsel, selector=selector,
        positions=np.arange(T, dtype=np.float32), expert_ids=np.arange(E, dtype=np.float32),
    )
    nc = bacc.Bacc("TRN2", target_bir_lowering=False, num_devices=1)
    args = {}
    arrays = {f"in_{n}": np.ascontiguousarray(v) for n, v in arrays.items()}
    for name, v in arrays.items():
        args[name[3:]] = nc.dram_tensor(name, v.shape, mybir.dt.from_np(v.dtype),
                                    kind="ExternalInput").ap()
    args["msw"] = [args.pop(f"msw{t}") for t in TAPS]
    out = nc.dram_tensor("out", (B, P, NC, D), mybir.dt.float32, kind="ExternalOutput").ap()
    decoder_layer(nc, out=out, **args)
    r = run_bass_kernel_spmd(nc, [arrays], core_ids=[0])
    got = r.results[0]["out"]
    return np.ascontiguousarray(got.transpose(0, 2, 1, 3).reshape(B, T, D))
```

```python
from contextlib import ExitStack

import concourse.bass as bass
from concourse import mybir

P = 128
B, T, D = 8, 256, 256
NC = T // P
H, HD = 4, 64
S2 = 120
XH, XD, NK = 16, 16, 5
E, TOPK, HID = 8, 2, 1024
CAP = int(1.5 * 4 * 512 * TOPK / E)
NT = CAP // P
EPS = 1e-5
TAPS = (3, 15, 31)
PAD = max(TAPS) - 1

(M_DIAG8, M_IN32, M_IN128, M_DIAG8T, M_IN32T, M_IN128T, M_INCL, M_EYE, M_BEFORE, M_ONES) = range(10)
NMASK = 10
ROUND = 1.5 * 2.0 ** 23
ZEROED, PREPARED = 8, 4
TAP_ORDER = [(tap, s, hf) for tap in range(max(TAPS)) for s in range(3) for hf in range(2)
             if tap < TAPS[s]]
TAP_AT = {tap: n for n, tap in enumerate(TAP_ORDER)}

INVERSE = ["gram", "gramT", "P2", "P2T", "P4", "T2T", "T8T", "T8", "W", "WT", "W2", "U", "T32T",
           "T32", "Y", "YT", "Y2", "V", "TT", "aT"]
A_USES = (["k_proj", "v_proj", "q_proj", "sums", "k_tok", "v_tok", "k_chan"]
          + [f"{s}{c}" for s in INVERSE for c in range(NC)]
          + ["u0", "wT1", "S0", "o0", "u1", "o1"]
          + ["mix", "ms", "statT", "hid0", "hid1", "logit", "oT", "attn"])
B_USES = (["Kt", "Vt", "x1T", "Qc", "off0", "off1", "Qt"]
          + [f"dist{k}{half}_{j}" for k in range(NK) for half in range(2) for j in range(XH // 4)]
          + ["ctxT", "xout", "x2T", "route", "pos"])
G_USES = [f"gather{k}_{c}" for k in range(NK) for c in range(NC)]
C_USES = ([f"xeT{j}" for j in range(NT // 2)] + [f"h{m}{a}" for m in range(HID // P) for a in "ab"]
          + [f"y{j}" for j in range(NT // 2)])

PER = dict(
    xT_in=16, xt_in=16, conv=24, tanh=3, silu=3, sq=2, rinv=2, beta_th=1, beta=2, vb=1, kb=1,
    x8=2, t1=2, taps=98, stat=3, fuse=6, wexp=1, v3=1, osum=2, osq=1, orms=2, orr=1, on=1,
    var1=4, rstd1=1, x1=2,
    ctx_in=16, mask_in=16, length=4, ixp=13, nhat=10, hats_used=5, prod=5, scr=5, scs=2, sexp=1, att=3, av=1,
    av0=1, actx=2, var2=5, rstd2=1, x2=2, rmax=1, rexp=1, top=11, ohs=2, count=2, slots=12,
    x2_out=16, slot_out=16, gate_out=16, scatter=64,
    w_in0=32, w_in1=32, be_in0=32, be_in1=32, xe_in0=16, xe_in1=16, y_out=16,
    f_in0=48, f_in1=48, row_in0=64, row_in1=64, mix=4, fvar=4, frs=1, fo=2, out_done=16,
)


SEGMENTS = {"A": len(INVERSE) + 14, "B": 22}


def run(*stages):
    ratio = max(SEGMENTS[name] for name, _ in stages)
    for n in range(ratio):
        for name, stage in stages:
            for _ in range((n + 1) * SEGMENTS[name] // ratio - n * SEGMENTS[name] // ratio):
                next(stage)
    for name, stage in stages:
        assert next(stage, "over") == "over", name


def at_least(eng, semaphore, value):
    if not (isinstance(value, int) and value <= 0):
        eng.wait_ge(semaphore, value)


def total(name, i, k):
    return i * PER[name] + k


def bank_ring(ctx, nc, name, uses, banks):
    return dict(
        use={u: n for n, u in enumerate(uses)}, uses=len(uses), banks=banks,
        filled=ctx.enter_context(nc.semaphore(f"{name}_filled")),
        read=[ctx.enter_context(nc.semaphore(f"{name}_read{b}")) for b in range(len(banks))],
        per=[len(range(b, len(uses), len(banks))) for b in range(len(banks))])


def place(ring, use):
    return ring["use"][use] % len(ring["banks"]), ring["use"][use] // len(ring["banks"])


def bank_of(ring, use):
    return ring["banks"][place(ring, use)[0]]


def was_read(ring, use):
    return ring["read"][place(ring, use)[0]]


def wait_read(ring, eng, i, *uses):
    last = {}
    for b, n in [place(ring, u) for u in uses]:
        last[b] = max(n, last[b]) if b in last else n
    for b in last:
        eng.wait_ge(ring["read"][b], i * ring["per"][b] + last[b] + 1)


def take(ring, pe, i, use, *after):
    b, n = place(ring, use)
    at_least(pe, ring["read"][b], i * ring["per"][b] + n)
    wait_read(ring, pe, i, *[u for u in after if place(ring, u)[0] != b])
    return ring["banks"][b]


def wait_filled(ring, eng, i, use):
    eng.wait_ge(ring["filled"], i * ring["uses"] + ring["use"][use] + 1)
    return bank_of(ring, use)


def wait_filled_before(ring, eng, i):
    at_least(eng, ring["filled"], i * ring["uses"])


def decoder_layer(nc, x_tok, xT, ctxT, mask, wqkv, wb, convw, msw, kmix, cmix, fw1, fw1s, fb1, fw2,
                  fb2, onorm, wo, xwT, xbias, xbq, woff, boff, ref_pos, wr, w1, b1, w2, b2, masks,
                  headsel, selector, positions, expert_ids, out):
    f32, bf16, u32 = mybir.dt.float32, mybir.dt.bfloat16, mybir.dt.uint32
    i32 = mybir.dt.int32
    ALU, ACT, AX = mybir.AluOpType, mybir.ActivationFunctionType, mybir.AxisListType

    x2_dram = nc.dram_tensor("x2_rows", (B, P, NC, D), f32).ap()
    slot_dram = nc.dram_tensor("slots", (B, P, NC * TOPK), u32).ap()
    gate_dram = nc.dram_tensor("gates", (B, P, NC * TOPK), f32).ap()
    xe_dram = nc.dram_tensor("expert_in", (E * CAP, D), f32).ap()
    ye_dram = nc.dram_tensor("expert_out", (E * CAP, D), f32).ap()

    ctx = ExitStack()
    with ctx:
        phase1 = ExitStack()

        def keep(name, shape, dt=f32):
            return ctx.enter_context(nc.sbuf_tensor(name, shape, dt))

        def sb(name, shape, dt=f32):
            return phase1.enter_context(nc.sbuf_tensor(name, shape, dt))

        sem = {n: ctx.enter_context(nc.semaphore(n)) for n in PER}
        consts_in = ctx.enter_context(nc.semaphore("consts_in"))
        zeroed = ctx.enter_context(nc.semaphore("zeroed"))
        xe_zero = ctx.enter_context(nc.semaphore("xe_zero"))
        prepared = ctx.enter_context(nc.semaphore("prepared"))

        psum = [ctx.enter_context(nc.psum_tensor(f"bank{b}", [P, 512], f32)) for b in range(8)]
        A = bank_ring(ctx, nc, "A", A_USES, psum[0:4])
        Bk = bank_ring(ctx, nc, "B", B_USES, psum[4:6])
        G = bank_ring(ctx, nc, "G", G_USES, psum[6:8])
        C = bank_ring(ctx, nc, "C", C_USES, psum)

        mk = keep("masks", [P, NMASK, P])
        half_m = keep("minus_half", [P, 16])
        wqkv_sb = sb("wqkv", [P, 3, 2, D])
        wb_sb = sb("wb", [P, 2, H])
        convw_sb = sb("convw", [P, 3, 2, 4])
        msw_sb = [sb(f"msw{s}", [P, 2, TAPS[s]]) for s in range(3)]
        kmix_sb = sb("kmix", [P, 6, P])
        cmix_sb = sb("cmix", [P, 2, D])
        fw1_sb = sb("fw1", [P, 2, 2 * D])
        fw1s_sb = sb("fw1s", [3 * H, 2 * D])
        fb1_sb = sb("fb1", [P, 4])
        fw2_sb = sb("fw2", [P, 4, 3 * H])
        fb2_sb = sb("fb2", [P, 3 * H])
        onorm_sb = sb("onorm", [P, 1])
        wo_sb = sb("wo", [P, 2, D])
        xwT_sb = sb("xwT", [P, 4, 2, D])
        bq_sb = sb("bq", [P, 2])
        xb_sb = sb("xb", [P, 3, D])
        woff_sb = sb("woff", [P, 2, 3, 96])
        offb_sb = sb("offb", [96, 3])
        refp_sb = sb("refp", [96, 3])
        offc_sb = sb("offc", [96, 3])
        wr_sb = sb("wr", [P, 2, E])
        headsel_sb = sb("headsel", [P, 2])
        sel_sb = sb("sel", [97, 32, S2], bf16)
        posq = sb("posq", [96, T])
        eids = sb("eids", [P, E])

        xT_sb = sb("xT", [P, 2, T])
        xt_sb = sb("x_tok", [P, NC, D])
        pre = sb("pre", [P, 3, 2, 3 + T])
        y = sb("y", [P, 3, 2, T])
        th = sb("th", [P, 3, 2, T])
        qk = sb("qk", [P, 2, 2, T])
        vpad = sb("vpad", [P, 2, PAD + T])
        sq = th
        sums = sb("sums", [P, 24])
        rinv = sb("rinv", [P, NC, 2, H])
        bth = sb("bth", [P, NC, H])
        beta = sb("beta", [P, NC, H])
        nbeta = sb("nbeta", [P, NC, H])
        kn = sb("kn", [P, NC, D])
        vt = sb("vt", [P, NC, D])
        vb = sb("vb", [P, NC, D])
        kb = sb("kb", [P, D])
        kz = sb("kz", [P, 2, 2, T])
        XT = [[sb(f"XT{s}_{c}", [P, H, P]) for s in range(3)] for c in range(NC)]
        W = [[sb(f"W{s}_{c}", [P, H, P]) for s in range(3)] for c in range(NC)]
        Ta = [sb(f"Ta{c}", [P, H, P]) for c in range(NC)]
        Tb = [sb(f"Tb{c}", [P, H, P]) for c in range(NC)]
        Tn = [sb(f"Tn{c}", [P, H, P]) for c in range(NC)]
        nbG = [W[c][2] for c in range(NC)]
        X8 = Tb
        aT = Tn
        u_sb = [sb(f"u{c}", [P, D]) for c in range(NC)]
        wTn = sb("wTn", [P, 2, P])
        S_sb = sb("S", [P, H, HD])
        delta = sb("delta", [P, NC, D])
        acc = sb("acc", [P, 3, 2, T])
        y1 = y[:, 0, :, :]
        ms = sb("ms", [P, NC, D])
        st = sb("st", [P, NC, 3 * H])
        gst = sb("gst", [3 * H, T])
        hdn = y[:, 1:3, :, :].rearrange("p a b t -> p (a b) t")
        lg = sb("lg", [P, NC * H, 3])
        lmx = sb("lmx", [P, NC * H])
        lex = sb("lex", [P, NC * H, 3])
        wts = sb("wts", [P, NC * H, 3])
        o1 = sb("o1", [P, NC, D])
        o2 = sb("o2", [P, NC, D])
        o3 = sb("o3", [P, NC, D])
        rms = sb("rms", [P, NC * H])
        rrms = sb("rrms", [P, NC * H])
        oT = qk[:, 0, :, :]
        bns = sb("bns", [P, NC, 6])
        mv = sb("mv", [P, NC, 2])
        ve = sb("ve", [P, NC])
        rstd = sb("rstd", [P, NC])
        xr = o3
        x1 = sb("x1", [P, NC, D])

        ctxT_sb = sb("ctxT", [P, 2, S2])
        mask_sb = sb("mask", [96, S2], i32)
        maskf = sb("maskf", [96, S2])
        msum = sb("msum", [96, 1])
        Lb = sb("L", [96, 1])
        rL = sb("rL", [96, 1])
        x1T = sb("x1T", [P, 2, T])
        QT = sb("QT", [P, 2, T])
        Qs = sb("Qs", [P, NC, D])
        ixp = sb("ixp", [97, 3, T], bf16)
        tab = sb("tab", [S2, XH, 2, XD])
        nhat = [sb(f"nhat{j}", [S2, XH // 2, T]) for j in range(2)]
        loc = nhat[1][0:96, 0:3, :]
        tmp = nhat[1][0:96, 3:6, :]
        gs = sb("gs", [P, NC, NK, XH, 2, XD])
        prod = [sb(f"prod{j}", [P, NC, XH, XD]) for j in range(2)]
        sc = sb("sc", [P, NC, NK, XH])
        scm = sb("scm", [P, NC, XH])
        scd = sb("scd", [P, NC, NK, XH])
        sce = sb("sce", [P, NC, NK, XH])
        av = gs[:, :, :, :, 1, :]
        actx = sb("actx", [P, NC, D])
        cT = x1T
        bns2 = sb("bns2", [P, NC, 6])
        mv2 = sb("mv2", [P, NC, 2])
        ve2 = sb("ve2", [P, NC])
        rstd2 = sb("rstd2", [P, NC])
        xr2 = actx
        x2 = sb("x2", [P, NC, D])
        x2T = QT
        pr = sb("pr", [P, NC, E])
        prm = sb("prm", [P, NC])
        prd = sb("prd", [P, NC, E])
        prx = sb("prx", [P, NC, E])
        top = sb("top", [P, NC, E])
        topi = sb("topi", [P, NC, E], u32)
        topf = sb("topf", [P, NC, E])
        gsum = sb("gsum", [P, NC])
        oh = sb("oh", [P, NC, TOPK, E])
        ohs = sb("ohs", [P, NC, E])
        count = sb("count", [P, E])
        pos = sb("pos", [P, NC, E])
        psel = sb("psel", [P, NC, TOPK, E])
        esel = sb("esel", [P, NC, TOPK, E])
        junk = sb("junk", [P, 2])
        pk = sb("pk", [P, NC, TOPK])
        ek = sb("ek", [P, NC, TOPK])
        drop = sb("drop", [P, NC, TOPK])
        gate = sb("gate", [P, NC, TOPK])
        gslot = sb("gslot", [P, NC, TOPK])
        sslot = sb("sslot", [P, NC, TOPK])
        gslot_i = sb("gslot_i", [P, NC * TOPK], u32)
        sslot_i = sb("sslot_i", [P, NC * TOPK], u32)
        zero = gs[:, :, :, :, :, :].rearrange("p a b c d e -> p (a b c d e)")[:, 0:4096]

        phase1.close()
        w1_sb = [keep(f"w1_{j}", [P, 2, HID]) for j in range(2)]
        w2_sb = [keep(f"w2_{j}", [P, HID // P, D]) for j in range(2)]
        xe = [ctx.enter_context(nc.sbuf_tensor(f"xe{j}", [P, NT, D], f32)) for j in range(2)]
        xeT = ctx.enter_context(nc.sbuf_tensor("xeT", [P, 2, CAP], f32))
        hT = ctx.enter_context(nc.sbuf_tensor("hT", [P, HID // P, CAP], f32))
        ye = [ctx.enter_context(nc.sbuf_tensor(f"ye{j}", [P, NT, D], f32)) for j in range(2)]
        b1_sb = [ctx.enter_context(nc.sbuf_tensor(f"b1_{j}", [P, HID // P], f32)) for j in range(2)]
        b2_sb = [ctx.enter_context(nc.sbuf_tensor(f"b2_{j}", [P, D], f32)) for j in range(2)]
        fx = [ctx.enter_context(nc.sbuf_tensor(f"fx{j}", [P, NC, D], f32)) for j in range(2)]
        fslot = [ctx.enter_context(nc.sbuf_tensor(f"fslot{j}", [P, NC * TOPK], u32)) for j in range(2)]
        fgate = [ctx.enter_context(nc.sbuf_tensor(f"fgate{j}", [P, NC * TOPK], f32)) for j in range(2)]
        frow = [ctx.enter_context(nc.sbuf_tensor(f"frow{j}", [P, NC, TOPK, D], f32)) for j in range(2)]
        fy = [ctx.enter_context(nc.sbuf_tensor(f"fy{j}", [P, NC, D], f32)) for j in range(2)]
        fbn = [ctx.enter_context(nc.sbuf_tensor(f"fbn{j}", [P, NC, 6], f32)) for j in range(2)]
        fmv = [ctx.enter_context(nc.sbuf_tensor(f"fmv{j}", [P, NC, 2], f32)) for j in range(2)]
        fve = [ctx.enter_context(nc.sbuf_tensor(f"fve{j}", [P, NC], f32)) for j in range(2)]
        frs = [ctx.enter_context(nc.sbuf_tensor(f"frs{j}", [P, NC], f32)) for j in range(2)]
        fo = [ctx.enter_context(nc.sbuf_tensor(f"fo{j}", [P, NC, D], f32)) for j in range(2)]

        eye = mk[:, M_EYE, :]

        def mask4(m):
            return mk[:, m, :].unsqueeze(1).broadcast_to([P, H, P])

        def heads(ap, width=HD):
            return ap.unsqueeze(3).broadcast_to([P, NC, H, width])

        def split(ap, h=H):
            return ap.rearrange("p c (h d) -> p c h d", h=h)

        block = ctx.enter_context(nc.Block())

        loads = [
            (mk[:, :, :], masks), (wqkv_sb[:, :, :, :], wqkv), (wb_sb[:, :, :], wb),
            (convw_sb[:, :, :, :], convw), (kmix_sb[:, :, :], kmix), (cmix_sb[:, :, :], cmix),
            (fw1_sb[:, :, :], fw1), (fw1s_sb[:, :], fw1s), (fb1_sb[:, :], fb1),
            (fw2_sb[:, :, :], fw2), (fb2_sb[:, :], fb2.partition_broadcast(P)),
            (onorm_sb[0:HD, :], onorm), (onorm_sb[HD:P, :], onorm), (wo_sb[:, :, :], wo),
            (xwT_sb[:, :, :, :], xwT), (bq_sb[:, :], xbq),
            (xb_sb[:, :, :], xbias.partition_broadcast(P)), (wr_sb[:, :, :], wr),
            (headsel_sb[:, :], headsel), (sel_sb[:, :, :], selector),
            (posq[:, :], positions.partition_broadcast(96)),
            (eids[:, :], expert_ids.partition_broadcast(P)),
            (offb_sb[:, :], boff), (refp_sb[:, :], ref_pos), (woff_sb[:, :, :, :], woff),
        ] + [(msw_sb[s][:, :, :], msw[s]) for s in range(3)]
        CONSTS = 16 * len(loads)

        @block.sync
        def _(sp):
            def a_loads(i):
                wait_filled_before(A, sp, i)
                sp.dma_start(xT_sb[:, :, :], xT[i, :, :, :]).then_inc(sem["xT_in"], 16)
                at_least(sp, sem["x1"], i * PER["x1"])
                sp.dma_start(xt_sb[:, :, :], x_tok[i, :, :, :]).then_inc(sem["xt_in"], 16)

            def b_loads(i):
                wait_filled_before(Bk, sp, i)
                sp.dma_start(ctxT_sb[:, :, :], ctxT[i, :, :, :]).then_inc(sem["ctx_in"], 16)
                at_least(sp, sem["ixp"], i * PER["ixp"])
                sp.dma_start(mask_sb[:, :], mask[i, :].partition_broadcast(96))\
                    .then_inc(sem["mask_in"], 16)

            def stores(i):
                sp.wait_ge(sem["x2"], (i + 1) * PER["x2"])
                sp.dma_start(x2_dram[i, :, :, :], x2[:, :, :]).then_inc(sem["x2_out"], 16)
                sp.wait_ge(sem["slots"], (i + 1) * PER["slots"])
                sp.dma_start(slot_dram[i, :, :], gslot_i[:, :]).then_inc(sem["slot_out"], 16)
                sp.dma_start(gate_dram[i, :, :], gate[:, :, :].rearrange("p c k -> p (c k)"))\
                    .then_inc(sem["gate_out"], 16)

            def load_weights(e, j):
                sp.dma_start(w1_sb[j][:, :, :], w1[e, :, :, :]).then_inc(sem[f"w_in{j}"], 16)
                sp.dma_start(w2_sb[j][:, :, :], w2[e, :, :, :]).then_inc(sem[f"w_in{j}"], 16)

            def load_rows(e, j):
                sp.dma_start(b1_sb[j][:, :], b1[e, :, :]).then_inc(sem[f"be_in{j}"], 16)
                sp.dma_start(b2_sb[j][:, :], b2[e, :].partition_broadcast(P))\
                    .then_inc(sem[f"be_in{j}"], 16)
                sp.dma_start(xe[j][:, :, :],
                             xe_dram[bass.ts(e, CAP), :].rearrange("(t p) d -> p t d", p=P))\
                    .then_inc(sem[f"xe_in{j}"], 16)

            for dst, src in loads:
                sp.dma_start(dst, src).then_inc(consts_in, 16)
            a_loads(0)
            b_loads(0)
            a_loads(1)
            stores(0)
            with sp.Fori(1, B - 1) as i:
                b_loads(i)
                a_loads(i + 1)
                stores(i)
            b_loads(B - 1)
            stores(B - 1)
            sp.wait_ge(sem["scatter"], B * PER["scatter"])
            sp.wait_ge(sem["gate_out"], B * PER["gate_out"])
            sp.wait_ge(sem["slot_out"], B * PER["slot_out"])
            sp.wait_ge(sem["x2_out"], B * PER["x2_out"])
            for j in range(2):
                load_weights(j, j)
                load_rows(j, j)

            def store_expert(e, j):
                wait_read(C, sp, e, C_USES[-1])
                sp.dma_start(ye_dram[bass.ts(e, CAP), :].rearrange("(t p) d -> p t d", p=P),
                             ye[j][:, :, :]).then_inc(sem["y_out"], 16)

            with sp.Fori(0, E // 2 - 1) as pair:
                for j in range(2):
                    e = pair * 2 + j
                    store_expert(e, j)
                    load_weights(e + 2, j)
                    load_rows(e + 2, j)
            for j in range(2):
                store_expert(E - 2 + j, j)

            def d_loads(i, j):
                sp.dma_start(fx[j][:, :, :], x2_dram[i, :, :, :]).then_inc(sem[f"f_in{j}"], 16)
                sp.dma_start(fslot[j][:, :], slot_dram[i, :, :]).then_inc(sem[f"f_in{j}"], 16)
                sp.dma_start(fgate[j][:, :], gate_dram[i, :, :]).then_inc(sem[f"f_in{j}"], 16)

            def d_store(i, j):
                sp.wait_ge(sem["fo"], (i + 1) * PER["fo"])
                sp.dma_start(out[i, :, :, :], fo[j][:, :, :]).then_inc(sem["out_done"], 16)

            for j in range(2):
                d_loads(j, j)
            with sp.Fori(0, B // 2 - 1) as pair:
                for j in range(2):
                    d_store(pair * 2 + j, j)
                    d_loads(pair * 2 + j + 2, j)
            for j in range(2):
                d_store(B - 2 + j, j)
            sp.wait_ge(sem["out_done"], B * PER["out_done"])

        @block.tensor
        def _(pe):
            def mm(o, lhsT, rhs, first=True, last=True):
                return nc.tensor.matmul(o, lhsT, rhs, start=first, stop=last)

            def turn(o, a, ident=None):
                return nc.tensor.transpose(o, a, eye if ident is None else ident)

            def turn_tiles(ring, i, use, src, *after):
                bank = take(ring, pe, i, use, *after)
                for hf in range(2):
                    for c in range(NC):
                        last = turn(bank[:, hf * T + c * P:hf * T + (c + 1) * P],
                                    src[:, c, hf * P:(hf + 1) * P])
                last.then_inc(ring["filled"], 1)

            def turn_chans(ring, i, use, src, *after):
                bank = take(ring, pe, i, use, *after)
                for c in range(NC):
                    for hf in range(2):
                        last = turn(bank[:, c * D + hf * P:c * D + (hf + 1) * P],
                                    src[:, hf, c * P:(c + 1) * P])
                last.then_inc(ring["filled"], 1)

            def chan_product(ring, i, use, w, src, *after, n=2):
                bank = take(ring, pe, i, use, *after)
                for m in range(n):
                    for k in range(2):
                        last = mm(bank[:, m * T:(m + 1) * T], w[:, k, m * P:(m + 1) * P],
                                  src[:, k, :], k == 0, k == 1)
                last.then_inc(ring["filled"], 1)

            def token_product(ring, i, use, src, w, *after):
                bank = take(ring, pe, i, use, *after)
                n = w.shape[2]
                for c in range(NC):
                    for k in range(2):
                        last = mm(bank[:, c * n:(c + 1) * n], src[:, k, c * P:(c + 1) * P],
                                  w[:, k, :], k == 0, k == 1)
                last.then_inc(ring["filled"], 1)

            def per_head(i, use, lhsT, rhs, after=()):
                bank = take(A, pe, i, use, *after)
                for h in range(H):
                    if rhs is None:
                        last = turn(bank[:, h * P:(h + 1) * P], lhsT(h))
                    else:
                        last = mm(bank[:, h * P:(h + 1) * P], lhsT(h), rhs(h))
                last.then_inc(A["filled"], 1)


            def stage_a(i):
                pe.wait_ge(sem["xT_in"], total("xT_in", i, 16))
                chan_product(A, i, "k_proj", wqkv_sb[:, 1, :, :], xT_sb)
                chan_product(A, i, "v_proj", wqkv_sb[:, 2, :, :], xT_sb)
                chan_product(A, i, "q_proj", wqkv_sb[:, 0, :, :], xT_sb)
                yield
                bank = take(A, pe, i, "sums")
                pe.wait_ge(sem["sq"], total("sq", i, 2))
                for c in range(NC):
                    for t in range(2):
                        for hf in range(2):
                            at = c * 8 + t * 4 + hf * 2
                            mm(bank[:, at:at + 2], sq[:, t, hf, c * P:(c + 1) * P], headsel_sb[:, :])
                for c in range(NC):
                    for k in range(2):
                        last = mm(bank[:, 16 + c * H:16 + (c + 1) * H],
                                  xT_sb[:, k, c * P:(c + 1) * P], wb_sb[:, k, :], k == 0, k == 1)
                last.then_inc(A["filled"], 1)
                turn_chans(A, i, "k_tok", qk[:, 1, :, :])
                pe.wait_ge(sem["silu"], total("silu", i, 2))
                turn_chans(A, i, "v_tok", vpad[:, :, PAD:])
                yield
                turn_tiles(A, i, "k_chan", kn, "k_tok")
                yield

                def chunk(c):
                    return slice(c * P, (c + 1) * P)

                steps = {
                    "gram": lambda c: per_head(i, f"gram{c}", lambda h: kz[:, h // 2, h % 2, chunk(c)],
                                               lambda h: kz[:, h // 2, h % 2, chunk(c)],
                                               ["k_chan"]),
                    "gramT": lambda c: per_head(i, f"gramT{c}", lambda h: nbG[c][:, h, :], None,
                                                [f"gram{c}"]),
                    "P2": lambda c: (pe.wait_ge(sem["x8"], total("x8", i, c + 1)),
                                     per_head(i, f"P2{c}", lambda h: XT[c][0][:, h, :],
                                              lambda h: X8[c][:, h, :], [f"gramT{c}"])),
                    "P2T": lambda c: per_head(i, f"P2T{c}", lambda h: X8[c][:, h, :],
                                              lambda h: XT[c][0][:, h, :]),
                    "P4": lambda c: per_head(i, f"P4{c}", lambda h: W[c][1][:, h, :],
                                             lambda h: W[c][0][:, h, :], [f"P2{c}", f"P2T{c}"]),
                    "T2T": lambda c: (pe.wait_ge(sem["t1"], total("t1", i, c + 1)),
                                      per_head(i, f"T2T{c}", lambda h: W[c][0][:, h, :],
                                               lambda h: Ta[c][:, h, :])),
                    "T8T": lambda c: per_head(i, f"T8T{c}", lambda h: W[c][2][:, h, :],
                                              lambda h: Tb[c][:, h, :], [f"P4{c}", f"T2T{c}"]),
                    "T8": lambda c: per_head(i, f"T8{c}", lambda h: Ta[c][:, h, :], None,
                                             [f"T8T{c}"]),
                    "aT": lambda c: per_head(i, f"aT{c}", lambda h: kz[:, h // 2, h % 2, chunk(c)],
                                             lambda h: qk[:, 0, h // 2, chunk(c)]),
                }
                for s, (t, w, wt, w2_, u, tt) in enumerate(
                        [("T8", "W", "WT", "W2", "U", "T32T"), ("T32", "Y", "YT", "Y2", "V", "TT")]):
                    def level(s=s, t=t, w=w, wt=wt, w2_=w2_, u=u, tt=tt):
                        xo = s + 1
                        return {
                            w: lambda c: per_head(i, f"{w}{c}", lambda h: XT[c][xo][:, h, :],
                                                  lambda h: Tn[c][:, h, :], [f"{t}{c}"]),
                            wt: lambda c: per_head(i, f"{wt}{c}", lambda h: Tn[c][:, h, :],
                                                   lambda h: XT[c][xo][:, h, :]),
                            w2_: lambda c: per_head(i, f"{w2_}{c}", lambda h: W[c][1][:, h, :],
                                                    lambda h: W[c][0][:, h, :],
                                                    [f"{w}{c}", f"{wt}{c}"]),
                            u: lambda c: per_head(i, f"{u}{c}", lambda h: W[c][2][:, h, :],
                                                  lambda h: Ta[c][:, h, :], [f"{w2_}{c}"]),
                            tt: lambda c: per_head(i, f"{tt}{c}", lambda h: W[c][0][:, h, :],
                                                   lambda h: Tb[c][:, h, :], [f"{u}{c}"]),
                        }
                    steps.update(level())
                steps["T32"] = lambda c: per_head(i, f"T32{c}", lambda h: Ta[c][:, h, :], None,
                                                  [f"T32T{c}"])
                for name in INVERSE:
                    for c in range(NC):
                        steps[name](c)
                    yield

                pe.wait_ge(sem["vb"], total("vb", i, 1))
                bank = take(A, pe, i, "u0", "TT0")
                for h in range(H):
                    last = mm(bank[:, h * HD:(h + 1) * HD], Ta[0][:, h, :],
                              vb[:, 0, h * HD:(h + 1) * HD])
                last.then_inc(A["filled"], 1)
                pe.wait_ge(sem["kb"], total("kb", i, 1))
                bank = take(A, pe, i, "wT1", "TT1")
                for h in range(H):
                    last = mm(bank[(h % 2) * HD:(h % 2 + 1) * HD, (h // 2) * P:(h // 2 + 1) * P],
                              kb[:, h * HD:(h + 1) * HD], Ta[1][:, h, :])
                last.then_inc(A["filled"], 1)
                yield
                bank = take(A, pe, i, "S0", "u0")
                for h in range(H):
                    last = mm(bank[(h % 2) * HD:(h % 2 + 1) * HD, h * HD:(h + 1) * HD],
                              kn[:, 0, h * HD:(h + 1) * HD], u_sb[0][:, h * HD:(h + 1) * HD])
                last.then_inc(A["filled"], 1)
                bank = take(A, pe, i, "o0", "aT0")
                for h in range(H):
                    last = mm(bank[:, h * HD:(h + 1) * HD], aT[0][:, h, :],
                              u_sb[0][:, h * HD:(h + 1) * HD])
                last.then_inc(A["filled"], 1)
                yield
                bank = take(A, pe, i, "u1", "wT1", "S0")
                for h in range(H):
                    mm(bank[:, h * HD:(h + 1) * HD], Ta[1][:, h, :],
                       vb[:, 1, h * HD:(h + 1) * HD], True, False)
                    last = mm(bank[:, h * HD:(h + 1) * HD], wTn[:, h // 2, :], S_sb[:, h, :],
                              False, True)
                last.then_inc(A["filled"], 1)
                yield
                bank = take(A, pe, i, "o1", "u1", "aT1")
                for h in range(H):
                    mm(bank[:, h * HD:(h + 1) * HD], aT[1][:, h, :],
                       u_sb[1][:, h * HD:(h + 1) * HD], True, False)
                    last = mm(bank[:, h * HD:(h + 1) * HD], qk[:, 0, h // 2, P:T], S_sb[:, h, :],
                              False, True)
                last.then_inc(A["filled"], 1)

                yield
                pe.wait_ge(sem["taps"], total("taps", i, PER["taps"]))
                bank = take(A, pe, i, "mix")
                for m in range(2):
                    for k in range(3):
                        j = 3 * m + k
                        last = mm(bank[:, m * T:(m + 1) * T], kmix_sb[:, j, :],
                                  acc[:, j // 2, j % 2, :], k == 0, k == 2)
                last.then_inc(A["filled"], 1)
                yield
                token_product(A, i, "ms", y1, cmix_sb, "mix")
                yield
                pe.wait_ge(sem["stat"], total("stat", i, 3))
                bank = take(A, pe, i, "statT")
                for c in range(NC):
                    last = turn(bank[0:3 * H, c * P:(c + 1) * P], st[:, c, :])
                last.then_inc(A["filled"], 1)
                yield
                for n in range(2):
                    bank = take(A, pe, i, f"hid{n}", "statT")
                    for m in range(2):
                        at = (2 * n + m) * P
                        for k in range(2):
                            mm(bank[:, m * T:(m + 1) * T], fw1_sb[:, k, at:at + P], xT_sb[:, k, :],
                               k == 0, False)
                        last = mm(bank[:, m * T:(m + 1) * T], fw1s_sb[:, at:at + P], gst[:, :],
                                  False, True)
                    last.then_inc(A["filled"], 1)
                yield
                bank = take(A, pe, i, "logit", "hid0", "hid1")
                for c in range(NC):
                    for m in range(4):
                        last = mm(bank[:, c * 3 * H:(c + 1) * 3 * H], hdn[:, m, c * P:(c + 1) * P],
                                  fw2_sb[:, m, :], m == 0, m == 3)
                last.then_inc(A["filled"], 1)
                yield
                pe.wait_ge(sem["on"], total("on", i, 1))
                turn_tiles(A, i, "oT", o1)
                yield
                token_product(A, i, "attn", oT, wo_sb, "oT")
                yield

            def stage_b(i):
                pe.wait_ge(sem["ctx_in"], total("ctx_in", i, 16))
                for use, t in (("Kt", 0), ("Vt", 1)):
                    bank = take(Bk, pe, i, use)
                    for k in range(2):
                        last = mm(bank[0:S2, 0:D], ctxT_sb[:, k, :], xwT_sb[:, t, k, :],
                                  k == 0, k == 1)
                    last.then_inc(Bk["filled"], 1)
                yield
                pe.wait_ge(sem["x1"], total("x1", i, 2))
                turn_tiles(Bk, i, "x1T", x1)
                yield
                chan_product(Bk, i, "Qc", xwT_sb[:, 2, :, :], x1T, "x1T")
                yield
                for n, groups in ((0, (0, 1)), (1, (2,))):
                    bank = take(Bk, pe, i, f"off{n}", "Qc")
                    for m, g in enumerate(groups):
                        for k in range(2):
                            last = mm(bank[0:96, m * T:(m + 1) * T], woff_sb[:, k, g, :],
                                      QT[:, k, :], k == 0, k == 1)
                    last.then_inc(Bk["filled"], 1)
                yield
                turn_chans(Bk, i, "Qt", QT)
                yield

                def distances(k, half):
                    for j in range(XH // 4):
                        bank = take(Bk, pe, i, f"dist{k}{half}_{j}")
                        for m in range(2):
                            r = (k % 2) * XH + half * XH // 2 + 2 * j + m
                            last = mm(bank[0:S2, m * T:(m + 1) * T], sel_sb[:, r, :],
                                      ixp[:, k // 2, :])
                        last.then_inc(Bk["filled"], 1)

                def gathers(k, half):
                    pe.wait_ge(sem["nhat"], total("nhat", i, 2 * k + half + 1))
                    if k == 0 and half == 0:
                        wait_read(Bk, pe, i, "Kt", "Vt")
                    for c in range(NC):
                        use = f"gather{k}_{c}"
                        bank = bank_of(G, use) if half else take(G, pe, i, use)
                        for h in range(XH // 2):
                            head = half * XH // 2 + h
                            last = mm(bank[:, head * 32:(head + 1) * 32],
                                      nhat[half][:, h, c * P:(c + 1) * P],
                                      tab[:, head, :, :].rearrange("p a d -> p (a d)"))
                        if half:
                            last.then_inc(G["filled"], 1)
                    if not half:
                        last.then_inc(sem["hats_used"], 1)

                pe.wait_ge(sem["ixp"], total("ixp", i, PER["ixp"]))
                distances(0, 0)
                distances(0, 1)
                yield
                for k in range(NK):
                    for half in range(2):
                        gathers(k, half)
                        if k + 1 < NK:
                            distances(k + 1, half)
                        yield
                yield
                pe.wait_ge(sem["actx"], total("actx", i, 2))
                turn_tiles(Bk, i, "ctxT", actx)
                yield
                token_product(Bk, i, "xout", cT, xwT_sb[:, 3, :, :], "ctxT")
                yield
                pe.wait_ge(sem["x2"], total("x2", i, 2))
                turn_tiles(Bk, i, "x2T", x2)
                yield
                token_product(Bk, i, "route", x2T, wr_sb, "x2T")
                yield
                pe.wait_ge(sem["ohs"], total("ohs", i, 2))
                bank = take(Bk, pe, i, "pos")
                for c in range(NC):
                    o = bank[:, c * E:(c + 1) * E]
                    mm(o, mk[:, M_BEFORE, :], ohs[:, c, :], True, False)
                    if c == 1:
                        mm(o, mk[:, M_ONES, :], ohs[:, 0, :], False, False)
                    last = mm(o, mk[:, M_ONES, :], count[:, :], False, True)
                last.then_inc(Bk["filled"], 1)
                yield

            def stage_c(e, pair, j):
                pe.wait_ge(sem[f"w_in{j}"], (pair + 1) * PER["w_in0"])
                pe.wait_ge(sem[f"xe_in{j}"], (pair + 1) * PER["xe_in0"])
                for n in range(NT // 2):
                    bank = take(C, pe, e, f"xeT{n}")
                    for k in range(2):
                        for t in range(2):
                            last = turn(bank[:, k * T + t * P:k * T + (t + 1) * P],
                                        xe[j][:, 2 * n + t, k * P:(k + 1) * P])
                    last.then_inc(C["filled"], 1)
                for m in range(HID // P):
                    for part, (lo, hi) in (("a", (0, 512)), ("b", (512, CAP))):
                        bank = take(C, pe, e, f"h{m}{part}", *(C_USES[:NT // 2] if m == 0 else ()))
                        for k in range(2):
                            last = mm(bank[:, 0:hi - lo], w1_sb[j][:, k, m * P:(m + 1) * P],
                                      xeT[:, k, lo:hi], k == 0, k == 1)
                        last.then_inc(C["filled"], 1)
                for n in range(NT // 2):
                    bank = take(C, pe, e, f"y{n}", *(C_USES[NT // 2:-NT // 2] if n == 0 else ()))
                    for t in range(2):
                        at = (2 * n + t) * P
                        for m in range(HID // P):
                            last = mm(bank[:, t * D:(t + 1) * D], hT[:, m, at:at + P],
                                      w2_sb[j][:, m, :], m == 0, m == HID // P - 1)
                    last.then_inc(C["filled"], 1)

            pe.wait_ge(consts_in, CONSTS)
            pe.wait_ge(prepared, PREPARED)
            pe.wait_ge(zeroed, ZEROED)
            run(("A", stage_a(0)))
            run(("A", stage_a(1)), ("B", stage_b(0)))
            with pe.Fori(1, B - 1) as i:
                run(("A", stage_a(i + 1)), ("B", stage_b(i)))
            run(("B", stage_b(B - 1)))
            for ring, banks in ((A, 4), (Bk, 2), (G, 2)):
                for b in range(banks):
                    pe.wait_ge(ring["read"][b], B * ring["per"][b])
            for j in range(2):
                stage_c(j, 0, j)
            with pe.Fori(1, E // 2) as pair:
                for j in range(2):
                    stage_c(pair * 2 + j, pair, j)

        @block.scalar
        def _(act):
            def read_out(ring, i, use, dst, view, func=ACT.Copy, **kw):
                bank = wait_filled(ring, act, i, use)
                nc.scalar.activation(dst, view(bank), func, **kw).then_inc(was_read(ring, use), 1)

            def all_of(bank):
                return bank[:, :]

            def halves(bank):
                return bank[:, :].rearrange("p (c t) -> p c t", c=2)

            def per_head(bank):
                return bank[:, :].rearrange("p (h t) -> p h t", h=H)

            def stage_a(i):
                for use, t in (("k_proj", 1), ("v_proj", 2), ("q_proj", 0)):
                    read_out(A, i, use, pre[:, t, :, 3:], halves)
                for n, t in enumerate((1, 2, 0)):
                    act.wait_ge(sem["conv"], total("conv", i, 8 * (n + 1)))
                    act.activation(th[:, t, :, :], y[:, t, :, :], ACT.Tanh).then_inc(sem["tanh"], 1)
                yield
                wait_read(A, act, i, "sums")
                act.activation(bth[:, :, :], sums[:, 16:24].rearrange("p (c h) -> p c h", c=NC),
                               ACT.Tanh, scale=0.5).then_inc(sem["beta_th"], 1)
                read_out(A, i, "v_tok", vt[:, :, :], halves)
                yield
                bank = wait_filled(A, act, i, "k_chan")
                for m in range(2):
                    rows = slice(m * HD, (m + 1) * HD)
                    last = act.activation(kz[rows, :, m, :], halves(bank)[rows], ACT.Copy)
                last.then_inc(was_read(A, "k_chan"), 1)
                yield
                into = {"P2": lambda c: W[c][0], "P2T": lambda c: W[c][1], "P4": lambda c: W[c][2],
                        "T8": lambda c: Tn[c], "W": lambda c: W[c][0], "WT": lambda c: W[c][1],
                        "W2": lambda c: W[c][2], "T32": lambda c: Tn[c], "Y": lambda c: W[c][0],
                        "YT": lambda c: W[c][1], "Y2": lambda c: W[c][2]}
                for name in INVERSE:
                    for c in range(NC):
                        if name in into:
                            read_out(A, i, f"{name}{c}", into[name](c)[:, :, :], per_head)
                    yield
                read_out(A, i, "u0", u_sb[0][:, :], lambda b: b[:, 0:D])
                read_out(A, i, "wT1", wTn[:, :, :],
                         lambda b: b[:, 0:2 * P].rearrange("p (c t) -> p c t", c=2), scale=-1.0)
                yield
                bank = wait_filled(A, act, i, "S0")
                for m in range(2):
                    rows = slice(m * HD, (m + 1) * HD)
                    last = act.activation(
                        S_sb[rows, m:H:2, :],
                        bank[rows, 0:D].rearrange("p (h d) -> p h d", h=H)[:, m:H:2, :], ACT.Copy)
                last.then_inc(was_read(A, "S0"), 1)
                yield
                read_out(A, i, "u1", u_sb[1][:, :], lambda b: b[:, 0:D])
                yield
                yield
                read_out(A, i, "mix", y1[:, :, :], halves)
                yield
                read_out(A, i, "ms", ms[:, :, :], halves)
                yield
                read_out(A, i, "statT", gst[:, :], lambda b: b[0:3 * H, 0:T], scale=1.0 / HD)
                yield
                for n in range(2):
                    bank = wait_filled(A, act, i, f"hid{n}")
                    for m in range(2):
                        last = nc.scalar.activation(hdn[:, 2 * n + m, :], bank[:, m * T:(m + 1) * T],
                                                    ACT.Gelu, bias=fb1_sb[:, 2 * n + m:2 * n + m + 1])
                    last.then_inc(was_read(A, f"hid{n}"), 1)
                yield
                act.wait_ge(sem["fuse"], total("fuse", i, 2))
                act.activation(lex[:, :, :], lg[:, :, :], ACT.Exp).then_inc(sem["wexp"], 1)
                yield
                read_out(A, i, "oT", oT[:, :, :], halves)
                yield
                yield

            def stage_b(i):
                yield
                read_out(Bk, i, "x1T", x1T[:, :, :], halves)
                yield
                bank = wait_filled(Bk, act, i, "Qc")
                for m in range(2):
                    last = nc.scalar.activation(QT[:, m, :], bank[:, m * T:(m + 1) * T],
                                                ACT.Identity, bias=bq_sb[:, m:m + 1])
                last.then_inc(was_read(Bk, "Qc"), 1)
                yield
                yield
                at_least(act, sem["prod"], total("prod", i, 0))
                read_out(Bk, i, "Qt", Qs[:, :, :], halves, scale=0.5 * XD ** -0.5)
                yield

                def distances(k, half):
                    if half:
                        at_least(act, G["filled"], i * G["uses"] + k * NC)
                    else:
                        at_least(act, sem["hats_used"], i * PER["hats_used"] + k)
                    for j in range(XH // 4):
                        read_out(Bk, i, f"dist{k}{half}_{j}", nhat[half][:, 2 * j:2 * j + 2, :],
                                 lambda b: b[0:S2, :].rearrange("p (m t) -> p m t", m=2), ACT.Abs)

                distances(0, 0)
                distances(0, 1)
                yield
                at_least(act, sem["actx"], total("actx", i, 0))
                for k in range(NK):
                    if k + 1 < NK:
                        distances(k + 1, 0)
                    yield
                    for c in range(NC):
                        read_out(G, i, f"gather{k}_{c}",
                                 gs[:, c, k, :, :, :].rearrange("p h a d -> p (h a d)"), all_of)
                    if k + 1 < NK:
                        distances(k + 1, 1)
                    yield
                act.wait_ge(sem["scs"], total("scs", i, 2))
                act.activation(sce[:, :, :, :], scd[:, :, :, :], ACT.Exp).then_inc(sem["sexp"], 1)
                yield
                read_out(Bk, i, "ctxT", cT[:, :, :], halves)
                yield
                yield
                read_out(Bk, i, "x2T", x2T[:, :, :], halves)
                yield
                wait_read(Bk, act, i, "route")
                act.activation(prx[:, :, :], prd[:, :, :], ACT.Exp).then_inc(sem["rexp"], 1)
                yield
                yield

            def stage_c(e, pair, j):
                act.wait_ge(sem[f"be_in{j}"], (pair + 1) * PER["be_in0"])
                for n in range(NT // 2):
                    read_out(C, e, f"xeT{n}", xeT[:, :, 2 * n * P:(2 * n + 2) * P], halves)
                for m in range(HID // P):
                    for part, (lo, hi) in (("a", (0, 512)), ("b", (512, CAP))):
                        read_out(C, e, f"h{m}{part}", hT[:, m, lo:hi],
                                 lambda b, n=hi - lo: b[:, 0:n], ACT.Relu,
                                 bias=b1_sb[j][:, m:m + 1])

            act.wait_ge(consts_in, CONSTS)
            act.wait_ge(zeroed, ZEROED)
            act.wait_ge(xe_zero, 48)
            run(("A", stage_a(0)))
            run(("A", stage_a(1)), ("B", stage_b(0)))
            with act.Fori(1, B - 1) as i:
                run(("A", stage_a(i + 1)), ("B", stage_b(i)))
            run(("B", stage_b(B - 1)))
            for j in range(2):
                stage_c(j, 0, j)
            with act.Fori(1, E // 2) as pair:
                for j in range(2):
                    stage_c(pair * 2 + j, pair, j)

        @block.vector
        def _(dve):
            given, batch = {}, {}

            def begin(i, names):
                for name in names:
                    given[name], batch[name] = 0, i

            def end(names):
                for name in names:
                    assert given[name] == PER[name], (name, given[name], PER[name])

            def count_in(ins, name):
                given[name] += 1
                ins.then_inc(sem[name], 1)

            def own(name, k):
                dve.wait_ge(sem[name], batch[name] * PER[name] + k)

            def link(ins, name):
                count_in(ins, name)
                own(name, given[name])

            def stage_a(i):
                names = ("conv", "silu", "beta", "t1", "taps", "stat", "fuse", "osum", "orms", "on",
                       "var1", "x1")
                begin(i, names)

                def short_conv(t):
                    for tap in range(4):
                        for hf in range(2):
                            w = convw_sb[:, t, hf, tap:tap + 1]
                            src = pre[:, t, hf, tap:tap + T]
                            if tap == 0:
                                ins = dve.tensor_scalar(y[:, t, hf, :], src, w, None, ALU.mult)
                            else:
                                own("conv", given["conv"] - 1)
                                ins = dve.scalar_tensor_tensor(y[:, t, hf, :], src, w,
                                                               y[:, t, hf, :], ALU.mult, ALU.add)
                            count_in(ins, "conv")

                def silu(n, t, dst):
                    dve.wait_ge(sem["tanh"], total("tanh", i, n))
                    count_in(dve.scalar_tensor_tensor(dst, th[:, t, :, :], 1.0, y[:, t, :, :],
                                                    ALU.add, ALU.mult), "silu")

                done = [0]

                def taps(n):
                    for _ in range(n):
                        if done[0] == PER["taps"]:
                            return
                        tap, scale, hf = TAP_ORDER[done[0]]
                        w = msw_sb[scale][:, hf, tap:tap + 1]
                        at = PAD - (TAPS[scale] - 1) + tap
                        src = vpad[:, hf, at:at + T]
                        dst = acc[:, scale, hf, :]
                        if tap == 0:
                            ins = dve.tensor_scalar(dst, src, w, None, ALU.mult)
                        else:
                            own("taps", TAP_AT[tap - 1, scale, hf] + 1)
                            ins = dve.scalar_tensor_tensor(dst, src, w, dst, ALU.mult, ALU.add)
                        count_in(ins, "taps")
                        done[0] += 1

                wait_read(A, dve, i, "k_proj")
                short_conv(1)
                wait_read(A, dve, i, "v_proj")
                short_conv(2)
                silu(1, 1, qk[:, 1, :, :])
                wait_read(A, dve, i, "q_proj")
                short_conv(0)
                silu(2, 2, vpad[:, :, PAD:])
                silu(3, 0, qk[:, 0, :, :])
                own("silu", 2)
                taps(6)
                yield
                bank = wait_filled(A, dve, i, "sums")
                dve.tensor_copy(sums[:, :], bank[:, 0:24]).then_inc(was_read(A, "sums"), 1)
                dve.wait_ge(sem["beta_th"], total("beta_th", i, 1))
                count_in(dve.tensor_scalar(beta[:, :, :], bth[:, :, :], 0.5, 0.5, ALU.mult, ALU.add),
                       "beta")
                link(dve.tensor_scalar(nbeta[:, :, :], bth[:, :, :], -0.5, -0.5, ALU.mult, ALU.add),
                     "beta")
                dve.wait_ge(sem["rinv"], total("rinv", i, 2))
                bank = wait_filled(A, dve, i, "k_tok")
                dve.tensor_tensor(split(kn[:, :, :]),
                                  bank[:, :].rearrange("p (c h d) -> p c h d", c=NC, h=H),
                                  heads(rinv[:, :, 1, :]), ALU.mult)\
                    .then_inc(was_read(A, "k_tok"), 1)
                yield
                yield

                def evict(use, dst, in1, op):
                    bank = wait_filled(A, dve, i, use)
                    dve.tensor_tensor(dst, bank[:, :].rearrange("p (h t) -> p h t", h=H), in1, op)\
                        .then_inc(was_read(A, use), 1)

                for name in INVERSE:
                    for c in range(NC):
                        use = f"{name}{c}"
                        if name == "gram":
                            evict(use, nbG[c][:, :, :],
                                  nbeta[:, c, :].unsqueeze(2).broadcast_to([P, H, P]), ALU.mult)
                        elif name == "gramT":
                            bank = wait_filled(A, dve, i, use)
                            for n, m in enumerate((M_IN128T, M_IN32T, M_DIAG8T)):
                                last = dve.tensor_tensor(
                                    XT[c][2 - n][:, :, :],
                                    bank[:, :].rearrange("p (h t) -> p h t", h=H), mask4(m), ALU.mult)
                            last.then_inc(was_read(A, use), 1)
                            wait_read(A, dve, i, use)
                            link(dve.tensor_tensor(Ta[c][:, :, :], XT[c][0][:, :, :], mask4(M_EYE),
                                                   ALU.add), "t1")
                        elif name in ("T2T", "U", "V"):
                            evict(use, Tb[c][:, :, :], Ta[c][:, :, :], ALU.add)
                            wait_read(A, dve, i, use)
                        elif name in ("T8T", "T32T", "TT"):
                            evict(use, Ta[c][:, :, :], Tb[c][:, :, :], ALU.add)
                            wait_read(A, dve, i, use)
                        elif name == "aT":
                            evict(use, aT[c][:, :, :], mask4(M_INCL), ALU.mult)
                        taps(3 if name not in ("gram", "gramT", "aT") else 1)
                    yield
                yield
                for c in range(NC):
                    bank = wait_filled(A, dve, i, f"o{c}")
                    dve.tensor_tensor(delta[:, c, :].rearrange("p (h d) -> p h d", h=H),
                                      bank[:, 0:D].rearrange("p (h d) -> p h d", h=H),
                                      rinv[:, c, 0, :].unsqueeze(2).broadcast_to([P, H, HD]),
                                      ALU.mult).then_inc(was_read(A, f"o{c}"), 1)
                    if c == 0:
                        taps(PER["taps"])
                        yield
                        yield
                yield
                yield
                wait_read(A, dve, i, "o0", "o1", "v_tok", "ms")
                for n, src in enumerate((ms, delta, vt)):
                    count_in(dve.tensor_reduce(st[:, :, n * H:(n + 1) * H], split(src[:, :, :]),
                                             AX.X, ALU.add, apply_absolute_value=True), "stat")
                yield
                yield
                yield
                bank = wait_filled(A, dve, i, "logit")
                dve.tensor_tensor(lg[:, :, :].rearrange("p (c h) x -> p c (h x)", c=NC),
                                  bank[:, 0:6 * H].rearrange("p (c x) -> p c x", c=NC),
                                  fb2_sb[:, :].unsqueeze(1).broadcast_to([P, NC, 3 * H]),
                                  ALU.add).then_inc(was_read(A, "logit"), 1)
                wait_read(A, dve, i, "logit")
                link(dve.tensor_reduce(lmx[:, :], lg[:, :, :], AX.X, ALU.max), "fuse")

                def over3(ap):
                    return ap.unsqueeze(2).broadcast_to([P, NC * H, 3])

                link(dve.tensor_tensor(lg[:, :, :], lg[:, :, :], over3(lmx[:, :]), ALU.subtract),
                     "fuse")
                dve.wait_ge(sem["wexp"], total("wexp", i, 1))
                link(dve.tensor_reduce(lmx[:, :], lex[:, :, :], AX.X, ALU.add), "fuse")
                link(dve.reciprocal(lmx[:, :], lmx[:, :]), "fuse")
                link(dve.tensor_tensor(wts[:, :, :], lex[:, :, :], over3(lmx[:, :]), ALU.mult),
                     "fuse")

                def weight(n):
                    return heads(wts[:, :, n].rearrange("p (c h) -> p c h", c=NC))

                dve.tensor_tensor(split(o1[:, :, :]), split(ms[:, :, :]), weight(0), ALU.mult)
                link(dve.tensor_tensor(split(o2[:, :, :]), split(delta[:, :, :]), weight(1),
                                       ALU.mult), "fuse")
                link(dve.tensor_tensor(o1[:, :, :], o1[:, :, :], o2[:, :, :], ALU.add), "osum")
                dve.wait_ge(sem["v3"], total("v3", i, 1))
                link(dve.tensor_tensor(o1[:, :, :], o1[:, :, :], o3[:, :, :], ALU.add), "osum")
                dve.wait_ge(sem["osq"], total("osq", i, 1))
                link(dve.tensor_reduce(rms[:, :].rearrange("p (c h) -> p c h", c=NC),
                                       split(o2[:, :, :]), AX.X, ALU.add), "orms")
                link(dve.tensor_scalar(rms[:, :], rms[:, :], 1.0 / HD, EPS, ALU.mult, ALU.add),
                     "orms")
                dve.wait_ge(sem["orr"], total("orr", i, 1))
                link(dve.tensor_tensor(split(o1[:, :, :]), split(o1[:, :, :]),
                                       heads(rrms[:, :].rearrange("p (c h) -> p c h", c=NC)),
                                       ALU.mult), "on")
                yield
                yield
                dve.wait_ge(sem["xt_in"], total("xt_in", i, 16))
                bank = wait_filled(A, dve, i, "attn")
                dve.tensor_tensor(xr[:, :, :], bank[:, :].rearrange("p (c d) -> p c d", c=NC),
                                  xt_sb[:, :, :], ALU.add).then_inc(was_read(A, "attn"), 1)
                wait_read(A, dve, i, "attn")
                layer_norm(i, xr, x1, bns, mv, ve, rstd, "var1", "rstd1", "x1")
                end(names)
                yield

            def layer_norm(i, src, dst, bn, m, v, r, var, rs, done):
                for c in range(NC):
                    count_in(dve.bn_stats(bn[:, c, :], src[:, c, :]), var)
                own(var, given[var])
                dve.nop(nofuse=True)
                for c in range(NC):
                    last = dve.bn_aggr(m[:, c, :], bn[:, c, :])
                link(last, var)
                link(dve.tensor_scalar(v[:, :], m[:, :, 1], EPS, None, ALU.add), var)
                dve.wait_ge(sem[rs], total(rs, i, 1))
                for c in range(NC):
                    count_in(dve.tensor_scalar(dst[:, c, :], src[:, c, :], m[:, c, 0:1],
                                             r[:, c:c + 1], ALU.subtract, ALU.mult), done)

            def stage_b(i):
                names = ("length", "ixp", "nhat", "scr", "scs", "att", "av0", "actx", "var2", "x2",
                       "rmax", "top", "ohs", "count", "slots")
                begin(i, names)
                dve.wait_ge(sem["mask_in"], total("mask_in", i, 16))
                link(dve.tensor_copy(maskf[:, :], mask_sb[:, :]), "length")
                link(dve.tensor_reduce(msum[:, :], maskf[:, :], AX.X, ALU.add), "length")
                link(dve.tensor_scalar(Lb[:, :], msum[:, :], -1.0, float(S2 - 1), ALU.mult, ALU.add),
                     "length")
                link(dve.reciprocal(rL[:, :], Lb[:, :]), "length")
                for n, use in enumerate(("Kt", "Vt")):
                    bank = wait_filled(Bk, dve, i, use)
                    dve.scalar_tensor_tensor(tab[:, :, n, :],
                                             bank[0:S2, 0:D].rearrange("p (h d) -> p h d", h=XH),
                                             (-1.0, -0.5)[n],
                                             xb_sb[0:S2, n, :].rearrange("p (h d) -> p h d", h=XH),
                                             ALU.mult, ALU.subtract)\
                        .then_inc(was_read(Bk, use), 1)
                at_least(dve, G["filled"], i * G["uses"])
                yield
                yield
                yield
                for n, groups in ((0, (0, 1)), (1, (2,))):
                    bank = wait_filled(Bk, dve, i, f"off{n}")
                    for m, g in enumerate(groups):
                        last = dve.scalar_tensor_tensor(loc[:, g, :], bank[0:96, m * T:(m + 1) * T],
                                                        offc_sb[:, g:g + 1], posq[:, :],
                                                        ALU.add, ALU.add)
                    last.then_inc(was_read(Bk, f"off{n}"), 1)
                wait_read(Bk, dve, i, "off0", "off1")
                link(dve.tensor_scalar(tmp[:, :, :], loc[:, :, :], rL[:, :], None, ALU.mult), "ixp")
                link(dve.tensor_scalar(tmp[:, :, :], tmp[:, :, :], ROUND, None, ALU.add), "ixp")
                link(dve.tensor_scalar(tmp[:, :, :], tmp[:, :, :], ROUND, Lb[:, :], ALU.subtract,
                                       ALU.mult), "ixp")
                link(dve.tensor_tensor(loc[:, :, :], loc[:, :, :], tmp[:, :, :], ALU.subtract),
                     "ixp")
                link(dve.tensor_scalar(tmp[:, :, :], loc[:, :, :], Lb[:, :], 0.0, ALU.mult,
                                       ALU.is_lt), "ixp")
                link(dve.tensor_scalar(tmp[:, :, :], tmp[:, :, :], Lb[:, :], None, ALU.mult), "ixp")
                link(dve.tensor_tensor(loc[:, :, :], loc[:, :, :], tmp[:, :, :], ALU.add), "ixp")
                link(dve.tensor_scalar(loc[:, :, :], loc[:, :, :], S2 / (S2 - 1.0), -0.5, ALU.mult,
                                       ALU.add), "ixp")
                wait_filled_before(Bk, dve, i)
                link(dve.tensor_copy(ixp[0:96, :, :], loc[:, :, :]), "ixp")
                link(dve.tensor_tensor(loc[:, :, :], loc[:, :, :], ixp[0:96, :, :], ALU.subtract),
                     "ixp")
                count_in(dve.tensor_copy(ixp[32:64, :, :], loc[32:64, :, :]), "ixp")
                link(dve.tensor_copy(ixp[64:96, :, :], loc[64:96, :, :]), "ixp")
                link(dve.tensor_tensor(ixp[64:96, :, :], loc[64:96, :, :], ixp[64:96, :, :],
                                       ALU.subtract), "ixp")
                def weights(k, half):
                    wait_read(Bk, dve, i, f"dist{k}{half}_{XH // 4 - 1}", f"dist{k}{half}_{XH // 4 - 2}")
                    count_in(dve.tensor_scalar(nhat[half][:, :, :], nhat[half][:, :, :], 1.0, 0.0,
                                               ALU.subtract, ALU.min), "nhat")

                yield
                yield
                weights(0, 0)
                weights(0, 1)
                yield
                for k in range(NK):
                    for half in range(2):
                        if k + 1 < NK:
                            weights(k + 1, half)
                        if half:
                            score(i, k)
                        yield
                own("scr", NK)
                link(dve.tensor_reduce(scm[:, :, :], sc[:, :, :, :].rearrange("p c k h -> p c h k"),
                                       AX.X, ALU.max), "scs")

                def over_k(ap):
                    return ap.unsqueeze(2).broadcast_to([P, NC, NK, XH])

                link(dve.tensor_tensor(scd[:, :, :, :], sc[:, :, :, :], over_k(scm[:, :, :]),
                                       ALU.subtract), "scs")
                dve.wait_ge(sem["sexp"], total("sexp", i, 1))
                link(dve.tensor_reduce(scm[:, :, :], sce[:, :, :, :].rearrange("p c k h -> p c h k"),
                                       AX.X, ALU.add), "att")
                link(dve.reciprocal(scm[:, :, :], scm[:, :, :]), "att")
                link(dve.tensor_tensor(sce[:, :, :, :], sce[:, :, :, :], over_k(scm[:, :, :]),
                                       ALU.mult), "att")
                link(dve.tensor_tensor(av[:, 0, :, :, :], gs[:, 0, :, :, 1, :],
                                       sce[:, 0, :, :].unsqueeze(3)
                                       .broadcast_to([P, NK, XH, XD]), ALU.mult), "av0")
                for c in range(NC):
                    if c == 1:
                        dve.wait_ge(sem["av"], total("av", i, 1))
                    count_in(dve.tensor_reduce(actx[:, c, :].rearrange("p (h d) -> p h d", h=XH),
                                             av[:, c, :, :, :].rearrange("p k h d -> p h d k"),
                                             AX.X, ALU.add),
                           "actx")
                yield
                yield
                bank = wait_filled(Bk, dve, i, "xout")
                dve.tensor_tensor(xr2[:, :, :], bank[:, :].rearrange("p (c d) -> p c d", c=NC),
                                  x1[:, :, :], ALU.add).then_inc(was_read(Bk, "xout"), 1)
                wait_read(Bk, dve, i, "xout")
                link(dve.tensor_tensor(xr2[:, :, :], xr2[:, :, :],
                                       xb_sb[:, 2, :].unsqueeze(1).broadcast_to([P, NC, D]),
                                       ALU.add), "var2")
                at_least(dve, sem["x2_out"], total("x2_out", i, 0))
                at_least(dve, sem["scatter"], total("scatter", i, 0))
                layer_norm(i, xr2, x2, bns2, mv2, ve2, rstd2, "var2", "rstd2", "x2")
                yield
                yield
                bank = wait_filled(Bk, dve, i, "route")
                logits = bank[:, 0:NC * E].rearrange("p (c e) -> p c e", c=NC)
                link(dve.tensor_reduce(prm[:, :], logits, AX.X, ALU.max), "rmax")

                def over_e(ap):
                    return ap.unsqueeze(2).broadcast_to([P, NC, E])

                dve.tensor_tensor(prd[:, :, :], logits, over_e(prm[:, :]), ALU.subtract)\
                    .then_inc(was_read(Bk, "route"), 1)
                dve.wait_ge(sem["rexp"], total("rexp", i, 1))
                link(dve.tensor_reduce(prm[:, :], prx[:, :, :], AX.X, ALU.add), "top")
                link(dve.reciprocal(prm[:, :], prm[:, :]), "top")
                link(dve.tensor_tensor(pr[:, :, :], prx[:, :, :], over_e(prm[:, :]), ALU.mult),
                     "top")
                dve.nop(nofuse=True)
                count_in(dve.max(top[:, 0, :], pr[:, 0, :]), "top")
                link(dve.max(top[:, 1, :], pr[:, 1, :]), "top")
                dve.nop(nofuse=True)
                count_in(dve.max_index(topi[:, 0, :], top[:, 0, :], pr[:, 0, :]), "top")
                link(dve.max_index(topi[:, 1, :], top[:, 1, :], pr[:, 1, :]), "top")
                link(dve.tensor_copy(topf[:, :, :], topi[:, :, :]), "top")
                link(dve.tensor_tensor(gsum[:, :], top[:, :, 0], top[:, :, 1], ALU.add), "top")
                link(dve.reciprocal(gsum[:, :], gsum[:, :]), "top")
                at_least(dve, sem["gate_out"], total("gate_out", i, 0))
                link(dve.tensor_tensor(gate[:, :, :], top[:, :, 0:TOPK],
                                       gsum[:, :].unsqueeze(2).broadcast_to([P, NC, TOPK]),
                                       ALU.mult), "top")
                ids = eids[:, :].unsqueeze(1).broadcast_to([P, TOPK, E])
                for c in range(NC):
                    dve.tensor_tensor(oh[:, c, :, :], ids, topf[:, c, 0:TOPK].unsqueeze(2)
                                      .broadcast_to([P, TOPK, E]), ALU.is_equal)
                link(dve.memset(junk[:, :], 0.0), "ohs")
                link(dve.tensor_tensor(ohs[:, :, :], oh[:, :, 0, :], oh[:, :, 1, :], ALU.add), "ohs")
                yield
                bank = wait_filled(Bk, dve, i, "pos")
                dve.tensor_copy(pos[:, :, :], bank[:, 0:NC * E].rearrange("p (c e) -> p c e", c=NC))\
                    .then_inc(was_read(Bk, "pos"), 1)
                for c in range(NC):
                    link(dve.tensor_tensor(count[:, :], count[:, :], ohs[:, c, :], ALU.add), "count")
                wait_read(Bk, dve, i, "pos")
                for c in range(NC):
                    count_in(dve.tensor_tensor(psel[:, c, :, :], oh[:, c, :, :],
                                             pos[:, c, :].unsqueeze(1).broadcast_to([P, TOPK, E]),
                                             ALU.mult), "slots")
                    link(dve.tensor_tensor(esel[:, c, :, :], oh[:, c, :, :], ids, ALU.mult), "slots")
                count_in(dve.tensor_reduce(pk[:, :, :], psel[:, :, :, :], AX.X, ALU.add), "slots")
                link(dve.tensor_reduce(ek[:, :, :], esel[:, :, :, :], AX.X, ALU.add), "slots")
                link(dve.tensor_scalar(drop[:, :, :], pk[:, :, :], float(CAP), None, ALU.is_ge),
                     "slots")
                link(dve.tensor_scalar(pk[:, :, :], pk[:, :, :], float(CAP - 1), None, ALU.min),
                     "slots")
                link(dve.scalar_tensor_tensor(gslot[:, :, :], ek[:, :, :], float(CAP), pk[:, :, :],
                                              ALU.mult, ALU.add), "slots")
                link(dve.scalar_tensor_tensor(sslot[:, :, :], drop[:, :, :], float(E * CAP),
                                              gslot[:, :, :], ALU.mult, ALU.add), "slots")
                at_least(dve, sem["slot_out"], total("slot_out", i, 0))
                dve.tensor_scalar(ek[:, :, :], drop[:, :, :], -1.0, 1.0, ALU.mult, ALU.add)
                dve.tensor_copy(gslot_i[:, :], gslot[:, :, :].rearrange("p c k -> p (c k)"))
                link(dve.tensor_copy(sslot_i[:, :], sslot[:, :, :].rearrange("p c k -> p (c k)")),
                     "slots")
                link(dve.tensor_tensor(gate[:, :, :], gate[:, :, :], ek[:, :, :], ALU.mult), "slots")
                end(names)
                yield

            def score(i, k):
                dve.wait_ge(sem["prod"], total("prod", i, k + 1))
                count_in(dve.tensor_reduce(sc[:, :, k, :], prod[k % 2][:, :, :, :], AX.X, ALU.add),
                       "scr")

            def stage_c(e, pair, j):
                dve.wait_ge(sem[f"be_in{j}"], (pair + 1) * PER["be_in0"])
                at_least(dve, sem["y_out"], pair * 2 * PER["y_out"])
                for n in range(NT // 2):
                    bank = wait_filled(C, dve, e, f"y{n}")
                    dve.tensor_tensor(ye[j][:, 2 * n:2 * n + 2, :],
                                      bank[:, :].rearrange("p (t d) -> p t d", t=2),
                                      b2_sb[j][:, :].unsqueeze(1).broadcast_to([P, 2, D]),
                                      ALU.add).then_inc(was_read(C, f"y{n}"), 1)

            def stage_d(i, pair, j):
                names = ("mix", "fvar", "fo")
                begin(i, names)
                dve.wait_ge(sem[f"f_in{j}"], total("f_in0", pair, PER["f_in0"]))
                dve.wait_ge(sem[f"row_in{j}"], total("row_in0", pair, PER["row_in0"]))
                for c in range(NC):
                    count_in(dve.scalar_tensor_tensor(fy[j][:, c, :], frow[j][:, c, 0, :],
                                                    fgate[j][:, 2 * c:2 * c + 1], fx[j][:, c, :],
                                                    ALU.mult, ALU.add), "mix")
                for c in range(NC):
                    own("mix", c + 1)
                    count_in(dve.scalar_tensor_tensor(fy[j][:, c, :], frow[j][:, c, 1, :],
                                                    fgate[j][:, 2 * c + 1:2 * c + 2],
                                                    fy[j][:, c, :], ALU.mult, ALU.add), "mix")
                own("mix", 4)
                at_least(dve, sem["out_done"], pair * 2 * PER["out_done"])
                layer_norm(i, fy[j], fo[j], fbn[j], fmv[j], fve[j], frs[j], "fvar", "frs", "fo")
                end(names)

            dve.wait_ge(consts_in, CONSTS)
            dve.wait_ge(zeroed, ZEROED)
            dve.tensor_scalar(convw_sb[:, :, :, :], convw_sb[:, :, :, :], 0.5, None, ALU.mult)\
                .then_inc(prepared, 1)
            dve.tensor_scalar(wo_sb[:, :, :], wo_sb[:, :, :], onorm_sb[:, :], None, ALU.mult)\
                .then_inc(prepared, 1)
            dve.tensor_scalar(xb_sb[:, 1, :], xb_sb[:, 1, :], 0.5, None, ALU.mult)\
                .then_inc(prepared, 1)
            dve.tensor_tensor(offc_sb[:, :], offb_sb[:, :], refp_sb[:, :], ALU.add)\
                .then_inc(prepared, 1)
            dve.wait_ge(prepared, PREPARED)
            run(("A", stage_a(0)))
            run(("A", stage_a(1)), ("B", stage_b(0)))
            with dve.Fori(1, B - 1) as i:
                run(("A", stage_a(i + 1)), ("B", stage_b(i)))
            run(("B", stage_b(B - 1)))
            for j in range(2):
                stage_c(j, 0, j)
            with dve.Fori(1, E // 2) as pair:
                for j in range(2):
                    stage_c(pair * 2 + j, pair, j)
            for j in range(2):
                stage_d(j, 0, j)
            with dve.Fori(1, B // 2) as pair:
                for j in range(2):
                    stage_d(pair * 2 + j, pair, j)

        @block.gpsimd
        def _(pool):
            def rsqrt(dst, src, shape, name):
                n = 1
                for d in shape:
                    n *= d
                h = half_m[:, 0:n]
                if len(shape) == 2:
                    h = h.rearrange("p (a b) -> p a b", a=shape[0])
                pool.tensor_tensor(dst, src, h, ALU.pow).then_inc(sem[name], 1)

            def stage_a(i):
                for n, t in ((1, 1), (3, 0)):
                    pool.wait_ge(sem["silu"], total("silu", i, n))
                    pool.tensor_tensor(sq[:, t, :, :], qk[:, t, :, :], qk[:, t, :, :], ALU.mult)\
                        .then_inc(sem["sq"], 1)
                yield
                wait_read(A, pool, i, "sums")
                pool.nop(nofuse=True)
                pool.tensor_scalar(sums[:, 0:16], sums[:, 0:16], 1e-6, None, ALU.add)\
                    .then_inc(sem["rinv"], 1)
                pool.wait_ge(sem["rinv"], total("rinv", i, 1))
                rsqrt(rinv[:, :, :, :].rearrange("p c t h -> p (c t h)"), sums[:, 0:16], [16],
                      "rinv")
                yield
                pool.wait_ge(sem["beta"], total("beta", i, 2))
                wait_read(A, pool, i, "v_tok")
                pool.tensor_tensor(split(vb[:, :, :]), split(vt[:, :, :]), heads(beta[:, :, :]),
                                   ALU.mult).then_inc(sem["vb"], 1)
                wait_read(A, pool, i, "k_tok")
                pool.tensor_tensor(kb[:, :].rearrange("p (h d) -> p h d", h=H),
                                   kn[:, 1, :].rearrange("p (h d) -> p h d", h=H),
                                   beta[:, 1, :].unsqueeze(2).broadcast_to([P, H, HD]),
                                   ALU.mult).then_inc(sem["kb"], 1)
                yield
                for c in range(NC):
                    wait_read(A, pool, i, f"gram{c}")
                    pool.tensor_tensor(X8[c][:, :, :], nbG[c][:, :, :], mask4(M_DIAG8), ALU.mult)\
                        .then_inc(sem["x8"], 1)
                for _ in range(len(INVERSE) + 8):
                    yield
                pool.wait_ge(sem["fuse"], total("fuse", i, 5))
                pool.tensor_tensor(split(o3[:, :, :]), split(vt[:, :, :]),
                                   heads(wts[:, :, 2].rearrange("p (c h) -> p c h", c=NC)),
                                   ALU.mult).then_inc(sem["v3"], 1)
                pool.wait_ge(sem["osum"], total("osum", i, 2))
                pool.tensor_tensor(o2[:, :, :], o1[:, :, :], o1[:, :, :], ALU.mult)\
                    .then_inc(sem["osq"], 1)
                pool.wait_ge(sem["orms"], total("orms", i, 2))
                rsqrt(rrms[:, :], rms[:, :], [8], "orr")
                yield
                yield
                pool.wait_ge(sem["var1"], total("var1", i, 4))
                rsqrt(rstd[:, :], ve[:, :], [2], "rstd1")
                yield

            def stage_b(i):
                for _ in range(6):
                    yield
                wait_read(Bk, pool, i, "Qt")
                for k in range(NK):
                    yield
                    for c in range(NC):
                        wait_read(G, pool, i, f"gather{k}_{c}")
                    at_least(pool, sem["scr"], total("scr", i, max(0, k - 1)))
                    pool.tensor_tensor(prod[k % 2][:, :, :, :], gs[:, :, k, :, 0, :],
                                       split(Qs[:, :, :], XH), ALU.mult).then_inc(sem["prod"], 1)
                    yield
                pool.wait_ge(sem["att"], total("att", i, 3))
                pool.tensor_tensor(av[:, 1, :, :, :], gs[:, 1, :, :, 1, :],
                                   sce[:, 1, :, :].unsqueeze(3).broadcast_to([P, NK, XH, XD]),
                                   ALU.mult).then_inc(sem["av"], 1)
                yield
                yield
                pool.wait_ge(sem["var2"], total("var2", i, 5))
                rsqrt(rstd2[:, :], ve2[:, :], [2], "rstd2")
                yield
                yield
                yield
                pool.wait_ge(sem["slots"], total("slots", i, PER["slots"]))
                pool.nop(nofuse=True)
                for c in range(NC):
                    for k in range(TOPK):
                        n = c * TOPK + k
                        pool.indirect_dma_start(
                            out=xe_dram, out_offset=bass.IndirectOffsetOnAxis(
                                ap=sslot_i[:, n:n + 1], axis=0),
                            in_=x2[:, c, :], in_offset=None, bounds_check=E * CAP - 1,
                            oob_is_err=False).then_inc(sem["scatter"], 16)
                yield

            def stage_d(pair, j):
                pool.wait_ge(sem[f"f_in{j}"], total("f_in0", pair, PER["f_in0"]))
                pool.nop(nofuse=True)
                for c in range(NC):
                    for k in range(TOPK):
                        n = c * TOPK + k
                        pool.indirect_dma_start(
                            out=frow[j][:, c, k, :], out_offset=None, in_=ye_dram,
                            in_offset=bass.IndirectOffsetOnAxis(ap=fslot[j][:, n:n + 1], axis=0))\
                            .then_inc(sem[f"row_in{j}"], 16)

            def norm_d(i, j):
                pool.wait_ge(sem["fvar"], total("fvar", i, 4))
                rsqrt(frs[j][:, :], fve[j][:, :], [2], "frs")

            for n, (ap, value) in enumerate(
                    ((pre[:, :, :, 0:3], 0.0), (vpad[:, :, 0:PAD], 0.0), (zero, 0.0),
                     (kz[:, :, :, :], 0.0), (S_sb[:, :, :], 0.0),
                     (half_m[:, :], -0.5), (count[:, :], 0.0), (ixp[96:97, :, :], 1.0))):
                pool.memset(ap, value).then_inc(zeroed, 1)
                pool.wait_ge(zeroed, n + 1)
            for n in range(3):
                pool.dma_start(xe_dram[bass.ts(n, E * CAP // 3), :]
                               .rearrange("(p t) d -> p (t d)", p=P), zero).then_inc(xe_zero, 16)
            pool.wait_ge(xe_zero, 48)
            pool.wait_ge(consts_in, CONSTS)
            run(("A", stage_a(0)))
            run(("A", stage_a(1)), ("B", stage_b(0)))
            with pool.Fori(1, B - 1) as i:
                run(("A", stage_a(i + 1)), ("B", stage_b(i)))
            run(("B", stage_b(B - 1)))
            pool.wait_ge(sem["y_out"], E * PER["y_out"])
            stage_d(0, 0)
            with pool.Fori(0, B // 2 - 1) as pair:
                i = pair * 2
                stage_d(pair, 1)
                norm_d(i, 0)
                pool.wait_ge(sem["fo"], total("fo", i, PER["fo"]))
                stage_d(pair + 1, 0)
                norm_d(i + 1, 1)
                pool.wait_ge(sem["fo"], total("fo", i + 1, PER["fo"]))
            stage_d(B // 2 - 1, 1)
            norm_d(B - 2, 0)
            norm_d(B - 1, 1)


def kernel(**inputs):
    import numpy as np
    import concourse.bacc as bacc
    from concourse.bass_utils import run_bass_kernel_spmd

    a = {k: np.asarray(v) for k, v in inputs.items()}

    def rows(w, k):
        return w.reshape(k, P, -1).transpose(1, 0, 2)

    x = a["x"]
    r, c = np.arange(P)[:, None], np.arange(P)[None, :]
    below = r > c
    diag8 = below & (r // 8 == c // 8)
    in32 = below & (r // 32 == c // 32) & ~diag8
    in128 = below & ~(r // 32 == c // 32)
    table = [diag8, in32, in128, diag8.T, in32.T, in128.T, r <= c, r == c, r < c, r + c >= 0]
    masks = np.stack(table, 1).astype(np.float32)
    kmw = a["L0_attn_kernel_mix_w"]
    kmix = np.zeros((6, P, P), np.float32)
    for row in range(0, 3 * D, HD):
        head, at = divmod(row, 3 * HD)
        j, p = divmod(row, P)
        kmix[j, p:p + HD, (head % 2) * HD:(head % 2 + 1) * HD] = kmw[at:at + HD]
    woff = a["L0_xattn_Woff"].reshape(XH, NK, D).transpose(1, 0, 2).reshape(NK * XH, D)
    boff = a["L0_xattn_boff"].reshape(XH, NK).T.reshape(NK * XH)
    wo3 = np.zeros((3, 96, D), np.float32)
    bo3 = np.zeros((3, 96), np.float32)
    ref3 = np.zeros((3, 96), np.float32)
    for g in range(3):
        for part in range(3):
            n = min(32, NK * XH - 32 * g)
            wo3[g, part * 32:part * 32 + n] = woff[32 * g:32 * g + n]
            bo3[g, part * 32:part * 32 + n] = boff[32 * g:32 * g + n]
            ref3[g, part * 32:part * 32 + n] = (np.arange(32 * g, 32 * g + n) // XH) - (NK + 1) // 2
    import ml_dtypes
    selector = np.zeros((97, 32, S2), ml_dtypes.bfloat16)
    for p in range(96):
        selector[p, p % 32, :] = 1
    selector[96, :, :] = -np.arange(S2)
    headsel = (r[:, 0:1] // HD == np.arange(2)[None, :]).astype(np.float32)
    arrays = dict(
        x_tok=x.reshape(B, NC, P, D).transpose(0, 2, 1, 3),
        xT=x.transpose(0, 2, 1).reshape(B, 2, P, T).transpose(0, 2, 1, 3),
        ctxT=a["ctx_1024"].transpose(0, 2, 1).reshape(B, 2, P, S2).transpose(0, 2, 1, 3),
        mask=a["mask_BxS2_if0"],
        wqkv=np.stack([rows(a[f"L0_attn_W{n}"], 2) for n in "qkv"], 1),
        wb=rows(a["L0_attn_Wb"], 2),
        convw=np.stack([rows(a[f"L0_attn_conv_{n}_w"], 2) for n in "qkv"], 1),
        msw3=rows(a["L0_attn_ms_w3"], 2), msw15=rows(a["L0_attn_ms_w15"], 2),
        msw31=rows(a["L0_attn_ms_w31"], 2),
        kmix=kmix.transpose(1, 0, 2), cmix=rows(a["L0_attn_channel_mixer_w"], 2),
        fw1=rows(a["L0_attn_fusion_w1"][:D], 2), fw1s=a["L0_attn_fusion_w1"][D:],
        fb1=a["L0_attn_fusion_b1"].reshape(4, P).T, fw2=rows(a["L0_attn_fusion_w2"], 4),
        fb2=a["L0_attn_fusion_b2"], onorm=a["L0_attn_o_norm_w"].reshape(HD, 1),
        wo=rows(a["L0_attn_Wo"], 2),
        xwT=np.stack([rows(a[f"L0_xattn_W{n}"].T, 2) for n in "kvqo"], 1),
        xbias=np.stack([a[f"L0_xattn_b{n}"] for n in "kvo"]), xbq=a["L0_xattn_bq"].reshape(2, P).T,
        woff=np.stack([rows(np.ascontiguousarray(wo3[g].T), 2) for g in range(3)], 2),
        boff=bo3.T, ref_pos=ref3.T, wr=rows(a["L0_ffn_w_router"], 2),
        w1=a["L0_ffn_w1"].reshape(E, 2, P, HID).transpose(0, 2, 1, 3),
        b1=a["L0_ffn_b1"].reshape(E, HID // P, P).transpose(0, 2, 1),
        w2=a["L0_ffn_w2"].reshape(E, HID // P, P, D).transpose(0, 2, 1, 3),
        b2=a["L0_ffn_b2"], masks=masks, headsel=headsel, selector=selector,
        positions=np.arange(T, dtype=np.float32), expert_ids=np.arange(E, dtype=np.float32),
    )
    nc = bacc.Bacc("TRN2", target_bir_lowering=False, num_devices=1)
    args = {}
    arrays = {f"in_{n}": np.ascontiguousarray(v) for n, v in arrays.items()}
    for name, v in arrays.items():
        args[name[3:]] = nc.dram_tensor(name, v.shape, mybir.dt.from_np(v.dtype),
                                    kind="ExternalInput").ap()
    args["msw"] = [args.pop(f"msw{t}") for t in TAPS]
    out = nc.dram_tensor("out", (B, P, NC, D), mybir.dt.float32, kind="ExternalOutput").ap()
    decoder_layer(nc, out=out, **args)
    r = run_bass_kernel_spmd(nc, [arrays], core_ids=[0])
    got = r.results[0]["out"]
    return np.ascontiguousarray(got.transpose(0, 2, 1, 3).reshape(B, T, D))
```

```python
from contextlib import ExitStack

import concourse.bass as bass
from concourse import mybir

P = 128
B, T, D = 8, 256, 256
NC = T // P
H, HD = 4, 64
S2 = 120
XH, XD, NK = 16, 16, 5
E, TOPK, HID = 8, 2, 1024
CAP = int(1.5 * 4 * 512 * TOPK / E)
NT = CAP // P
EPS = 1e-5
TAPS = (3, 15, 31)
PAD = max(TAPS) - 1

(M_DIAG8, M_DIAG8T, M_IN32T, M_IN128T, M_INCL, M_EYE, M_BEFORE, M_ONES) = range(8)
NMASK = 8
ROUND = 1.5 * 2.0 ** 23
ZEROED, PREPARED = 8, 4
ZERO_DMAS = 6
TAP_ORDER = [(tap, s, hf) for tap in range(max(TAPS)) for s in range(3) for hf in range(2)
             if tap < TAPS[s]]
TAP_AT = {tap: n for n, tap in enumerate(TAP_ORDER)}

INVERSE = ["gram", "gramT", "P2", "P2T", "P4", "T2T", "T8T", "T8", "W", "WT", "W2", "U", "T32T",
           "T32", "Y", "YT", "Y2", "V", "TT", "aT"]
F_USES = ["k_proj", "v_proj", "q_proj"]
A_USES = (["sums", "k_tok", "v_tok", "k_chan"]
          + [f"{s}{c}" for s in INVERSE for c in range(NC)]
          + ["u0", "wT1", "S0", "o0", "u1", "o1"]
          + ["mix", "ms", "statT", "hid0", "hid1", "logit", "oT", "attn"])
B_USES = (["x1T", "Qc", "off", "Kt", "Vt", "Qt"]
          + [f"dist{k}{half}_{j}" for k in range(NK) for half in range(2) for j in range(XH // 4)])
R_USES = ["ctxT", "xout", "x2T", "route", "pos"]
G_USES = [f"gather{k}_{c}" for k in range(NK) for c in range(NC)]
X_USES = [f"xeT{j}" for j in range(NT // 2)]
C_USES = ([f"h{m}{a}" for m in range(HID // P) for a in "ab"]
          + [f"y{j}" for j in range(NT // 2)])

PER = dict(
    xT_in=16, xTf_in=16, xt_in=16, conv=24, tanh=3, silu=3, sq=2, rinv=2, beta_th=1, beta=2,
    vb=1, kb=1, x8=2, t1=4, xm=4, taps=98, stat=3, fuse=6, wexp=1, v3=1, osum=2, osq=1, orms=2,
    orr=1, on=1, var1=4, rstd1=1, x1=2,
    ctx_in=16, mask_in=16, length=4, loc=8, parts=5, ixp_in=144, nhat=10, hats_used=5, prod=5,
    scr=4, scr_last=1, scs=2, sexp=1, att=3, av=1, av0=1, actx=2, var2=4, rstd2=1, x2=2, rmax=1,
    rexp=1, top=11, ohs=2, count=2, slots=12, res=1, x2_out=16, slot_out=16, gate_out=16,
    scatter=64,
    w1_parts=2, w2_hi=1, w2_parts=1, x_hi=3, h_parts=16, w_in0=32, w_in1=32, be_in0=32,
    be_in1=32, xe_in0=16, xe_in1=16, y_out=16,
    mix=4, fvar=4, frs=1, fo=2,
)
DB = 4
for j in range(DB):
    PER[f"f_in{j}"], PER[f"row_in{j}"], PER[f"out_done{j}"] = 48, 64, 16


LATE = ["u0", "S0", "u1", "o1", "mix", "ms", "statT", "hid", "logit", "fuse", "gate", "rms", "oT",
        "attn", "norm"]
SEGMENTS = dict(
    A=["sums", "k_tok", "k_chan"] + INVERSE + LATE,
    B=(["x1T", "Qc", "off", "tables", "Qt", "first0", "first1"]
       + [f"{part}{k}{half}" for k in range(NK - 1) for half in range(2)
          for part in ("gather", "dist", "hats")]),
    R=["gather0", "gather1", "last", "max", "exp", "ctx", "ctxT", "xout", "norm", "x2T", "route",
       "top", "pos", "slots"],
    F=[name + part for name in "kvq" for part in ("", "_conv", "_act")],
)
TAPS_AT = [3, 3, 3, 5, 3, 4, 4, 4, 4, 3, 4, 4, 5, 2, 4, 9, 4, 4, 4, 6, 2, 4, 0, 3, 4, 4]
SEGMENTS["T"] = list(range(len(TAPS_AT)))
LAST = len(SEGMENTS["A"])
BESIDE = dict(
    A=range(LAST), T=range(len(TAPS_AT)),
    B=[0, 1, 2, 4, 6, 7, 8, 9, 10, 12, 12, 13, 14, 16, 17, 18, 19, 20, 21, 25, 26, 27, 27, 27,
       28, 30, 32, 33, 34, 34, 35],
    R=[2, 3, 4, 6, 6, 6, 8, 9, 10, 11, 12, 13, 15, 17],
    F=[22, 23, 25, 25, 26, 26, 28, 28, 29],
)


def order(names):
    return [(name, segment) for n in range(LAST) for name in "ABRFT" if name in names
            for at, segment in zip(BESIDE[name], SEGMENTS[name]) if at == n]


def run(**stages):
    ahead = {name: next(stages[name]) for name in stages}
    for name, segment in order(list(stages)):
        if name in stages and ahead[name] == segment:
            ahead[name] = next(stages[name], None)
    assert all(ahead[name] is None for name in stages), ahead


def at_least(eng, semaphore, value):
    if not (isinstance(value, int) and value <= 0):
        eng.wait_ge(semaphore, value)


def total(name, i, k):
    return i * PER[name] + k


def bank_ring(ctx, nc, name, uses, banks):
    return dict(
        use={u: n for n, u in enumerate(uses)}, uses=len(uses), banks=banks,
        filled=ctx.enter_context(nc.semaphore(f"{name}_filled")),
        read=[ctx.enter_context(nc.semaphore(f"{name}_read{b}")) for b in range(len(banks))],
        per=[len(range(b, len(uses), len(banks))) for b in range(len(banks))])


def place(ring, use):
    return ring["use"][use] % len(ring["banks"]), ring["use"][use] // len(ring["banks"])


def bank_of(ring, use):
    return ring["banks"][place(ring, use)[0]]


def was_read(ring, use):
    return ring["read"][place(ring, use)[0]]


def wait_read(ring, eng, i, *uses):
    last = {}
    for b, n in [place(ring, u) for u in uses]:
        last[b] = max(n, last[b]) if b in last else n
    for b in last:
        eng.wait_ge(ring["read"][b], i * ring["per"][b] + last[b] + 1)


def take(ring, pe, i, use, *after):
    b, n = place(ring, use)
    at_least(pe, ring["read"][b], i * ring["per"][b] + n)
    wait_read(ring, pe, i, *[u for u in after if place(ring, u)[0] != b])
    return ring["banks"][b]


def wait_filled(ring, eng, i, use):
    eng.wait_ge(ring["filled"], i * ring["uses"] + ring["use"][use] + 1)
    return bank_of(ring, use)


def wait_filled_before(ring, eng, i):
    at_least(eng, ring["filled"], i * ring["uses"])


def decoder_layer(nc, x_tok, xT, ctxT, mask, wqkv, wb, convw, msw, kmix, cmix, fw1, fw1s, fb1, fw2,
                  fb2, onorm, wo, xwT, xbias, xbq, woff, boff, ref_pos, wr, w1, b1, w2, b2, masks,
                  headsel, selector, positions, expert_ids, out):
    f32, bf16, u32 = mybir.dt.float32, mybir.dt.bfloat16, mybir.dt.uint32
    i32, f32r = mybir.dt.int32, mybir.dt.float32r
    ALU, ACT, AX = mybir.AluOpType, mybir.ActivationFunctionType, mybir.AxisListType

    x2_dram = nc.dram_tensor("x2_rows", (B, P, NC, D), f32).ap()
    slot_dram = nc.dram_tensor("slots", (B, P, NC * TOPK), u32).ap()
    gate_dram = nc.dram_tensor("gates", (B, P, NC * TOPK), f32).ap()
    xe_dram = nc.dram_tensor("expert_in", (E * CAP, D), f32).ap()
    ye_dram = nc.dram_tensor("expert_out", (E * CAP, D), f32).ap()

    ctx = ExitStack()
    with ctx:
        phase1 = ExitStack()

        def keep(name, shape, dt=f32):
            return ctx.enter_context(nc.sbuf_tensor(name, shape, dt))

        def sb(name, shape, dt=f32):
            return phase1.enter_context(nc.sbuf_tensor(name, shape, dt))

        sem = {n: ctx.enter_context(nc.semaphore(n)) for n in PER}
        first_in = ctx.enter_context(nc.semaphore("first_in"))
        early_in = ctx.enter_context(nc.semaphore("early_in"))
        consts_in = ctx.enter_context(nc.semaphore("consts_in"))
        zeroed = ctx.enter_context(nc.semaphore("zeroed"))
        xe_zero = ctx.enter_context(nc.semaphore("xe_zero"))
        prepared = ctx.enter_context(nc.semaphore("prepared"))

        psum = [ctx.enter_context(nc.psum_tensor(f"bank{b}", [P, 512], f32)) for b in range(8)]
        F = bank_ring(ctx, nc, "F", F_USES, psum[3:4])
        A = bank_ring(ctx, nc, "A", A_USES, psum[0:3])
        R = bank_ring(ctx, nc, "R", R_USES, psum[3:4])
        Bk = bank_ring(ctx, nc, "B", B_USES, psum[4:6])
        G = bank_ring(ctx, nc, "G", G_USES, psum[6:8])
        C = bank_ring(ctx, nc, "C", C_USES, psum[0:5])
        X = bank_ring(ctx, nc, "X", X_USES, psum[5:8])

        mk = keep("masks", [P, NMASK, P])
        half_m = keep("minus_half", [P, 16])
        wqkv_sb = sb("wqkv", [P, 3, 2, D])
        wb_sb = sb("wb", [P, 2, H])
        convw_sb = sb("convw", [P, 3, 2, 4])
        msw_sb = [sb(f"msw{s}", [P, 2, TAPS[s]]) for s in range(3)]
        kmix_sb = sb("kmix", [P, 6, P])
        cmix_sb = sb("cmix", [P, 2, D])
        fw1_sb = sb("fw1", [P, 2, 2 * D])
        fw1s_sb = sb("fw1s", [3 * H, 2 * D])
        fb1_sb = sb("fb1", [P, 4])
        fw2_sb = sb("fw2", [P, 4, 3 * H])
        fb2_sb = sb("fb2", [P, 3 * H])
        onorm_sb = sb("onorm", [P, 1])
        wo_sb = sb("wo", [P, 2, D])
        headsel_sb = sb("headsel", [P, 2])

        xT_sb = sb("xT", [P, 2, T])
        xTf_sb = sb("xT_fusion", [P, 2, T])
        xt_sb = sb("x_tok", [P, NC, D])
        pre = sb("pre", [P, 3, 2, 3 + T])
        y = sb("y", [P, 3, 2, T])
        th = sb("th", [P, 3, 2, T])
        qk = sb("qk", [P, 2, 2, T])
        vpad = sb("vpad", [P, 2, PAD + T])
        sq = th
        sums = sb("sums", [P, 24])
        rinv = sb("rinv", [P, NC, 2, H])
        bth = sb("bth", [P, NC, H])
        beta = sb("beta", [P, NC, H])
        nbeta = sb("nbeta", [P, NC, H])
        kn = sb("kn", [P, NC, D])
        vt = sb("vt", [P, NC, D])
        vb = sb("vb", [P, NC, D])
        kb = sb("kb", [P, D])
        kz = sb("kz", [P, 2, 2, T])
        XT = [[sb(f"XT{s}_{c}", [P, H, P]) for s in range(3)] for c in range(NC)]
        W = [[sb(f"W{s}_{c}", [P, H, P]) for s in range(3)] for c in range(NC)]
        Ta = [sb(f"Ta{c}", [P, H, P]) for c in range(NC)]
        Tb = [sb(f"Tb{c}", [P, H, P]) for c in range(NC)]
        Tn = [sb(f"Tn{c}", [P, H, P]) for c in range(NC)]
        nbG = [W[c][2] for c in range(NC)]
        X8 = Tb
        aT = Tn
        u_sb = [sb(f"u{c}", [P, D]) for c in range(NC)]
        wTn = sb("wTn", [P, 2, P])
        S_sb = sb("S", [P, H, HD])
        delta = sb("delta", [P, NC, D])
        acc = sb("acc", [P, 3, 2, T])
        y1 = W[0][0][:, :, :].rearrange("p (a h) t -> p a (h t)", a=2)
        ms = sb("ms", [P, NC, D])
        st = sb("st", [P, NC, 3 * H])
        gst = sb("gst", [3 * H, T])
        hdn = [W[n][1][:, :, :].rearrange("p (a h) t -> p a (h t)", a=2) for n in range(2)]
        lg = sb("lg", [P, NC * H, 3])
        lmx = sb("lmx", [P, NC * H])
        lex = sb("lex", [P, NC * H, 3])
        wts = sb("wts", [P, NC * H, 3])
        o1 = sb("o1", [P, NC, D])
        o2 = sb("o2", [P, NC, D])
        o3 = sb("o3", [P, NC, D])
        rms = sb("rms", [P, NC * H])
        rrms = sb("rrms", [P, NC * H])
        oT = W[1][0][:, :, :].rearrange("p (a h) t -> p a (h t)", a=2)
        bns = sb("bns", [P, NC, 6])
        mv = sb("mv", [P, NC, 2])
        ve = sb("ve", [P, NC])
        rstd = sb("rstd", [P, NC])
        xr = o3
        x1 = sb("x1", [P, NC, D])

        xwT_sb = sb("xwT", [P, 4, 2, D])
        bq_sb = sb("bq", [P, 2])
        xb_sb = sb("xb", [P, 3, D])
        woff_sb = sb("woff", [P, 2, 96])
        offb_sb = sb("offb", [96, 1])
        refp_sb = sb("refp", [96, 1])
        offc_sb = sb("offc", [96, 1])
        wr_sb = sb("wr", [P, 2, E])
        sel_sb = sb("sel", [97, 32, S2], bf16)
        posq = sb("posq", [96, T])
        eids = sb("eids", [P, E])

        ctxT_sb = sb("ctxT", [P, 2, S2])
        mask_sb = sb("mask", [96, S2], i32)
        maskf = sb("maskf", [96, S2])
        msum = sb("msum", [96, 1])
        Lb = sb("L", [96, 1])
        rL = sb("rL", [96, 1])
        x1T = sb("x1T", [P, 2, T])
        QT = sb("QT", [P, 2, T])
        Qs = sb("Qs", [P, NC, D])
        ixp = sb("ixp", [97, 3, T], bf16)
        tab = sb("tab", [S2, XH, 2, XD])
        nhat = [sb(f"nhat{j}", [S2, XH // 2, T]) for j in range(2)]
        loc_sb = sb("loc", [96, T])
        tmp_sb = sb("tmp", [96, T])
        loc, tmp = loc_sb[:, :], tmp_sb[:, :]
        parts = sb("parts", [96, 3, T], bf16)
        gs = sb("gs", [P, NC, 2 + NK, XH, XD])
        prod = [sb(f"prod{j}", [P, NC, XH, XD]) for j in range(2)]
        sc = sb("sc", [P, NC, NK, XH])
        scm = sb("scm", [P, NC, XH])
        scd = sb("scd", [P, NC, NK, XH])
        sce = sb("sce", [P, NC, NK, XH])
        av = gs[:, :, 2:, :, :]
        actx = sb("actx", [P, NC, D])
        res = sb("x1_bo", [P, NC, D])
        cT = sb("cT", [P, 2, T])
        bns2 = sb("bns2", [P, NC, 6])
        mv2 = sb("mv2", [P, NC, 2])
        ve2 = sb("ve2", [P, NC])
        rstd2 = sb("rstd2", [P, NC])
        xr2 = actx
        x2 = sb("x2", [P, NC, D])
        x2T = cT
        pr = sb("pr", [P, NC, E])
        prm = sb("prm", [P, NC])
        prd = sb("prd", [P, NC, E])
        prx = sb("prx", [P, NC, E])
        top = sb("top", [P, NC, E])
        topi = sb("topi", [P, NC, E], u32)
        topf = sb("topf", [P, NC, E])
        gsum = sb("gsum", [P, NC])
        oh = sb("oh", [P, NC, TOPK, E])
        ohs = sb("ohs", [P, NC, E])
        count = sb("count", [P, E])
        pos = sb("pos", [P, NC, E])
        psel = sb("psel", [P, NC, TOPK, E])
        esel = sb("esel", [P, NC, TOPK, E])
        pk = sb("pk", [P, NC, TOPK])
        ek = sb("ek", [P, NC, TOPK])
        drop = sb("drop", [P, NC, TOPK])
        gate = sb("gate", [P, NC, TOPK])
        gslot = sb("gslot", [P, NC, TOPK])
        sslot = sb("sslot", [P, NC, TOPK])
        gslot_i = sb("gslot_i", [P, NC * TOPK], u32)
        sslot_i = sb("sslot_i", [P, NC * TOPK], u32)
        zero = gs[:, :, :, :, :].rearrange("p a b c d -> p (a b c d)")
        zero = zero[:, 0:E * CAP * D // P // ZERO_DMAS]

        phase1.close()
        w1_sb = [keep(f"w1_{j}", [P, 2, HID]) for j in range(2)]
        w2_sb = [keep(f"w2_{j}", [P, HID // P, D]) for j in range(2)]
        w1_p = [keep(f"w1_part{n}", [P, 2, HID], f32r) for n in range(2)]
        w2_p = [keep(f"w2_part{n}", [P, HID // P, D], f32r) for n in range(2)]
        xeT_p = [keep(f"xeT_part{n}", [P, 2, CAP], f32r) for n in range(2)]
        hT_p = [keep(f"hT_part{n}", [P, HID // P, CAP], f32r) for n in range(2)]
        h_sb = [keep(f"h{n}", [P, CAP]) for n in range(2)]
        xe = [keep(f"xe{j}", [P, NT, D]) for j in range(2)]
        ye = [keep(f"ye{j}", [P, NT, D]) for j in range(2)]
        b1_sb = [keep(f"b1_{j}", [P, HID // P]) for j in range(2)]
        b2_sb = [keep(f"b2_{j}", [P, D]) for j in range(2)]
        fx = [keep(f"fx{j}", [P, NC, D]) for j in range(DB)]
        fslot = [keep(f"fslot{j}", [P, NC * TOPK], u32) for j in range(DB)]
        fgate = [keep(f"fgate{j}", [P, NC * TOPK]) for j in range(DB)]
        frow = [keep(f"frow{j}", [P, NC, TOPK, D]) for j in range(DB)]
        fy = [keep(f"fy{j}", [P, NC, D]) for j in range(DB)]
        fbn = [keep(f"fbn{j}", [P, NC, 6]) for j in range(DB)]
        fmv = [keep(f"fmv{j}", [P, NC, 2]) for j in range(DB)]
        fve = [keep(f"fve{j}", [P, NC]) for j in range(DB)]
        frs = [keep(f"frs{j}", [P, NC]) for j in range(DB)]
        fo = [keep(f"fo{j}", [P, NC, D]) for j in range(DB)]

        eye = mk[:, M_EYE, :]

        def mask4(m):
            return mk[:, m, :].unsqueeze(1).broadcast_to([P, H, P])

        def heads(ap, width=HD):
            return ap.unsqueeze(3).broadcast_to([P, NC, H, width])

        def split(ap, h=H):
            return ap.rearrange("p c (h d) -> p c h d", h=h)

        block = ctx.enter_context(nc.Block())

        first_loads = [(wqkv_sb[:, :, :, :], wqkv), (convw_sb[:, :, :, :], convw)]
        early_loads = [
            (mk[:, :, :], masks), (wb_sb[:, :, :], wb), (headsel_sb[:, :], headsel),
            (fb1_sb[:, :], fb1), (fb2_sb[:, :], fb2.partition_broadcast(P)),
            (onorm_sb[0:HD, :], onorm), (onorm_sb[HD:P, :], onorm), (wo_sb[:, :, :], wo),
        ] + [(msw_sb[s][:, :, :], msw[s]) for s in range(3)]
        loads = [
            (kmix_sb[:, :, :], kmix), (cmix_sb[:, :, :], cmix), (fw1_sb[:, :, :], fw1),
            (fw1s_sb[:, :], fw1s), (fw2_sb[:, :, :], fw2),
            (xwT_sb[:, :, :, :], xwT), (bq_sb[:, :], xbq),
            (xb_sb[:, :, :], xbias.partition_broadcast(P)), (wr_sb[:, :, :], wr),
            (sel_sb[:, :, :], selector), (posq[:, :], positions.partition_broadcast(96)),
            (eids[:, :], expert_ids.partition_broadcast(P)),
            (offb_sb[:, :], boff), (refp_sb[:, :], ref_pos), (woff_sb[:, :, :], woff),
        ]
        FIRST, EARLY = 16 * len(first_loads), 16 * len(early_loads)
        CONSTS = 16 * len(loads)

        @block.sync
        def _(sp):
            def f_load(i):
                at_least(sp, F["filled"], i * F["uses"])
                if not (isinstance(i, int) and i == 0):
                    wait_filled(A, sp, i - 1, "sums")
                sp.dma_start(xT_sb[:, :, :], xT[i, :, :, :]).then_inc(sem["xT_in"], 16)

            def a_loads(i):
                wait_filled_before(A, sp, i)
                sp.dma_start(xTf_sb[:, :, :], xT[i, :, :, :]).then_inc(sem["xTf_in"], 16)
                at_least(sp, sem["x1"], i * PER["x1"])
                sp.dma_start(xt_sb[:, :, :], x_tok[i, :, :, :]).then_inc(sem["xt_in"], 16)

            def spread_parts(i):
                wait_filled_before(Bk, sp, i)
                sp.wait_ge(sem["parts"], total("parts", i, PER["parts"]))
                for part in range(3):
                    for g in range(3):
                        sp.dma_start(ixp[bass.ts(part, 32), g, :], parts[bass.ts(g, 32), part, :])\
                            .then_inc(sem["ixp_in"], 16)

            def b_loads(i):
                if not (isinstance(i, int) and i == 0):
                    wait_filled(Bk, sp, i - 1, "Vt")
                sp.dma_start(ctxT_sb[:, :, :], ctxT[i, :, :, :]).then_inc(sem["ctx_in"], 16)
                at_least(sp, sem["parts"], i * PER["parts"])
                sp.dma_start(mask_sb[:, :], mask[i, :].partition_broadcast(96))\
                    .then_inc(sem["mask_in"], 16)

            def stores(i):
                sp.wait_ge(sem["x2"], total("x2", i, 2))
                sp.dma_start(x2_dram[i, :, :, :], x2[:, :, :]).then_inc(sem["x2_out"], 16)
                sp.wait_ge(sem["slots"], total("slots", i, PER["slots"]))
                sp.dma_start(slot_dram[i, :, :], gslot_i[:, :]).then_inc(sem["slot_out"], 16)
                sp.dma_start(gate_dram[i, :, :], gate[:, :, :].rearrange("p c k -> p (c k)"))\
                    .then_inc(sem["gate_out"], 16)

            def load_weights(e, j):
                sp.dma_start(w1_sb[j][:, :, :], w1[e, :, :, :]).then_inc(sem[f"w_in{j}"], 16)
                sp.dma_start(w2_sb[j][:, :, :], w2[e, :, :, :]).then_inc(sem[f"w_in{j}"], 16)

            def load_rows(e, j):
                sp.dma_start(b1_sb[j][:, :], b1[e, :, :]).then_inc(sem[f"be_in{j}"], 16)
                sp.dma_start(b2_sb[j][:, :], b2[e, :].partition_broadcast(P))\
                    .then_inc(sem[f"be_in{j}"], 16)
                sp.dma_start(xe[j][:, :, :],
                             xe_dram[bass.ts(e, CAP), :].rearrange("(t p) d -> p t d", p=P))\
                    .then_inc(sem[f"xe_in{j}"], 16)

            for dst, src in first_loads:
                sp.dma_start(dst, src).then_inc(first_in, 16)
            f_load(0)
            for dst, src in early_loads:
                sp.dma_start(dst, src).then_inc(early_in, 16)
            for dst, src in loads:
                sp.dma_start(dst, src).then_inc(consts_in, 16)
            a_loads(0)
            b_loads(0)
            f_load(1)
            a_loads(1)
            f_load(2)
            spread_parts(0)
            b_loads(1)
            a_loads(2)
            f_load(3)
            spread_parts(1)
            b_loads(2)
            stores(0)
            a_loads(3)
            with sp.Fori(2, B - 2) as i:
                f_load(i + 2)
                spread_parts(i)
                b_loads(i + 1)
                stores(i - 1)
                a_loads(i + 2)
            spread_parts(B - 2)
            b_loads(B - 1)
            stores(B - 3)
            sp.wait_ge(sem["x1"], B * PER["x1"])
            for j in range(2):
                load_weights(j, j)
            spread_parts(B - 1)
            stores(B - 2)
            stores(B - 1)
            sp.wait_ge(sem["scatter"], B * PER["scatter"])
            sp.wait_ge(sem["gate_out"], B * PER["gate_out"])
            sp.wait_ge(sem["slot_out"], B * PER["slot_out"])
            sp.wait_ge(sem["x2_out"], B * PER["x2_out"])
            for j in range(2):
                load_rows(j, j)

            def store_expert(e, j):
                wait_read(C, sp, e, C_USES[-1])
                sp.dma_start(ye_dram[bass.ts(e, CAP), :].rearrange("(t p) d -> p t d", p=P),
                             ye[j][:, :, :]).then_inc(sem["y_out"], 16)

            with sp.Fori(0, E // 2 - 1) as pair:
                for j in range(2):
                    e = pair * 2 + j
                    store_expert(e, j)
                    load_rows(e + 2, j)
                    load_weights(e + 2, j)

            def d_loads(i, j):
                sp.dma_start(fx[j][:, :, :], x2_dram[i, :, :, :]).then_inc(sem[f"f_in{j}"], 16)
                sp.dma_start(fslot[j][:, :], slot_dram[i, :, :]).then_inc(sem[f"f_in{j}"], 16)
                sp.dma_start(fgate[j][:, :], gate_dram[i, :, :]).then_inc(sem[f"f_in{j}"], 16)

            def d_store(i, j):
                sp.wait_ge(sem["fo"], total("fo", i, PER["fo"]))
                sp.dma_start(out[i, :, :, :], fo[j][:, :, :]).then_inc(sem[f"out_done{j}"], 16)

            for j in range(DB):
                d_loads(j, j)
            for j in range(2):
                store_expert(E - 2 + j, j)
            with sp.Fori(0, B // DB - 1) as turn:
                for j in range(DB):
                    sp.wait_ge(sem["mix"], total("mix", turn * DB + j, PER["mix"]))
                    d_loads((turn + 1) * DB + j, j)
                for j in range(DB):
                    d_store(turn * DB + j, j)
            for j in range(DB):
                d_store(B - DB + j, j)
            for j in range(DB):
                sp.wait_ge(sem[f"out_done{j}"], B // DB * PER["out_done0"])

        @block.tensor
        def _(pe):
            def mm(o, lhsT, rhs, first=True, last=True):
                return nc.tensor.matmul(o, lhsT, rhs, start=first, stop=last)

            def turn(o, a, ident=None):
                return nc.tensor.transpose(o, a, eye if ident is None else ident)

            def turn_tiles(ring, i, use, src, *after):
                bank = take(ring, pe, i, use, *after)
                for hf in range(2):
                    for c in range(NC):
                        last = turn(bank[:, hf * T + c * P:hf * T + (c + 1) * P],
                                    src[:, c, hf * P:(hf + 1) * P])
                last.then_inc(ring["filled"], 1)

            def turn_chans(ring, i, use, src, *after):
                bank = take(ring, pe, i, use, *after)
                for c in range(NC):
                    for hf in range(2):
                        last = turn(bank[:, c * D + hf * P:c * D + (hf + 1) * P],
                                    src[:, hf, c * P:(c + 1) * P])
                last.then_inc(ring["filled"], 1)

            def chan_product(ring, i, use, w, src, *after, n=2):
                bank = take(ring, pe, i, use, *after)
                for m in range(n):
                    for k in range(2):
                        last = mm(bank[:, m * T:(m + 1) * T], w[:, k, m * P:(m + 1) * P],
                                  src[:, k, :], k == 0, k == 1)
                last.then_inc(ring["filled"], 1)

            def token_product(ring, i, use, src, w, *after):
                bank = take(ring, pe, i, use, *after)
                n = w.shape[2]
                for c in range(NC):
                    for k in range(2):
                        last = mm(bank[:, c * n:(c + 1) * n], src[:, k, c * P:(c + 1) * P],
                                  w[:, k, :], k == 0, k == 1)
                last.then_inc(ring["filled"], 1)

            def per_head(i, use, lhsT, rhs, after=()):
                bank = take(A, pe, i, use, *after)
                for h in range(H):
                    if rhs is None:
                        last = turn(bank[:, h * P:(h + 1) * P], lhsT(h))
                    else:
                        last = mm(bank[:, h * P:(h + 1) * P], lhsT(h), rhs(h))
                last.then_inc(A["filled"], 1)

            def stage_f(i):
                yield "k"
                pe.wait_ge(sem["xT_in"], total("xT_in", i, 16))
                if not (isinstance(i, int) and i < 3):
                    wait_read(R, pe, i - 3, "pos")
                chan_product(F, i, "k_proj", wqkv_sb[:, 1, :, :], xT_sb)
                yield "v"
                chan_product(F, i, "v_proj", wqkv_sb[:, 2, :, :], xT_sb)
                yield "q"
                chan_product(F, i, "q_proj", wqkv_sb[:, 0, :, :], xT_sb)

            def stage_a(i):
                yield "sums"
                bank = take(A, pe, i, "sums")
                pe.wait_ge(sem["sq"], total("sq", i, 2))
                for c in range(NC):
                    for t in range(2):
                        for hf in range(2):
                            at = c * 8 + t * 4 + hf * 2
                            mm(bank[:, at:at + 2], sq[:, t, hf, c * P:(c + 1) * P],
                               headsel_sb[:, :])
                for c in range(NC):
                    for k in range(2):
                        last = mm(bank[:, 16 + c * H:16 + (c + 1) * H],
                                  xT_sb[:, k, c * P:(c + 1) * P], wb_sb[:, k, :], k == 0, k == 1)
                last.then_inc(A["filled"], 1)
                yield "k_tok"
                turn_chans(A, i, "k_tok", qk[:, 1, :, :])
                pe.wait_ge(sem["silu"], total("silu", i, 2))
                turn_chans(A, i, "v_tok", vpad[:, :, PAD:])
                yield "k_chan"
                turn_tiles(A, i, "k_chan", kn, "k_tok")

                def chunk(c):
                    return slice(c * P, (c + 1) * P)

                steps = {
                    "gram": lambda c: per_head(i, f"gram{c}", lambda h: kz[:, h // 2, h % 2, chunk(c)],
                                               lambda h: kz[:, h // 2, h % 2, chunk(c)],
                                               ["k_chan"]),
                    "gramT": lambda c: per_head(i, f"gramT{c}", lambda h: nbG[c][:, h, :], None,
                                                [f"gram{c}"]),
                    "P2": lambda c: (pe.wait_ge(sem["x8"], total("x8", i, c + 1)),
                                     pe.wait_ge(sem["t1"], total("t1", i, 2 * c + 1)),
                                     per_head(i, f"P2{c}", lambda h: XT[c][0][:, h, :],
                                              lambda h: X8[c][:, h, :], [f"gramT{c}"])),
                    "P2T": lambda c: per_head(i, f"P2T{c}", lambda h: W[c][0][:, h, :], None,
                                              [f"P2{c}"]),
                    "P4": lambda c: per_head(i, f"P4{c}", lambda h: W[c][1][:, h, :],
                                             lambda h: W[c][0][:, h, :], [f"P2{c}", f"P2T{c}"]),
                    "T2T": lambda c: (pe.wait_ge(sem["t1"], total("t1", i, 2 * c + 2)),
                                      per_head(i, f"T2T{c}", lambda h: W[c][0][:, h, :],
                                               lambda h: Ta[c][:, h, :])),
                    "T8T": lambda c: per_head(i, f"T8T{c}", lambda h: W[c][2][:, h, :],
                                              lambda h: Tb[c][:, h, :], [f"P4{c}", f"T2T{c}"]),
                    "T8": lambda c: per_head(i, f"T8{c}", lambda h: Ta[c][:, h, :], None,
                                             [f"T8T{c}"]),
                    "aT": lambda c: per_head(i, f"aT{c}", lambda h: kz[:, h // 2, h % 2, chunk(c)],
                                             lambda h: qk[:, 0, h // 2, chunk(c)]),
                }
                for s, (t, w, wt, w2_, u, tt) in enumerate(
                        [("T8", "W", "WT", "W2", "U", "T32T"), ("T32", "Y", "YT", "Y2", "V", "TT")]):
                    def level(s=s, t=t, w=w, wt=wt, w2_=w2_, u=u, tt=tt):
                        xo = s + 1
                        return {
                            w: lambda c: (pe.wait_ge(sem["xm"], total("xm", i, 2 * c + xo)),
                                          per_head(i, f"{w}{c}", lambda h: XT[c][xo][:, h, :],
                                                  lambda h: Tn[c][:, h, :], [f"{t}{c}"])),
                            wt: lambda c: per_head(i, f"{wt}{c}", lambda h: W[c][0][:, h, :],
                                                   None, [f"{w}{c}"]),
                            w2_: lambda c: per_head(i, f"{w2_}{c}", lambda h: W[c][1][:, h, :],
                                                    lambda h: W[c][0][:, h, :],
                                                    [f"{w}{c}", f"{wt}{c}"]),
                            u: lambda c: per_head(i, f"{u}{c}", lambda h: W[c][2][:, h, :],
                                                  lambda h: Ta[c][:, h, :], [f"{w2_}{c}"]),
                            tt: lambda c: per_head(i, f"{tt}{c}", lambda h: W[c][0][:, h, :],
                                                   lambda h: Tb[c][:, h, :], [f"{u}{c}"]),
                        }
                    steps.update(level())
                steps["T32"] = lambda c: per_head(i, f"T32{c}", lambda h: Ta[c][:, h, :], None,
                                                  [f"T32T{c}"])
                for name in INVERSE:
                    yield name
                    for c in range(NC):
                        steps[name](c)

                yield "u0"
                pe.wait_ge(sem["vb"], total("vb", i, 1))
                bank = take(A, pe, i, "u0", "TT0")
                for h in range(H):
                    last = mm(bank[:, h * HD:(h + 1) * HD], Ta[0][:, h, :],
                              vb[:, 0, h * HD:(h + 1) * HD])
                last.then_inc(A["filled"], 1)
                pe.wait_ge(sem["kb"], total("kb", i, 1))
                bank = take(A, pe, i, "wT1", "TT1")
                for h in range(H):
                    last = mm(bank[(h % 2) * HD:(h % 2 + 1) * HD, (h // 2) * P:(h // 2 + 1) * P],
                              kb[:, h * HD:(h + 1) * HD], Ta[1][:, h, :])
                last.then_inc(A["filled"], 1)
                yield "S0"
                bank = take(A, pe, i, "S0", "u0")
                for h in range(H):
                    last = mm(bank[(h % 2) * HD:(h % 2 + 1) * HD, h * HD:(h + 1) * HD],
                              kn[:, 0, h * HD:(h + 1) * HD], u_sb[0][:, h * HD:(h + 1) * HD])
                last.then_inc(A["filled"], 1)
                bank = take(A, pe, i, "o0", "aT0")
                for h in range(H):
                    last = mm(bank[:, h * HD:(h + 1) * HD], aT[0][:, h, :],
                              u_sb[0][:, h * HD:(h + 1) * HD])
                last.then_inc(A["filled"], 1)
                yield "u1"
                bank = take(A, pe, i, "u1", "wT1", "S0")
                for h in range(H):
                    mm(bank[:, h * HD:(h + 1) * HD], Ta[1][:, h, :],
                       vb[:, 1, h * HD:(h + 1) * HD], True, False)
                    last = mm(bank[:, h * HD:(h + 1) * HD], wTn[:, h // 2, :], S_sb[:, h, :],
                              False, True)
                last.then_inc(A["filled"], 1)
                yield "o1"
                bank = take(A, pe, i, "o1", "u1", "aT1")
                for h in range(H):
                    mm(bank[:, h * HD:(h + 1) * HD], aT[1][:, h, :],
                       u_sb[1][:, h * HD:(h + 1) * HD], True, False)
                    last = mm(bank[:, h * HD:(h + 1) * HD], qk[:, 0, h // 2, P:T], S_sb[:, h, :],
                              False, True)
                last.then_inc(A["filled"], 1)

                yield "mix"
                if isinstance(i, int) and i == 0:
                    pe.wait_ge(consts_in, CONSTS)
                pe.wait_ge(sem["taps"], total("taps", i, PER["taps"]))
                bank = take(A, pe, i, "mix")
                for m in range(2):
                    for k in range(3):
                        j = 3 * m + k
                        last = mm(bank[:, m * T:(m + 1) * T], kmix_sb[:, j, :],
                                  acc[:, j // 2, j % 2, :], k == 0, k == 2)
                last.then_inc(A["filled"], 1)
                yield "ms"
                token_product(A, i, "ms", y1, cmix_sb, "mix")
                yield "statT"
                pe.wait_ge(sem["stat"], total("stat", i, 3))
                bank = take(A, pe, i, "statT")
                for c in range(NC):
                    last = turn(bank[0:3 * H, c * P:(c + 1) * P], st[:, c, :])
                last.then_inc(A["filled"], 1)
                yield "hid"
                pe.wait_ge(sem["xTf_in"], total("xTf_in", i, 16))
                for n in range(2):
                    bank = take(A, pe, i, f"hid{n}", "statT")
                    for m in range(2):
                        at = (2 * n + m) * P
                        for k in range(2):
                            mm(bank[:, m * T:(m + 1) * T], fw1_sb[:, k, at:at + P], xTf_sb[:, k, :],
                               k == 0, False)
                        last = mm(bank[:, m * T:(m + 1) * T], fw1s_sb[:, at:at + P], gst[:, :],
                                  False, True)
                    last.then_inc(A["filled"], 1)
                yield "logit"
                bank = take(A, pe, i, "logit", "hid0", "hid1")
                for c in range(NC):
                    for m in range(4):
                        last = mm(bank[:, c * 3 * H:(c + 1) * 3 * H],
                                  hdn[m // 2][:, m % 2, c * P:(c + 1) * P], fw2_sb[:, m, :], m == 0, m == 3)
                last.then_inc(A["filled"], 1)
                yield "oT"
                pe.wait_ge(sem["on"], total("on", i, 1))
                turn_tiles(A, i, "oT", o1)
                yield "attn"
                token_product(A, i, "attn", oT, wo_sb, "oT")

            def gathers(i, k, half, c):
                use = f"gather{k}_{c}"
                bank = bank_of(G, use) if half else take(G, pe, i, use)
                for h in range(XH // 2):
                    head = half * XH // 2 + h
                    last = mm(bank[:, head * 32:(head + 1) * 32],
                              nhat[half][:, h, c * P:(c + 1) * P],
                              tab[:, head, :, :].rearrange("p a d -> p (a d)"))
                if half:
                    last.then_inc(G["filled"], 1)
                elif c == NC - 1:
                    last.then_inc(sem["hats_used"], 1)

            def stage_b(i):
                yield "x1T"
                pe.wait_ge(sem["x1"], total("x1", i, 2))
                turn_tiles(Bk, i, "x1T", x1)
                yield "Qc"
                chan_product(Bk, i, "Qc", xwT_sb[:, 2, :, :], x1T, "x1T")
                yield "off"
                bank = take(Bk, pe, i, "off", "Qc")
                for k in range(2):
                    last = mm(bank[0:96, 0:T], woff_sb[:, k, :], QT[:, k, :], k == 0, k == 1)
                last.then_inc(Bk["filled"], 1)
                yield "tables"
                pe.wait_ge(sem["ctx_in"], total("ctx_in", i, 16))
                for use, t in (("Kt", 0), ("Vt", 1)):
                    bank = take(Bk, pe, i, use)
                    for k in range(2):
                        last = mm(bank[0:S2, 0:D], ctxT_sb[:, k, :], xwT_sb[:, t, k, :],
                                  k == 0, k == 1)
                    last.then_inc(Bk["filled"], 1)
                yield "Qt"
                turn_chans(Bk, i, "Qt", QT)

                def distances(k, half, part):
                    for j in (2 * part, 2 * part + 1):
                        bank = take(Bk, pe, i, f"dist{k}{half}_{j}")
                        for m in range(2):
                            r = (k % 2) * XH + half * XH // 2 + 2 * j + m
                            last = mm(bank[0:S2, m * T:(m + 1) * T], sel_sb[:, r, :],
                                      ixp[:, k // 2, :])
                        last.then_inc(Bk["filled"], 1)

                yield "first0"
                pe.wait_ge(sem["ixp_in"], total("ixp_in", i, PER["ixp_in"]))
                distances(0, 0, 0)
                distances(0, 0, 1)
                yield "first1"
                distances(0, 1, 0)
                distances(0, 1, 1)
                for k in range(NK - 1):
                    for half in range(2):
                        yield f"gather{k}{half}"
                        pe.wait_ge(sem["nhat"], total("nhat", i, 2 * k + half + 1))
                        if k == 0 and half == 0:
                            wait_read(Bk, pe, i, "Kt", "Vt")
                        gathers(i, k, half, 0)
                        yield f"dist{k}{half}"
                        gathers(i, k, half, 1)
                        distances(k + 1, half, 0)
                        yield f"hats{k}{half}"
                        distances(k + 1, half, 1)

            def stage_r(i):
                for half in range(2):
                    yield f"gather{half}"
                    pe.wait_ge(sem["nhat"], total("nhat", i, 2 * (NK - 1) + half + 1))
                    for c in range(NC):
                        gathers(i, NK - 1, half, c)
                yield "ctxT"
                pe.wait_ge(sem["actx"], total("actx", i, 2))
                if not (isinstance(i, int) and i + 2 >= B):
                    wait_read(F, pe, i + 2, "q_proj")
                turn_tiles(R, i, "ctxT", actx)
                yield "xout"
                token_product(R, i, "xout", cT, xwT_sb[:, 3, :, :], "ctxT")
                yield "x2T"
                pe.wait_ge(sem["x2"], total("x2", i, 2))
                turn_tiles(R, i, "x2T", x2)
                yield "route"
                token_product(R, i, "route", x2T, wr_sb, "x2T")
                yield "pos"
                pe.wait_ge(sem["ohs"], total("ohs", i, 2))
                bank = take(R, pe, i, "pos")
                for c in range(NC):
                    o = bank[:, c * E:(c + 1) * E]
                    mm(o, mk[:, M_BEFORE, :], ohs[:, c, :], True, False)
                    if c == 1:
                        mm(o, mk[:, M_ONES, :], ohs[:, 0, :], False, False)
                    last = mm(o, mk[:, M_ONES, :], count[:, :], False, True)
                last.then_inc(R["filled"], 1)

            def product(o, lhsT, rhs, first, last):
                for n, (a, b) in enumerate(((1, 0), (0, 1), (0, 0))):
                    ins = mm(o, lhsT(a), rhs(b), first and n == 0, last and n == 2)
                return ins

            def turn_rows(e, pair, j):
                pe.wait_ge(sem[f"xe_in{j}"], (pair + 1) * PER["xe_in0"])
                for n in range(NT // 2):
                    bank = take(X, pe, e, f"xeT{n}")
                    for k in range(2):
                        for t in range(2):
                            last = turn(bank[:, k * T + t * P:k * T + (t + 1) * P],
                                        xe[j][:, 2 * n + t, k * P:(k + 1) * P])
                    last.then_inc(X["filled"], 1)

            def stage_c(e, pair, j, more=True):
                pe.wait_ge(sem["w1_parts"], total("w1_parts", e, PER["w1_parts"]))
                wait_read(X, pe, e, *X_USES)
                for m in range(HID // P):
                    at = slice(m * P, (m + 1) * P)
                    for part, (lo, hi) in (("a", (0, 512)), ("b", (512, CAP))):
                        bank = take(C, pe, e, f"h{m}{part}")
                        for k in range(2):
                            last = product(bank[:, 0:hi - lo], lambda n: w1_p[n][:, k, at],
                                           lambda n: xeT_p[n][:, k, lo:hi], k == 0, k == 1)
                        last.then_inc(C["filled"], 1)
                if more:
                    turn_rows(e + 1, pair + j, 1 - j)
                pe.wait_ge(sem["w2_parts"], total("w2_parts", e, PER["w2_parts"]))
                for n in range(NT // 2):
                    bank = take(C, pe, e, f"y{n}")
                    for t in range(2):
                        at = slice((2 * n + t) * P, (2 * n + t + 1) * P)
                        for m in range(HID // P):
                            if n == 0 and t == 0:
                                pe.wait_ge(sem["h_parts"], total("h_parts", e, 2 * (m + 1)))
                            last = product(bank[:, t * D:(t + 1) * D],
                                           lambda n: hT_p[n][:, m, at],
                                           lambda n: w2_p[n][:, m, :],
                                           m == 0, m == HID // P - 1)
                    last.then_inc(C["filled"], 1)

            pe.wait_ge(first_in, FIRST)
            run(F=stage_f(0))
            pe.wait_ge(early_in, EARLY)
            pe.wait_ge(prepared, 2)
            pe.wait_ge(zeroed, ZEROED)
            run(A=stage_a(0), F=stage_f(1))
            run(A=stage_a(1), B=stage_b(0), F=stage_f(2))
            run(A=stage_a(2), B=stage_b(1), R=stage_r(0), F=stage_f(3))
            with pe.Fori(2, B - 2) as i:
                run(A=stage_a(i + 1), B=stage_b(i), R=stage_r(i - 1), F=stage_f(i + 2))
            run(A=stage_a(B - 1), B=stage_b(B - 2), R=stage_r(B - 3))
            run(B=stage_b(B - 1), R=stage_r(B - 2))
            run(R=stage_r(B - 1))
            for ring in (F, R, A, Bk, G):
                for b in range(len(ring["banks"])):
                    pe.wait_ge(ring["read"][b], B * ring["per"][b])
            turn_rows(0, 0, 0)
            for j in range(2):
                stage_c(j, 0, j)
            with pe.Fori(1, E // 2 - 1) as pair:
                for j in range(2):
                    stage_c(pair * 2 + j, pair, j)
            stage_c(E - 2, E // 2 - 1, 0)
            stage_c(E - 1, E // 2 - 1, 1, more=False)

        @block.scalar
        def _(act):
            def read_out(ring, i, use, dst, view, func=ACT.Copy, **kw):
                bank = wait_filled(ring, act, i, use)
                nc.scalar.activation(dst, view(bank), func, **kw).then_inc(was_read(ring, use), 1)

            def all_of(bank):
                return bank[:, :]

            def halves(bank):
                return bank[:, :].rearrange("p (c t) -> p c t", c=2)

            def per_head(bank):
                return bank[:, :].rearrange("p (h t) -> p h t", h=H)

            def samples(c, k):
                step = 2 + k - k % 2
                return gs[:, c, k % 2:3 + k:step, :, :]

            def keys_values(bank):
                return bank[:, :].rearrange("p (h a d) -> p a h d", a=2, h=XH)

            def stage_f(i):
                for n, (name, t) in enumerate((("k", 1), ("v", 2), ("q", 0))):
                    yield name
                    read_out(F, i, f"{name}_proj", pre[:, t, :, 3:], halves)
                    yield name + "_act"
                    act.wait_ge(sem["conv"], total("conv", i, 8 * (n + 1)))
                    act.activation(th[:, t, :, :], y[:, t, :, :], ACT.Tanh).then_inc(sem["tanh"], 1)

            def stage_a(i):
                yield "sums"
                wait_read(A, act, i, "sums")
                act.activation(bth[:, :, :], sums[:, 16:24].rearrange("p (c h) -> p c h", c=NC),
                               ACT.Tanh, scale=0.5).then_inc(sem["beta_th"], 1)
                yield "k_tok"
                read_out(A, i, "v_tok", vt[:, :, :], halves)
                yield "k_chan"
                bank = wait_filled(A, act, i, "k_chan")
                for m in range(2):
                    rows = slice(m * HD, (m + 1) * HD)
                    last = act.activation(kz[rows, :, m, :], halves(bank)[rows], ACT.Copy)
                last.then_inc(was_read(A, "k_chan"), 1)
                into = {"gramT": lambda c: XT[c][2], "P2": lambda c: W[c][0],
                        "P2T": lambda c: W[c][1], "P4": lambda c: W[c][2],
                        "T8": lambda c: Tn[c], "W": lambda c: W[c][0], "WT": lambda c: W[c][1],
                        "W2": lambda c: W[c][2], "T32": lambda c: Tn[c], "Y": lambda c: W[c][0],
                        "YT": lambda c: W[c][1], "Y2": lambda c: W[c][2]}
                for name in INVERSE:
                    yield name
                    for c in range(NC):
                        if name in into:
                            read_out(A, i, f"{name}{c}", into[name](c)[:, :, :], per_head)
                yield "u0"
                read_out(A, i, "u0", u_sb[0][:, :], lambda b: b[:, 0:D])
                read_out(A, i, "wT1", wTn[:, :, :],
                         lambda b: b[:, 0:2 * P].rearrange("p (c t) -> p c t", c=2), scale=-1.0)
                yield "S0"
                bank = wait_filled(A, act, i, "S0")
                for m in range(2):
                    rows = slice(m * HD, (m + 1) * HD)
                    last = act.activation(
                        S_sb[rows, m:H:2, :],
                        bank[rows, 0:D].rearrange("p (h d) -> p h d", h=H)[:, m:H:2, :], ACT.Copy)
                last.then_inc(was_read(A, "S0"), 1)
                yield "u1"
                read_out(A, i, "u1", u_sb[1][:, :], lambda b: b[:, 0:D])
                yield "mix"
                read_out(A, i, "mix", y1[:, :, :], halves)
                yield "ms"
                read_out(A, i, "ms", ms[:, :, :], halves)
                yield "statT"
                read_out(A, i, "statT", gst[:, :], lambda b: b[0:3 * H, 0:T], scale=1.0 / HD)
                yield "hid"
                for n in range(2):
                    bank = wait_filled(A, act, i, f"hid{n}")
                    for m in range(2):
                        last = nc.scalar.activation(hdn[n][:, m, :], bank[:, m * T:(m + 1) * T],
                                                    ACT.Gelu,
                                                    bias=fb1_sb[:, 2 * n + m:2 * n + m + 1])
                    last.then_inc(was_read(A, f"hid{n}"), 1)
                yield "logit"
                act.wait_ge(sem["fuse"], total("fuse", i, 2))
                act.activation(lex[:, :, :], lg[:, :, :], ACT.Exp).then_inc(sem["wexp"], 1)
                yield "oT"
                read_out(A, i, "oT", oT[:, :, :], halves)

            def stage_b(i):
                yield "x1T"
                read_out(Bk, i, "x1T", x1T[:, :, :], halves)
                yield "Qc"
                bank = wait_filled(Bk, act, i, "Qc")
                for m in range(2):
                    last = nc.scalar.activation(QT[:, m, :], bank[:, m * T:(m + 1) * T],
                                                ACT.Identity, bias=bq_sb[:, m:m + 1])
                last.then_inc(was_read(Bk, "Qc"), 1)
                yield "Qt"
                at_least(act, sem["prod"], total("prod", i, 0))
                read_out(Bk, i, "Qt", Qs[:, :, :], halves, scale=0.5 * XD ** -0.5)

                def distances(k, half, part):
                    for j in (2 * part, 2 * part + 1):
                        read_out(Bk, i, f"dist{k}{half}_{j}", nhat[half][:, 2 * j:2 * j + 2, :],
                                 lambda b: b[0:S2, :].rearrange("p (m t) -> p m t", m=2), ACT.Abs)

                def weights(k, half):
                    wait_read(Bk, act, i, f"dist{k}{half}_2", f"dist{k}{half}_3")
                    act.activation(nhat[half][:, :, :], nhat[half][:, :, :], ACT.Relu, scale=-1.0,
                                   bias=1.0).then_inc(sem["nhat"], 1)

                yield "first0"
                at_least(act, G["filled"], i * G["uses"])
                distances(0, 0, 0)
                distances(0, 0, 1)
                weights(0, 0)
                yield "first1"
                distances(0, 1, 0)
                distances(0, 1, 1)
                weights(0, 1)
                for k in range(NK - 1):
                    for half in range(2):
                        if half:
                            yield f"gather{k}1"
                            if k == 0:
                                at_least(act, sem["actx"], total("actx", i, 0))
                            if k > 1:
                                act.wait_ge(sem["prod"], total("prod", i, k - 1))
                            read_out(G, i, f"gather{k}_0", samples(0, k), keys_values)
                        yield f"dist{k}{half}"
                        if half:
                            act.wait_ge(G["filled"], i * G["uses"] + (k + 1) * NC)
                        else:
                            act.wait_ge(sem["hats_used"], total("hats_used", i, k + 1))
                        distances(k + 1, half, 0)
                        if half:
                            read_out(G, i, f"gather{k}_1", samples(1, k), keys_values)
                        yield f"hats{k}{half}"
                        distances(k + 1, half, 1)
                        weights(k + 1, half)

            def stage_r(i):
                yield "gather1"
                act.wait_ge(sem["prod"], total("prod", i, NK - 2))
                for c in range(NC):
                    read_out(G, i, f"gather{NK - 1}_{c}", samples(c, NK - 1), keys_values)
                yield "exp"
                act.wait_ge(sem["scs"], total("scs", i, 2))
                act.activation(sce[:, :, :, :], scd[:, :, :, :], ACT.Exp).then_inc(sem["sexp"], 1)
                yield "ctxT"
                read_out(R, i, "ctxT", cT[:, :, :], halves)
                yield "x2T"
                read_out(R, i, "x2T", x2T[:, :, :], halves)
                yield "route"
                wait_read(R, act, i, "route")
                act.activation(prx[:, :, :], prd[:, :, :], ACT.Exp).then_inc(sem["rexp"], 1)

            def split_w2(e, pair, j):
                act.wait_ge(sem[f"w_in{j}"], (pair + 1) * PER["w_in0"])
                act.activation(w2_p[0][:, :, :], w2_sb[j][:, :, :], ACT.Copy)\
                    .then_inc(sem["w2_hi"], 1)

            def turn_rows(e):
                for n in range(NT // 2):
                    bank = wait_filled(X, act, e, f"xeT{n}")
                    act.activation(xeT_p[0][:, :, 2 * n * P:(2 * n + 2) * P], halves(bank),
                                   ACT.Copy).then_inc(sem["x_hi"], 1)

            def stage_c(e, pair, j, more=True):
                act.wait_ge(sem[f"be_in{j}"], (pair + 1) * PER["be_in0"])
                for m in range(HID // P):
                    if m < 2:
                        at_least(act, sem["h_parts"], total("h_parts", e, 0))
                    else:
                        act.wait_ge(sem["h_parts"], total("h_parts", e, 2 * (m - 1)))
                    for part, (lo, hi) in (("a", (0, 512)), ("b", (512, CAP))):
                        read_out(C, e, f"h{m}{part}", h_sb[m % 2][:, lo:hi],
                                 lambda b, n=hi - lo: b[:, 0:n], ACT.Relu,
                                 bias=b1_sb[j][:, m:m + 1])
                if more:
                    turn_rows(e + 1)
                    wait_filled(C, act, e, f"y{NT // 2 - 1}")
                    split_w2(e + 1, pair + j, 1 - j)

            run(F=stage_f(0))
            act.wait_ge(early_in, EARLY)
            act.wait_ge(zeroed, ZEROED)
            run(A=stage_a(0), F=stage_f(1))
            act.wait_ge(consts_in, CONSTS)
            act.wait_ge(xe_zero, 16 * ZERO_DMAS)
            run(A=stage_a(1), B=stage_b(0), F=stage_f(2))
            run(A=stage_a(2), B=stage_b(1), R=stage_r(0), F=stage_f(3))
            with act.Fori(2, B - 2) as i:
                run(A=stage_a(i + 1), B=stage_b(i), R=stage_r(i - 1), F=stage_f(i + 2))
            run(A=stage_a(B - 1), B=stage_b(B - 2), R=stage_r(B - 3))
            run(B=stage_b(B - 1), R=stage_r(B - 2))
            split_w2(0, 0, 0)
            run(R=stage_r(B - 1))
            turn_rows(0)
            for j in range(2):
                stage_c(j, 0, j)
            with act.Fori(1, E // 2 - 1) as pair:
                for j in range(2):
                    stage_c(pair * 2 + j, pair, j)
            stage_c(E - 2, E // 2 - 1, 0)
            stage_c(E - 1, E // 2 - 1, 1, more=False)

        @block.vector
        def _(dve):
            given, batch = {}, {}

            def begin(i, names):
                for name in names:
                    given[name], batch[name] = 0, i

            def end(names):
                for name in names:
                    assert given[name] == PER[name], (name, given[name], PER[name])

            def count_in(ins, name):
                given[name] += 1
                ins.then_inc(sem[name], 1)

            def own(name, k):
                dve.wait_ge(sem[name], batch[name] * PER[name] + k)

            def link(ins, name):
                count_in(ins, name)
                own(name, given[name])

            def stage_f(i):
                names = ("conv", "silu")
                begin(i, names)

                def short_conv(t):
                    for tap in range(4):
                        for hf in range(2):
                            w = convw_sb[:, t, hf, tap:tap + 1]
                            src = pre[:, t, hf, tap:tap + T]
                            if tap == 0:
                                ins = dve.tensor_scalar(y[:, t, hf, :], src, w, None, ALU.mult)
                            else:
                                own("conv", given["conv"] - 1)
                                ins = dve.scalar_tensor_tensor(y[:, t, hf, :], src, w,
                                                               y[:, t, hf, :], ALU.mult, ALU.add)
                            count_in(ins, "conv")

                def silu(n, t, dst):
                    dve.wait_ge(sem["tanh"], total("tanh", i, n))
                    count_in(dve.scalar_tensor_tensor(dst, th[:, t, :, :], 1.0, y[:, t, :, :],
                                                    ALU.add, ALU.mult), "silu")

                for n, (name, t) in enumerate((("k", 1), ("v", 2), ("q", 0))):
                    yield name + "_conv"
                    wait_read(F, dve, i, f"{name}_proj")
                    short_conv(t)
                    yield name + "_act"
                    if name == "v" and not (isinstance(i, int) and i == 0):
                        dve.wait_ge(sem["taps"], i * PER["taps"])
                    if name == "q" and not (isinstance(i, int) and i == 0):
                        wait_filled(A, dve, i - 1, "o1")
                    silu(n + 1, t, vpad[:, :, PAD:] if name == "v" else qk[:, t, :, :])
                end(names)

            def taps(i):
                begin(i, ("taps",))
                for n in range(len(TAPS_AT)):
                    yield n
                    for tap, scale, hf in TAP_ORDER[given["taps"]:given["taps"] + TAPS_AT[n]]:
                        w = msw_sb[scale][:, hf, tap:tap + 1]
                        at = PAD - (TAPS[scale] - 1) + tap
                        src = vpad[:, hf, at:at + T]
                        dst = acc[:, scale, hf, :]
                        if tap == 0:
                            ins = dve.tensor_scalar(dst, src, w, None, ALU.mult)
                        else:
                            own("taps", TAP_AT[tap - 1, scale, hf] + 1)
                            ins = dve.scalar_tensor_tensor(dst, src, w, dst, ALU.mult, ALU.add)
                        count_in(ins, "taps")
                end(("taps",))

            def stage_a(i):
                names = ("beta", "t1", "stat", "fuse", "osum", "orms", "on", "var1", "x1")
                begin(i, names)
                yield "sums"

                bank = wait_filled(A, dve, i, "sums")
                dve.tensor_copy(sums[:, :], bank[:, 0:24]).then_inc(was_read(A, "sums"), 1)
                dve.wait_ge(sem["beta_th"], total("beta_th", i, 1))
                count_in(dve.tensor_scalar(beta[:, :, :], bth[:, :, :], 0.5, 0.5, ALU.mult, ALU.add),
                       "beta")
                link(dve.tensor_scalar(nbeta[:, :, :], bth[:, :, :], -0.5, -0.5, ALU.mult, ALU.add),
                     "beta")
                yield "k_tok"
                dve.wait_ge(sem["rinv"], total("rinv", i, 2))
                bank = wait_filled(A, dve, i, "k_tok")
                dve.tensor_tensor(split(kn[:, :, :]),
                                  bank[:, :].rearrange("p (c h d) -> p c h d", c=NC, h=H),
                                  heads(rinv[:, :, 1, :]), ALU.mult)\
                    .then_inc(was_read(A, "k_tok"), 1)

                def evict(use, dst, in1, op):
                    bank = wait_filled(A, dve, i, use)
                    dve.tensor_tensor(dst, bank[:, :].rearrange("p (h t) -> p h t", h=H), in1, op)\
                        .then_inc(was_read(A, use), 1)

                for name in INVERSE:
                    yield name
                    for c in range(NC):
                        use = f"{name}{c}"
                        if name == "gram":
                            evict(use, nbG[c][:, :, :],
                                  nbeta[:, c, :].unsqueeze(2).broadcast_to([P, H, P]), ALU.mult)
                        elif name == "gramT":
                            wait_read(A, dve, i, use)
                            link(dve.tensor_tensor(XT[c][0][:, :, :], XT[c][2][:, :, :],
                                                   mask4(M_DIAG8T), ALU.mult), "t1")
                            link(dve.tensor_tensor(Ta[c][:, :, :], XT[c][0][:, :, :],
                                                   mask4(M_EYE), ALU.add), "t1")
                        elif name in ("T2T", "U", "V"):
                            evict(use, Tb[c][:, :, :], Ta[c][:, :, :], ALU.add)
                            wait_read(A, dve, i, use)
                        elif name in ("T8T", "T32T", "TT"):
                            evict(use, Ta[c][:, :, :], Tb[c][:, :, :], ALU.add)
                            wait_read(A, dve, i, use)
                        elif name == "aT":
                            evict(use, aT[c][:, :, :], mask4(M_INCL), ALU.mult)
                for c in range(NC):
                    yield ("S0", "o1")[c]
                    bank = wait_filled(A, dve, i, f"o{c}")
                    dve.tensor_tensor(delta[:, c, :].rearrange("p (h d) -> p h d", h=H),
                                      bank[:, 0:D].rearrange("p (h d) -> p h d", h=H),
                                      rinv[:, c, 0, :].unsqueeze(2).broadcast_to([P, H, HD]),
                                      ALU.mult).then_inc(was_read(A, f"o{c}"), 1)
                yield "ms"
                wait_read(A, dve, i, "o0", "o1", "v_tok", "ms")
                for n, src in enumerate((ms, delta, vt)):
                    count_in(dve.tensor_reduce(st[:, :, n * H:(n + 1) * H], split(src[:, :, :]),
                                             AX.X, ALU.add, apply_absolute_value=True), "stat")
                yield "logit"
                bank = wait_filled(A, dve, i, "logit")
                dve.tensor_tensor(lg[:, :, :].rearrange("p (c h) x -> p c (h x)", c=NC),
                                  bank[:, 0:6 * H].rearrange("p (c x) -> p c x", c=NC),
                                  fb2_sb[:, :].unsqueeze(1).broadcast_to([P, NC, 3 * H]),
                                  ALU.add).then_inc(was_read(A, "logit"), 1)
                wait_read(A, dve, i, "logit")
                link(dve.tensor_reduce(lmx[:, :], lg[:, :, :], AX.X, ALU.max), "fuse")

                def over3(ap):
                    return ap.unsqueeze(2).broadcast_to([P, NC * H, 3])

                link(dve.tensor_tensor(lg[:, :, :], lg[:, :, :], over3(lmx[:, :]), ALU.subtract),
                     "fuse")
                yield "fuse"
                dve.wait_ge(sem["wexp"], total("wexp", i, 1))
                link(dve.tensor_reduce(lmx[:, :], lex[:, :, :], AX.X, ALU.add), "fuse")
                link(dve.reciprocal(lmx[:, :], lmx[:, :]), "fuse")
                link(dve.tensor_tensor(wts[:, :, :], lex[:, :, :], over3(lmx[:, :]), ALU.mult),
                     "fuse")

                def weight(n):
                    return heads(wts[:, :, n].rearrange("p (c h) -> p c h", c=NC))

                dve.tensor_tensor(split(o1[:, :, :]), split(ms[:, :, :]), weight(0), ALU.mult)
                link(dve.tensor_tensor(split(o2[:, :, :]), split(delta[:, :, :]), weight(1),
                                       ALU.mult), "fuse")
                link(dve.tensor_tensor(o1[:, :, :], o1[:, :, :], o2[:, :, :], ALU.add), "osum")
                yield "gate"
                dve.wait_ge(sem["v3"], total("v3", i, 1))
                link(dve.tensor_tensor(o1[:, :, :], o1[:, :, :], o3[:, :, :], ALU.add), "osum")
                yield "rms"
                dve.wait_ge(sem["osq"], total("osq", i, 1))
                link(dve.tensor_reduce(rms[:, :].rearrange("p (c h) -> p c h", c=NC),
                                       split(o2[:, :, :]), AX.X, ALU.add), "orms")
                link(dve.tensor_scalar(rms[:, :], rms[:, :], 1.0 / HD, EPS, ALU.mult, ALU.add),
                     "orms")
                yield "oT"
                dve.wait_ge(sem["orr"], total("orr", i, 1))
                link(dve.tensor_tensor(split(o1[:, :, :]), split(o1[:, :, :]),
                                       heads(rrms[:, :].rearrange("p (c h) -> p c h", c=NC)),
                                       ALU.mult), "on")
                yield "attn"
                dve.wait_ge(sem["xt_in"], total("xt_in", i, 16))
                bank = wait_filled(A, dve, i, "attn")
                dve.tensor_tensor(xr[:, :, :], bank[:, :].rearrange("p (c d) -> p c d", c=NC),
                                  xt_sb[:, :, :], ALU.add).then_inc(was_read(A, "attn"), 1)
                wait_read(A, dve, i, "attn")
                moments(xr, bns, mv, ve, "var1")
                yield "norm"
                at_least(dve, sem["res"], total("res", i, 0))
                normalize(i, xr, x1, mv, rstd, "rstd1", "x1")
                end(names)

            def moments(src, bn, m, v, var):
                for c in range(NC):
                    count_in(dve.bn_stats(bn[:, c, :], src[:, c, :]), var)
                own(var, given[var])
                dve.nop(nofuse=True)
                for c in range(NC):
                    last = dve.bn_aggr(m[:, c, :], bn[:, c, :])
                link(last, var)
                link(dve.tensor_scalar(v[:, :], m[:, :, 1], EPS, None, ALU.add), var)

            def normalize(i, src, dst, m, r, rs, done):
                dve.wait_ge(sem[rs], total(rs, i, 1))
                for c in range(NC):
                    count_in(dve.tensor_scalar(dst[:, c, :], src[:, c, :], m[:, c, 0:1],
                                             r[:, c:c + 1], ALU.subtract, ALU.mult), done)

            def stage_b(i):
                names = ("length", "loc", "parts", "scr")
                begin(i, names)
                yield "Qc"
                dve.wait_ge(sem["mask_in"], total("mask_in", i, 16))
                link(dve.tensor_copy(maskf[:, :], mask_sb[:, :]), "length")
                link(dve.tensor_reduce(msum[:, :], maskf[:, :], AX.X, ALU.add), "length")
                link(dve.tensor_scalar(Lb[:, :], msum[:, :], -1.0, float(S2 - 1), ALU.mult, ALU.add),
                     "length")
                link(dve.reciprocal(rL[:, :], Lb[:, :]), "length")
                yield "off"
                bank = wait_filled(Bk, dve, i, "off")
                dve.scalar_tensor_tensor(loc, bank[0:96, 0:T], offc_sb[:, :], posq[:, :],
                                         ALU.add, ALU.add).then_inc(was_read(Bk, "off"), 1)
                wait_read(Bk, dve, i, "off")
                link(dve.tensor_scalar(tmp, loc, rL[:, :], None, ALU.mult), "loc")
                link(dve.tensor_scalar(tmp, tmp, ROUND, None, ALU.add), "loc")
                link(dve.tensor_scalar(tmp, tmp, ROUND, Lb[:, :], ALU.subtract, ALU.mult), "loc")
                link(dve.tensor_tensor(loc, loc, tmp, ALU.subtract), "loc")
                link(dve.tensor_scalar(tmp, loc, Lb[:, :], 0.0, ALU.mult, ALU.is_lt), "loc")
                link(dve.tensor_scalar(tmp, tmp, Lb[:, :], None, ALU.mult), "loc")
                link(dve.tensor_tensor(loc, loc, tmp, ALU.add), "loc")
                link(dve.tensor_scalar(loc, loc, S2 / (S2 - 1.0), -0.5, ALU.mult, ALU.add), "loc")
                at_least(dve, sem["ixp_in"], total("ixp_in", i, 0))
                for part in range(3):
                    link(dve.tensor_copy(parts[:, part, :], loc), "parts")
                    if part < 2:
                        link(dve.tensor_tensor(loc, loc, parts[:, part, :], ALU.subtract), "parts")
                yield "tables"
                at_least(dve, G["filled"], i * G["uses"])
                for n, use in enumerate(("Kt", "Vt")):
                    bank = wait_filled(Bk, dve, i, use)
                    dve.scalar_tensor_tensor(tab[:, :, n, :],
                                             bank[0:S2, 0:D].rearrange("p (h d) -> p h d", h=XH),
                                             (1.0, 0.5)[n],
                                             xb_sb[0:S2, n, :].rearrange("p (h d) -> p h d", h=XH),
                                             ALU.mult, ALU.add)\
                        .then_inc(was_read(Bk, use), 1)
                for k in range(NK - 2):
                    yield f"gather{k + 1}0"
                    score(i, k, "scr")
                yield f"hats{NK - 2}1"
                score(i, NK - 2, "scr")
                end(names)

            def stage_r(i):
                names = ("scr_last", "scs", "att", "av0", "actx", "var2", "x2", "rmax", "top",
                         "ohs", "count", "slots")
                begin(i, names)
                yield "last"
                score(i, NK - 1, "scr_last")
                yield "max"
                own("scr_last", 1)
                link(dve.tensor_reduce(scm[:, :, :], sc[:, :, :, :].rearrange("p c k h -> p c h k"),
                                       AX.X, ALU.max), "scs")

                def over_k(ap):
                    return ap.unsqueeze(2).broadcast_to([P, NC, NK, XH])

                link(dve.tensor_tensor(scd[:, :, :, :], sc[:, :, :, :], over_k(scm[:, :, :]),
                                       ALU.subtract), "scs")
                yield "exp"
                dve.wait_ge(sem["sexp"], total("sexp", i, 1))
                link(dve.tensor_reduce(scm[:, :, :], sce[:, :, :, :].rearrange("p c k h -> p c h k"),
                                       AX.X, ALU.add), "att")
                link(dve.reciprocal(scm[:, :, :], scm[:, :, :]), "att")
                link(dve.tensor_tensor(sce[:, :, :, :], sce[:, :, :, :], over_k(scm[:, :, :]),
                                       ALU.mult), "att")
                link(dve.tensor_tensor(av[:, 0, :, :, :], gs[:, 0, 2:, :, :],
                                       sce[:, 0, :, :].unsqueeze(3)
                                       .broadcast_to([P, NK, XH, XD]), ALU.mult), "av0")
                yield "ctx"
                for c in range(NC):
                    if c == 1:
                        dve.wait_ge(sem["av"], total("av", i, 1))
                    count_in(dve.tensor_reduce(actx[:, c, :].rearrange("p (h d) -> p h d", h=XH),
                                             av[:, c, :, :, :].rearrange("p k h d -> p h d k"),
                                             AX.X, ALU.add),
                           "actx")
                yield "xout"
                bank = wait_filled(R, dve, i, "xout")
                dve.tensor_tensor(xr2[:, :, :], bank[:, :].rearrange("p (c d) -> p c d", c=NC),
                                  res[:, :, :], ALU.add).then_inc(was_read(R, "xout"), 1)
                wait_read(R, dve, i, "xout")
                moments(xr2, bns2, mv2, ve2, "var2")
                yield "norm"
                at_least(dve, sem["x2_out"], total("x2_out", i, 0))
                at_least(dve, sem["scatter"], total("scatter", i, 0))
                normalize(i, xr2, x2, mv2, rstd2, "rstd2", "x2")
                yield "route"
                bank = wait_filled(R, dve, i, "route")
                logits = bank[:, 0:NC * E].rearrange("p (c e) -> p c e", c=NC)
                link(dve.tensor_reduce(prm[:, :], logits, AX.X, ALU.max), "rmax")

                def over_e(ap):
                    return ap.unsqueeze(2).broadcast_to([P, NC, E])

                dve.tensor_tensor(prd[:, :, :], logits, over_e(prm[:, :]), ALU.subtract)\
                    .then_inc(was_read(R, "route"), 1)
                yield "top"
                dve.wait_ge(sem["rexp"], total("rexp", i, 1))
                link(dve.tensor_reduce(prm[:, :], prx[:, :, :], AX.X, ALU.add), "top")
                link(dve.reciprocal(prm[:, :], prm[:, :]), "top")
                link(dve.tensor_tensor(pr[:, :, :], prx[:, :, :], over_e(prm[:, :]), ALU.mult),
                     "top")
                dve.nop(nofuse=True)
                count_in(dve.max(top[:, 0, :], pr[:, 0, :]), "top")
                link(dve.max(top[:, 1, :], pr[:, 1, :]), "top")
                dve.nop(nofuse=True)
                count_in(dve.max_index(topi[:, 0, :], top[:, 0, :], pr[:, 0, :]), "top")
                link(dve.max_index(topi[:, 1, :], top[:, 1, :], pr[:, 1, :]), "top")
                link(dve.tensor_copy(topf[:, :, :], topi[:, :, :]), "top")
                link(dve.tensor_tensor(gsum[:, :], top[:, :, 0], top[:, :, 1], ALU.add), "top")
                link(dve.reciprocal(gsum[:, :], gsum[:, :]), "top")
                at_least(dve, sem["gate_out"], total("gate_out", i, 0))
                link(dve.tensor_tensor(gate[:, :, :], top[:, :, 0:TOPK],
                                       gsum[:, :].unsqueeze(2).broadcast_to([P, NC, TOPK]),
                                       ALU.mult), "top")
                ids = eids[:, :].unsqueeze(1).broadcast_to([P, TOPK, E])
                for c in range(NC):
                    last = dve.tensor_tensor(oh[:, c, :, :], ids, topf[:, c, 0:TOPK].unsqueeze(2)
                                             .broadcast_to([P, TOPK, E]), ALU.is_equal)
                link(last, "ohs")
                link(dve.tensor_tensor(ohs[:, :, :], oh[:, :, 0, :], oh[:, :, 1, :], ALU.add), "ohs")
                yield "pos"
                bank = wait_filled(R, dve, i, "pos")
                dve.tensor_copy(pos[:, :, :], bank[:, 0:NC * E].rearrange("p (c e) -> p c e", c=NC))\
                    .then_inc(was_read(R, "pos"), 1)
                for c in range(NC):
                    link(dve.tensor_tensor(count[:, :], count[:, :], ohs[:, c, :], ALU.add), "count")
                wait_read(R, dve, i, "pos")
                for c in range(NC):
                    count_in(dve.tensor_tensor(psel[:, c, :, :], oh[:, c, :, :],
                                             pos[:, c, :].unsqueeze(1).broadcast_to([P, TOPK, E]),
                                             ALU.mult), "slots")
                    link(dve.tensor_tensor(esel[:, c, :, :], oh[:, c, :, :], ids, ALU.mult), "slots")
                count_in(dve.tensor_reduce(pk[:, :, :], psel[:, :, :, :], AX.X, ALU.add), "slots")
                link(dve.tensor_reduce(ek[:, :, :], esel[:, :, :, :], AX.X, ALU.add), "slots")
                link(dve.tensor_scalar(drop[:, :, :], pk[:, :, :], float(CAP), None, ALU.is_ge),
                     "slots")
                link(dve.tensor_scalar(pk[:, :, :], pk[:, :, :], float(CAP - 1), None, ALU.min),
                     "slots")
                link(dve.scalar_tensor_tensor(gslot[:, :, :], ek[:, :, :], float(CAP), pk[:, :, :],
                                              ALU.mult, ALU.add), "slots")
                link(dve.scalar_tensor_tensor(sslot[:, :, :], drop[:, :, :], float(E * CAP),
                                              gslot[:, :, :], ALU.mult, ALU.add), "slots")
                at_least(dve, sem["slot_out"], total("slot_out", i, 0))
                dve.tensor_scalar(ek[:, :, :], drop[:, :, :], -1.0, 1.0, ALU.mult, ALU.add)
                dve.tensor_copy(gslot_i[:, :], gslot[:, :, :].rearrange("p c k -> p (c k)"))
                link(dve.tensor_copy(sslot_i[:, :], sslot[:, :, :].rearrange("p c k -> p (c k)")),
                     "slots")
                link(dve.tensor_tensor(gate[:, :, :], gate[:, :, :], ek[:, :, :], ALU.mult), "slots")
                end(names)

            def score(i, k, name):
                dve.wait_ge(sem["prod"], total("prod", i, k + 1))
                count_in(dve.tensor_reduce(sc[:, :, k, :], prod[k % 2][:, :, :, :], AX.X, ALU.add),
                         name)

            def split_off(parts, x, name, e, k):
                dve.tensor_copy(parts[0], x).then_inc(sem[name], 1)
                dve.wait_ge(sem[name], total(name, e, k + 1))
                dve.tensor_tensor(parts[1], x, parts[0].bitcast(f32), ALU.subtract)\
                    .then_inc(sem[name], 1)

            def split_rows(e):
                for n in range(NT // 2):
                    dve.wait_ge(sem["x_hi"], total("x_hi", e, n + 1))
                    bank = wait_filled(X, dve, e, f"xeT{n}")
                    at = slice(2 * n * P, (2 * n + 2) * P)
                    dve.tensor_tensor(xeT_p[1][:, :, at], bank[:, :].rearrange("p (c t) -> p c t", c=2),
                                      xeT_p[0][:, :, at].bitcast(f32), ALU.subtract)\
                        .then_inc(was_read(X, f"xeT{n}"), 1)

            def split_w1(e, pair, j):
                dve.wait_ge(sem[f"w_in{j}"], (pair + 1) * PER["w_in0"])
                split_off([w[:, :, :] for w in w1_p], w1_sb[j][:, :, :], "w1_parts", e, 0)

            def split_w2(e, j):
                dve.wait_ge(sem["w2_hi"], total("w2_hi", e, 1))
                dve.tensor_tensor(w2_p[1][:, :, :], w2_sb[j][:, :, :],
                                  w2_p[0][:, :, :].bitcast(f32), ALU.subtract)\
                    .then_inc(sem["w2_parts"], 1)

            def stage_c(e, pair, j, more=True):
                for m in range(HID // P):
                    wait_read(C, dve, e, f"h{m}a", f"h{m}b")
                    split_off([h[:, m, :] for h in hT_p], h_sb[m % 2][:, :], "h_parts", e, 2 * m)
                if more:
                    split_rows(e + 1)
                    split_w1(e + 1, pair + j, 1 - j)
                dve.wait_ge(sem[f"be_in{j}"], (pair + 1) * PER["be_in0"])
                at_least(dve, sem["y_out"], pair * 2 * PER["y_out"])
                for n in range(NT // 2):
                    bank = wait_filled(C, dve, e, f"y{n}")
                    dve.tensor_tensor(ye[j][:, 2 * n:2 * n + 2, :],
                                      bank[:, :].rearrange("p (t d) -> p t d", t=2),
                                      b2_sb[j][:, :].unsqueeze(1).broadcast_to([P, 2, D]),
                                      ALU.add).then_inc(was_read(C, f"y{n}"), 1)
                if more:
                    split_w2(e + 1, 1 - j)

            def add_up(i, turn, j):
                names = ("mix", "fvar")
                begin(i, names)
                at_least(dve, sem["fo"], (i - DB + 1) * PER["fo"])
                at_least(dve, sem[f"out_done{j}"], turn * PER["out_done0"])
                dve.wait_ge(sem[f"f_in{j}"], total("f_in0", turn, PER["f_in0"]))
                dve.wait_ge(sem[f"row_in{j}"], total("row_in0", turn, PER["row_in0"]))
                for c in range(NC):
                    count_in(dve.scalar_tensor_tensor(fy[j][:, c, :], frow[j][:, c, 0, :],
                                                    fgate[j][:, 2 * c:2 * c + 1], fx[j][:, c, :],
                                                    ALU.mult, ALU.add), "mix")
                for c in range(NC):
                    own("mix", c + 1)
                    count_in(dve.scalar_tensor_tensor(fy[j][:, c, :], frow[j][:, c, 1, :],
                                                    fgate[j][:, 2 * c + 1:2 * c + 2],
                                                    fy[j][:, c, :], ALU.mult, ALU.add), "mix")
                own("mix", 4)
                moments(fy[j], fbn[j], fmv[j], fve[j], "fvar")
                end(names)

            def finish(i, j):
                begin(i, ("fo",))
                normalize(i, fy[j], fo[j], fmv[j], frs[j], "frs", "fo")
                end(("fo",))

            dve.wait_ge(first_in, FIRST)
            dve.wait_ge(zeroed, 2)
            dve.tensor_scalar(convw_sb[:, :, :, :], convw_sb[:, :, :, :], 0.5, None, ALU.mult)\
                .then_inc(prepared, 1)
            dve.wait_ge(prepared, 1)
            run(F=stage_f(0))
            dve.wait_ge(early_in, EARLY)
            dve.wait_ge(zeroed, ZEROED)
            dve.tensor_scalar(wo_sb[:, :, :], wo_sb[:, :, :], onorm_sb[:, :], None, ALU.mult)\
                .then_inc(prepared, 1)
            run(A=stage_a(0), F=stage_f(1), T=taps(0))
            dve.wait_ge(consts_in, CONSTS)
            dve.tensor_scalar(xb_sb[:, 1, :], xb_sb[:, 1, :], 0.5, None, ALU.mult)\
                .then_inc(prepared, 1)
            dve.tensor_tensor(offc_sb[:, :], offb_sb[:, :], refp_sb[:, :], ALU.add)\
                .then_inc(prepared, 1)
            dve.wait_ge(prepared, PREPARED)
            run(A=stage_a(1), B=stage_b(0), F=stage_f(2), T=taps(1))
            run(A=stage_a(2), B=stage_b(1), R=stage_r(0), F=stage_f(3), T=taps(2))
            with dve.Fori(2, B - 2) as i:
                run(A=stage_a(i + 1), B=stage_b(i), R=stage_r(i - 1), F=stage_f(i + 2),
                    T=taps(i + 1))
            run(A=stage_a(B - 1), B=stage_b(B - 2), R=stage_r(B - 3), T=taps(B - 1))
            run(B=stage_b(B - 1), R=stage_r(B - 2))
            split_w1(0, 0, 0)
            split_w2(0, 0)
            run(R=stage_r(B - 1))
            split_rows(0)
            for j in range(2):
                stage_c(j, 0, j)
            with dve.Fori(1, E // 2 - 1) as pair:
                for j in range(2):
                    stage_c(pair * 2 + j, pair, j)
            stage_c(E - 2, E // 2 - 1, 0)
            stage_c(E - 1, E // 2 - 1, 1, more=False)
            for j in range(DB):
                add_up(j, 0, j)
                if j:
                    finish(j - 1, j - 1)
            with dve.Fori(1, B // DB) as turn:
                for j in range(DB):
                    add_up(turn * DB + j, turn, j)
                    finish(turn * DB + j - 1, (j - 1) % DB)
            finish(B - 1, DB - 1)

        @block.gpsimd
        def _(pool):
            def rsqrt(dst, src, shape, name):
                n = 1
                for d in shape:
                    n *= d
                h = half_m[:, 0:n]
                if len(shape) == 2:
                    h = h.rearrange("p (a b) -> p a b", a=shape[0])
                pool.tensor_tensor(dst, src, h, ALU.pow).then_inc(sem[name], 1)

            def stage_f(i):
                for n, name, t in ((1, "k", 1), (3, "q", 0)):
                    yield name + "_act"
                    pool.wait_ge(sem["silu"], total("silu", i, n))
                    pool.tensor_tensor(sq[:, t, :, :], qk[:, t, :, :], qk[:, t, :, :], ALU.mult)\
                        .then_inc(sem["sq"], 1)

            def stage_a(i):
                yield "sums"
                wait_read(A, pool, i, "sums")
                pool.nop(nofuse=True)
                pool.tensor_scalar(sums[:, 0:16], sums[:, 0:16], 1e-6, None, ALU.add)\
                    .then_inc(sem["rinv"], 1)
                pool.wait_ge(sem["rinv"], total("rinv", i, 1))
                rsqrt(rinv[:, :, :, :].rearrange("p c t h -> p (c t h)"), sums[:, 0:16], [16],
                      "rinv")
                yield "k_chan"
                pool.wait_ge(sem["beta"], total("beta", i, 2))
                wait_read(A, pool, i, "v_tok")
                pool.tensor_tensor(split(vb[:, :, :]), split(vt[:, :, :]), heads(beta[:, :, :]),
                                   ALU.mult).then_inc(sem["vb"], 1)
                wait_read(A, pool, i, "k_tok")
                pool.tensor_tensor(kb[:, :].rearrange("p (h d) -> p h d", h=H),
                                   kn[:, 1, :].rearrange("p (h d) -> p h d", h=H),
                                   beta[:, 1, :].unsqueeze(2).broadcast_to([P, H, HD]),
                                   ALU.mult).then_inc(sem["kb"], 1)
                yield "gram"
                for c in range(NC):
                    wait_read(A, pool, i, f"gram{c}")
                    pool.tensor_tensor(X8[c][:, :, :], nbG[c][:, :, :], mask4(M_DIAG8), ALU.mult)\
                        .then_inc(sem["x8"], 1)
                yield "gramT"
                for c in range(NC):
                    pool.wait_ge(sem["t1"], total("t1", i, 2 * c + 1))
                    pool.tensor_tensor(XT[c][1][:, :, :], XT[c][2][:, :, :], mask4(M_IN32T),
                                       ALU.mult).then_inc(sem["xm"], 1)
                    pool.wait_ge(sem["xm"], total("xm", i, 2 * c + 1))
                    pool.tensor_tensor(XT[c][2][:, :, :], XT[c][2][:, :, :], mask4(M_IN128T),
                                       ALU.mult).then_inc(sem["xm"], 1)
                yield "fuse"
                pool.wait_ge(sem["fuse"], total("fuse", i, 5))
                pool.tensor_tensor(split(o3[:, :, :]), split(vt[:, :, :]),
                                   heads(wts[:, :, 2].rearrange("p (c h) -> p c h", c=NC)),
                                   ALU.mult).then_inc(sem["v3"], 1)
                yield "gate"
                pool.wait_ge(sem["osum"], total("osum", i, 2))
                pool.tensor_tensor(o2[:, :, :], o1[:, :, :], o1[:, :, :], ALU.mult)\
                    .then_inc(sem["osq"], 1)
                yield "rms"
                pool.wait_ge(sem["orms"], total("orms", i, 2))
                rsqrt(rrms[:, :], rms[:, :], [8], "orr")
                yield "attn"
                pool.wait_ge(sem["var1"], total("var1", i, 4))
                rsqrt(rstd[:, :], ve[:, :], [2], "rstd1")

            def products(i, k):
                for c in range(NC):
                    wait_read(G, pool, i, f"gather{k}_{c}")
                at_least(pool, sem["scr"], total("scr", i, max(0, k - 1)))
                pool.tensor_tensor(prod[k % 2][:, :, :, :], gs[:, :, k % 2, :, :],
                                   split(Qs[:, :, :], XH), ALU.mult).then_inc(sem["prod"], 1)

            def stage_b(i):
                for k in range(NK - 1):
                    if k == 3:
                        yield "gather30"
                        pool.wait_ge(sem["x1"], total("x1", i, 2))
                        if not (isinstance(i, int) and i == 0):
                            wait_read(R, pool, i - 1, "xout")
                        pool.tensor_tensor(res[:, :, :], x1[:, :, :],
                                           xb_sb[:, 2, :].unsqueeze(1).broadcast_to([P, NC, D]),
                                           ALU.add).then_inc(sem["res"], 1)
                    yield f"hats{k}1"
                    if k == 0:
                        wait_read(Bk, pool, i, "Qt")
                        at_least(pool, sem["scr_last"], total("scr_last", i, 0))
                    products(i, k)

            def stage_r(i):
                yield "gather1"
                products(i, NK - 1)
                yield "exp"
                pool.wait_ge(sem["att"], total("att", i, 3))
                pool.tensor_tensor(av[:, 1, :, :, :], gs[:, 1, 2:, :, :],
                                   sce[:, 1, :, :].unsqueeze(3).broadcast_to([P, NK, XH, XD]),
                                   ALU.mult).then_inc(sem["av"], 1)
                yield "xout"
                pool.wait_ge(sem["var2"], total("var2", i, 4))
                rsqrt(rstd2[:, :], ve2[:, :], [2], "rstd2")
                yield "slots"
                pool.wait_ge(sem["slots"], total("slots", i, PER["slots"]))
                pool.nop(nofuse=True)
                for c in range(NC):
                    for k in range(TOPK):
                        n = c * TOPK + k
                        pool.indirect_dma_start(
                            out=xe_dram, out_offset=bass.IndirectOffsetOnAxis(
                                ap=sslot_i[:, n:n + 1], axis=0),
                            in_=x2[:, c, :], in_offset=None, bounds_check=E * CAP - 1,
                            oob_is_err=False).then_inc(sem["scatter"], 16)

            def stage_d(turn, j):
                pool.wait_ge(sem[f"f_in{j}"], total("f_in0", turn, PER["f_in0"]))
                pool.nop(nofuse=True)
                for c in range(NC):
                    for k in range(TOPK):
                        n = c * TOPK + k
                        pool.indirect_dma_start(
                            out=frow[j][:, c, k, :], out_offset=None, in_=ye_dram,
                            in_offset=bass.IndirectOffsetOnAxis(ap=fslot[j][:, n:n + 1], axis=0))\
                            .then_inc(sem[f"row_in{j}"], 16)

            def norm_d(i, j):
                pool.wait_ge(sem["fvar"], total("fvar", i, 4))
                rsqrt(frs[j][:, :], fve[j][:, :], [2], "frs")

            for n, (ap, value) in enumerate(
                    ((pre[:, :, :, 0:3], 0.0), (vpad[:, :, 0:PAD], 0.0), (half_m[:, :], -0.5),
                     (zero, 0.0), (kz[:, :, :, :], 0.0), (S_sb[:, :, :], 0.0),
                     (count[:, :], 0.0), (ixp[96:97, :, :], 1.0))):
                pool.memset(ap, value).then_inc(zeroed, 1)
                pool.wait_ge(zeroed, n + 1)
            for n in range(ZERO_DMAS):
                pool.dma_start(xe_dram[bass.ts(n, E * CAP // ZERO_DMAS), :]
                               .rearrange("(p t) d -> p (t d)", p=P), zero).then_inc(xe_zero, 16)
            run(F=stage_f(0))
            pool.wait_ge(early_in, EARLY)
            run(A=stage_a(0), F=stage_f(1))
            pool.wait_ge(consts_in, CONSTS)
            pool.wait_ge(xe_zero, 16 * ZERO_DMAS)
            run(A=stage_a(1), B=stage_b(0), F=stage_f(2))
            run(A=stage_a(2), B=stage_b(1), R=stage_r(0), F=stage_f(3))
            with pool.Fori(2, B - 2) as i:
                run(A=stage_a(i + 1), B=stage_b(i), R=stage_r(i - 1), F=stage_f(i + 2))
            run(A=stage_a(B - 1), B=stage_b(B - 2), R=stage_r(B - 3))
            run(B=stage_b(B - 1), R=stage_r(B - 2))
            run(R=stage_r(B - 1))
            pool.wait_ge(sem["y_out"], E * PER["y_out"])
            for j in range(DB):
                stage_d(0, j)
            with pool.Fori(0, B // DB - 1) as turn:
                for j in range(DB):
                    pool.wait_ge(sem["mix"], total("mix", turn * DB + j, PER["mix"]))
                    stage_d(turn + 1, j)
                    norm_d(turn * DB + j, j)
            for j in range(DB):
                norm_d(B - DB + j, j)


def kernel(**inputs):
    import numpy as np
    import concourse.bacc as bacc
    from concourse.bass_utils import run_bass_kernel_spmd

    a = {k: np.asarray(v) for k, v in inputs.items()}

    def rows(w, k):
        return w.reshape(k, P, -1).transpose(1, 0, 2)

    x = a["x"]
    r, c = np.arange(P)[:, None], np.arange(P)[None, :]
    below = r > c
    diag8 = below & (r // 8 == c // 8)
    in32 = below & (r // 32 == c // 32) & ~diag8
    in128 = below & ~(r // 32 == c // 32)
    table = [diag8, diag8.T, in32.T, in128.T, r <= c, r == c, r < c, r + c >= 0]
    masks = np.stack(table, 1).astype(np.float32)
    kmw = a["L0_attn_kernel_mix_w"]
    kmix = np.zeros((6, P, P), np.float32)
    for row in range(0, 3 * D, HD):
        head, at = divmod(row, 3 * HD)
        j, p = divmod(row, P)
        kmix[j, p:p + HD, (head % 2) * HD:(head % 2 + 1) * HD] = kmw[at:at + HD]
    woff = a["L0_xattn_Woff"].reshape(XH, NK, D).transpose(1, 0, 2).reshape(NK * XH, D)
    boff = a["L0_xattn_boff"].reshape(XH, NK).T.reshape(NK * XH)
    wo3, bo3, ref3 = np.zeros((96, D), np.float32), np.zeros(96, np.float32), np.zeros(96)
    wo3[:NK * XH], bo3[:NK * XH] = woff, boff
    ref3[:NK * XH] = np.arange(NK * XH) // XH - (NK + 1) // 2
    import ml_dtypes
    selector = np.zeros((97, 32, S2), ml_dtypes.bfloat16)
    for p in range(96):
        selector[p, p % 32, :] = 1
    selector[96, :, :] = -np.arange(S2)
    headsel = (r[:, 0:1] // HD == np.arange(2)[None, :]).astype(np.float32)
    arrays = dict(
        x_tok=x.reshape(B, NC, P, D).transpose(0, 2, 1, 3),
        xT=x.transpose(0, 2, 1).reshape(B, 2, P, T).transpose(0, 2, 1, 3),
        ctxT=a["ctx_1024"].transpose(0, 2, 1).reshape(B, 2, P, S2).transpose(0, 2, 1, 3),
        mask=a["mask_BxS2_if0"],
        wqkv=np.stack([rows(a[f"L0_attn_W{n}"], 2) for n in "qkv"], 1),
        wb=rows(a["L0_attn_Wb"], 2),
        convw=np.stack([rows(a[f"L0_attn_conv_{n}_w"], 2) for n in "qkv"], 1),
        msw3=rows(a["L0_attn_ms_w3"], 2), msw15=rows(a["L0_attn_ms_w15"], 2),
        msw31=rows(a["L0_attn_ms_w31"], 2),
        kmix=kmix.transpose(1, 0, 2), cmix=rows(a["L0_attn_channel_mixer_w"], 2),
        fw1=rows(a["L0_attn_fusion_w1"][:D], 2), fw1s=a["L0_attn_fusion_w1"][D:],
        fb1=a["L0_attn_fusion_b1"].reshape(4, P).T, fw2=rows(a["L0_attn_fusion_w2"], 4),
        fb2=a["L0_attn_fusion_b2"], onorm=a["L0_attn_o_norm_w"].reshape(HD, 1),
        wo=rows(a["L0_attn_Wo"], 2),
        xwT=np.stack([rows(a[f"L0_xattn_W{n}"].T, 2) for n in "kvqo"], 1),
        xbias=np.stack([a[f"L0_xattn_b{n}"] for n in "kvo"]), xbq=a["L0_xattn_bq"].reshape(2, P).T,
        woff=rows(np.ascontiguousarray(wo3.T), 2), boff=bo3[:, None],
        ref_pos=ref3[:, None].astype(np.float32), wr=rows(a["L0_ffn_w_router"], 2),
        w1=a["L0_ffn_w1"].reshape(E, 2, P, HID).transpose(0, 2, 1, 3),
        b1=a["L0_ffn_b1"].reshape(E, HID // P, P).transpose(0, 2, 1),
        w2=a["L0_ffn_w2"].reshape(E, HID // P, P, D).transpose(0, 2, 1, 3),
        b2=a["L0_ffn_b2"], masks=masks, headsel=headsel, selector=selector,
        positions=np.arange(T, dtype=np.float32), expert_ids=np.arange(E, dtype=np.float32),
    )
    nc = bacc.Bacc("TRN2", target_bir_lowering=False, num_devices=1)
    args = {}
    arrays = {f"in_{n}": np.ascontiguousarray(v) for n, v in arrays.items()}
    for name, v in arrays.items():
        args[name[3:]] = nc.dram_tensor(name, v.shape, mybir.dt.from_np(v.dtype),
                                    kind="ExternalInput").ap()
    args["msw"] = [args.pop(f"msw{t}") for t in TAPS]
    out = nc.dram_tensor("out", (B, P, NC, D), mybir.dt.float32, kind="ExternalOutput").ap()
    decoder_layer(nc, out=out, **args)
    r = run_bass_kernel_spmd(nc, [arrays], core_ids=[0])
    got = r.results[0]["out"]
    return np.ascontiguousarray(got.transpose(0, 2, 1, 3).reshape(B, T, D))
```
